# Optimizing a Trainium2 kernel written in Bass

```python
import numpy as np
import jax
import jax.numpy as jnp

def _softmax(x, axis=-1):
    return jax.nn.softmax(x, axis=axis)

def _gelu(x):
    return jax.nn.gelu(x, approximate=True)

def _silu(x):
    return jax.nn.silu(x)

def _sigmoid(x):
    return jax.nn.sigmoid(x)

def _layernorm(x, axis=-1, eps=1e-05):
    m = jnp.mean(x, axis=axis, keepdims=True)
    v = jnp.var(x, axis=axis, keepdims=True)
    return (x - m) / jnp.sqrt(v + eps)

def _scatter_add(tgt, idx, src, axis=0):
    return tgt.at[idx].add(src)

def _segment_sum(src, seg, n):
    return jax.ops.segment_sum(src, seg, n)
kernel_name = 'mk_xattn_ffn_d2_seqx_r8_c9ff1e'

def setup_inputs(seed: int=0):
    np.random.seed(seed)
    _w = jnp.asarray

    def _rec_inputs():
        import jax
        import jax.numpy as jnp
        _rk = jax.random.key(seed)
        x = -0.0002928 + 1 * jax.random.normal(jax.random.fold_in(_rk, 1), (4, 512, 128), jnp.float32)
        _lenS = 512 - jax.random.randint(jax.random.fold_in(_rk, 7), (4,), 0, max(1, 512 // 4) + 1, jnp.int32)
        _lenS2 = 77 - jax.random.randint(jax.random.fold_in(_rk, 8), (4,), 0, max(1, 77 // 4) + 1, jnp.int32)
        _ctx_1024P = jax.random.normal(jax.random.fold_in(_rk, 11), (4, 16, 128), jnp.float32)
        _ctx_1024c = jax.random.dirichlet(jax.random.fold_in(_rk, 511), 0.3 * jnp.ones((16,), jnp.float32), (4, 77))
        _ctx_1024t = jnp.einsum('bsk,bkd->bsd', _ctx_1024c, _ctx_1024P)
        _ctx_1024t = _ctx_1024t * jax.lax.rsqrt(jnp.mean(jnp.square(_ctx_1024t)) + 1e-12) * 0.953939
        ctx_1024 = 4.13588e-05 + 0.999923 * (_ctx_1024t + 0.3 * jax.random.normal(jax.random.fold_in(_rk, 611), (4, 77, 128), jnp.float32))
        fside_1xSxS2_0 = 0.000675642 + 1.00031 * jax.random.normal(jax.random.fold_in(_rk, 13), (1, 512, 77), jnp.float32)
        _validS = jnp.arange(512)[None, :] < _lenS[:, None]
        _validS2 = jnp.arange(77)[None, :] < _lenS2[:, None]
        _causal = jnp.tril(jnp.ones((512, 512), dtype=bool))
        mask_BxS2_bk0 = jnp.logical_not(jnp.broadcast_to(_validS2[:, :], (4, 77)))
        return (x, ctx_1024, fside_1xSxS2_0, mask_BxS2_bk0)
    x, ctx_1024, fside_1xSxS2_0, mask_BxS2_bk0 = _rec_inputs()

    def _L0_xattn_setup():
        import jax, jax.numpy as jnp
        import numpy as np
        D_MODEL = 128
        N_HEAD = 16
        D_H = D_MODEL // N_HEAD
        key = jax.random.key(seed)
        ks = jax.random.split(key, 12)
        B, LQ, LK = (4, 128, 256)
        s = 1.0 / np.sqrt(D_MODEL)
        inp = {'q_input': jax.random.normal(ks[0], (B, LQ, D_MODEL), jnp.float32), 'kv_input': jax.random.normal(ks[1], (B, LK, D_MODEL), jnp.float32), 'key_padding_mask': jax.random.randint(ks[2], (B, LK), 0, 2) > 0, 'W_Q': jax.random.normal(ks[3], (D_MODEL, D_MODEL), jnp.float32) * s, 'b_Q': jnp.zeros((D_MODEL,), jnp.float32), 'W_K': jax.random.normal(ks[4], (D_MODEL, D_MODEL), jnp.float32) * s, 'b_K': jnp.zeros((D_MODEL,), jnp.float32), 'W_V': jax.random.normal(ks[5], (D_MODEL, D_MODEL), jnp.float32) * s, 'b_V': jnp.zeros((D_MODEL,), jnp.float32), 'W_O': jax.random.normal(ks[6], (D_MODEL, D_MODEL), jnp.float32) * s, 'b_O': jnp.zeros((D_MODEL,), jnp.float32)}
        return inp
    _L0_xattn_all = _L0_xattn_setup()
    _L0_xattn_in = {k: v for k, v in _L0_xattn_all.items() if k in ('W_Q', 'b_Q', 'W_K', 'b_K', 'W_V', 'b_V', 'W_O', 'b_O')}
    del _L0_xattn_all

    def _L0_ffn_setup():
        import jax, jax.numpy as jnp
        import numpy as np
        from jax import lax
        LOKAL_GRUP = 7
        TOP_K = 2
        EPS = 1e-08
        CACHE_BONUS = 0.1

        def _route(tokens, uzman_embeddings, onbellek_durumu):
            sim = tokens @ uzman_embeddings.T
            _, local_idx = lax.top_k(sim, LOKAL_GRUP)
            t_norm = tokens / (jnp.linalg.norm(tokens, axis=-1, keepdims=True) + EPS)
            e_norm = uzman_embeddings / (jnp.linalg.norm(uzman_embeddings, axis=-1, keepdims=True) + EPS)
            local_embs = e_norm[local_idx]
            scores = jnp.einsum('nld,nd->nl', local_embs, t_norm)
            scores = scores + CACHE_BONUS * onbellek_durumu[local_idx]
            top_scores, top_local = lax.top_k(scores, TOP_K)
            global_idx = jnp.take_along_axis(local_idx, top_local, axis=1)
            weights = jax.nn.softmax(top_scores, axis=-1)
            return (global_idx, lax.stop_gradient(weights))
        key = jax.random.key(seed)
        ks = jax.random.split(key, 6)
        B, S, D, E, H = (2, 256, 128, 8, 512)
        return {'x': jax.random.normal(ks[0], (B, S, D), jnp.float32), 'uzman_embeddings': jax.random.normal(ks[1], (E, D), jnp.float32) * 0.01, 'W1': jax.random.normal(ks[2], (E, D, H), jnp.float32) * 0.02, 'b1': jax.random.normal(ks[3], (E, H), jnp.float32) * 0.02, 'W2': jax.random.normal(ks[4], (E, H, D), jnp.float32) * 0.02, 'b2': jax.random.normal(ks[5], (E, D), jnp.float32) * 0.02, 'onbellek_durumu': jnp.ones((E,), jnp.float32)}
    _L0_ffn_all = _L0_ffn_setup()
    _L0_ffn_in = {k: v for k, v in _L0_ffn_all.items() if k in ('uzman_embeddings', 'W1', 'b1', 'W2', 'b2', 'onbellek_durumu')}
    del _L0_ffn_all

    def _L1_xattn_setup():
        import jax, jax.numpy as jnp
        import numpy as np
        import math
        D = 128
        B, S = (8, 256)

        def _proj(x, W1, b1, W2, b2):
            h = jnp.einsum('bsd,od->bso', x, W1) + b1
            return jnp.einsum('bsd,od->bso', h, W2) + b2
        key = jax.random.key(seed)
        ks = jax.random.split(key, 8)
        q = jax.random.normal(ks[0], (B, S, D), dtype=jnp.float32)
        k = jax.random.normal(ks[1], (B, S, D), dtype=jnp.float32)
        v1 = jax.random.normal(ks[2], (B, S, D), dtype=jnp.float32)
        mask = jax.random.normal(ks[3], (1, S, S), dtype=jnp.float32)
        lim = 1.0 / math.sqrt(D)
        W1 = jax.random.uniform(ks[4], (D, D), jnp.float32, -lim, lim)
        b1 = jax.random.uniform(ks[5], (D,), jnp.float32, -lim, lim)
        W2 = jax.random.uniform(ks[6], (D, D), jnp.float32, -lim, lim)
        b2 = jax.random.uniform(ks[7], (D,), jnp.float32, -lim, lim)
        return {'q': q, 'k': k, 'v1': v1, 'mask': mask, 'W1': W1, 'b1': b1, 'W2': W2, 'b2': b2}
    _L1_xattn_all = _L1_xattn_setup()
    _L1_xattn_in = {k: v for k, v in _L1_xattn_all.items() if k in ('W1', 'b1', 'W2', 'b2')}
    del _L1_xattn_all

    def _L1_ffn_setup():
        import jax, jax.numpy as jnp
        import numpy as np
        E = 8
        K = 2
        D = 128
        F = 512
        EPS = 1e-05

        def _layernorm(h, g, b):
            mu = h.mean(axis=-1, keepdims=True)
            var = ((h - mu) ** 2).mean(axis=-1, keepdims=True)
            return (h - mu) * jax.lax.rsqrt(var + EPS) * g[:, None, :] + b[:, None, :]
        key = jax.random.key(seed)
        ks = jax.random.split(key, 8)
        B, S = (2, 256)
        x = jax.random.normal(ks[0], (B, S, D), dtype=jnp.float32)
        Wr = jax.random.normal(ks[1], (D, E), dtype=jnp.float32) / np.sqrt(D)
        br = jnp.zeros((E,), dtype=jnp.float32)
        W1 = jax.random.normal(ks[2], (E, D, F), dtype=jnp.float32) / np.sqrt(D)
        b1 = jnp.zeros((E, F), dtype=jnp.float32)
        g1 = jnp.ones((E, F), dtype=jnp.float32)
        be1 = jnp.zeros((E, F), dtype=jnp.float32)
        W2 = jax.random.normal(ks[3], (E, F, D), dtype=jnp.float32) / np.sqrt(F)
        b2 = jnp.zeros((E, D), dtype=jnp.float32)
        g2 = jnp.ones((E, D), dtype=jnp.float32)
        be2 = jnp.zeros((E, D), dtype=jnp.float32)
        return {'x': x, 'Wr': Wr, 'br': br, 'W1': W1, 'b1': b1, 'g1': g1, 'be1': be1, 'W2': W2, 'b2': b2, 'g2': g2, 'be2': be2}
    _L1_ffn_all = _L1_ffn_setup()
    _L1_ffn_in = {k: v for k, v in _L1_ffn_all.items() if k in ('Wr', 'br', 'W1', 'b1', 'g1', 'be1', 'W2', 'b2', 'g2', 'be2')}
    del _L1_ffn_all
    return {'x': x, 'ctx_1024': ctx_1024, 'fside_1xSxS2_0': fside_1xSxS2_0, 'mask_BxS2_bk0': mask_BxS2_bk0, 'L0_xattn_W_Q': _L0_xattn_in['W_Q'], 'L0_xattn_b_Q': _L0_xattn_in['b_Q'], 'L0_xattn_W_K': _L0_xattn_in['W_K'], 'L0_xattn_b_K': _L0_xattn_in['b_K'], 'L0_xattn_W_V': _L0_xattn_in['W_V'], 'L0_xattn_b_V': _L0_xattn_in['b_V'], 'L0_xattn_W_O': _L0_xattn_in['W_O'], 'L0_xattn_b_O': _L0_xattn_in['b_O'], 'L0_ffn_uzman_embeddings': _L0_ffn_in['uzman_embeddings'], 'L0_ffn_W1': _L0_ffn_in['W1'], 'L0_ffn_b1': _L0_ffn_in['b1'], 'L0_ffn_W2': _L0_ffn_in['W2'], 'L0_ffn_b2': _L0_ffn_in['b2'], 'L0_ffn_onbellek_durumu': _L0_ffn_in['onbellek_durumu'], 'L1_xattn_W1': _L1_xattn_in['W1'], 'L1_xattn_b1': _L1_xattn_in['b1'], 'L1_xattn_W2': _L1_xattn_in['W2'], 'L1_xattn_b2': _L1_xattn_in['b2'], 'L1_ffn_Wr': _L1_ffn_in['Wr'], 'L1_ffn_br': _L1_ffn_in['br'], 'L1_ffn_W1': _L1_ffn_in['W1'], 'L1_ffn_b1': _L1_ffn_in['b1'], 'L1_ffn_g1': _L1_ffn_in['g1'], 'L1_ffn_be1': _L1_ffn_in['be1'], 'L1_ffn_W2': _L1_ffn_in['W2'], 'L1_ffn_b2': _L1_ffn_in['b2'], 'L1_ffn_g2': _L1_ffn_in['g2'], 'L1_ffn_be2': _L1_ffn_in['be2']}

def reference(x, ctx_1024, fside_1xSxS2_0, mask_BxS2_bk0, L0_xattn_W_Q, L0_xattn_b_Q, L0_xattn_W_K, L0_xattn_b_K, L0_xattn_W_V, L0_xattn_b_V, L0_xattn_W_O, L0_xattn_b_O, L0_ffn_uzman_embeddings, L0_ffn_W1, L0_ffn_b1, L0_ffn_W2, L0_ffn_b2, L0_ffn_onbellek_durumu, L1_xattn_W1, L1_xattn_b1, L1_xattn_W2, L1_xattn_b2, L1_ffn_Wr, L1_ffn_br, L1_ffn_W1, L1_ffn_b1, L1_ffn_g1, L1_ffn_be1, L1_ffn_W2, L1_ffn_b2, L1_ffn_g2, L1_ffn_be2):
    import jax
    import jax.numpy as jnp

    def _L0_xattn_ref(q_input, kv_input, key_padding_mask, W_Q, b_Q, W_K, b_K, W_V, b_V, W_O, b_O):
        import jax, jax.numpy as jnp
        import numpy as np
        D_MODEL = 128
        N_HEAD = 16
        D_H = D_MODEL // N_HEAD
        B, LQ, _ = q_input.shape
        LK = kv_input.shape[1]
        q = q_input @ W_Q + b_Q
        k = kv_input @ W_K + b_K
        v = kv_input @ W_V + b_V
        q = q.reshape(B, LQ, N_HEAD, D_H).transpose(0, 2, 1, 3)
        k = k.reshape(B, LK, N_HEAD, D_H).transpose(0, 2, 1, 3)
        v = v.reshape(B, LK, N_HEAD, D_H).transpose(0, 2, 1, 3)
        sim = jnp.einsum('bhqd,bhkd->bhqk', q, k) / jnp.sqrt(jnp.float32(D_H))
        neg_inf = jnp.finfo(sim.dtype).min
        mask = key_padding_mask[:, None, None, :]
        sim = jnp.where(mask, neg_inf, sim)
        attn = jax.nn.softmax(sim, axis=-1)
        out = jnp.einsum('bhqk,bhkd->bhqd', attn, v)
        out = out.transpose(0, 2, 1, 3).reshape(B, LQ, D_MODEL)
        return out @ W_O + b_O

    def _L0_ffn_ref(x, uzman_embeddings, W1, b1, W2, b2, onbellek_durumu):
        import jax, jax.numpy as jnp
        import numpy as np
        from jax import lax
        LOKAL_GRUP = 7
        TOP_K = 2
        EPS = 1e-08
        CACHE_BONUS = 0.1

        def _route(tokens, uzman_embeddings, onbellek_durumu):
            sim = tokens @ uzman_embeddings.T
            _, local_idx = lax.top_k(sim, LOKAL_GRUP)
            t_norm = tokens / (jnp.linalg.norm(tokens, axis=-1, keepdims=True) + EPS)
            e_norm = uzman_embeddings / (jnp.linalg.norm(uzman_embeddings, axis=-1, keepdims=True) + EPS)
            local_embs = e_norm[local_idx]
            scores = jnp.einsum('nld,nd->nl', local_embs, t_norm)
            scores = scores + CACHE_BONUS * onbellek_durumu[local_idx]
            top_scores, top_local = lax.top_k(scores, TOP_K)
            global_idx = jnp.take_along_axis(local_idx, top_local, axis=1)
            weights = jax.nn.softmax(top_scores, axis=-1)
            return (global_idx, lax.stop_gradient(weights))
        B, S, D = x.shape
        tokens = x.reshape(-1, D)
        global_idx, weights = _route(tokens, uzman_embeddings, onbellek_durumu)
        h = jnp.einsum('nd,edh->enh', tokens, W1) + b1[:, None, :]
        h = jax.nn.gelu(h, approximate=False)
        out_all = jnp.einsum('enh,ehd->end', h, W2) + b2[:, None, :]
        N = tokens.shape[0]
        out_sel = out_all[global_idx, jnp.arange(N)[:, None]]
        out = jnp.sum(weights[..., None] * out_sel, axis=1)
        return out.reshape(B, S, D)

    def _L1_xattn_ref(q, k, v1, mask, W1, b1, W2, b2):
        import jax, jax.numpy as jnp
        import numpy as np
        import math
        D = 128
        B, S = (8, 256)

        def _proj(x, W1, b1, W2, b2):
            h = jnp.einsum('bsd,od->bso', x, W1) + b1
            return jnp.einsum('bsd,od->bso', h, W2) + b2
        qp = _proj(q, W1, b1, W2, b2)
        kp = _proj(k, W1, b1, W2, b2)
        scale = 1.0 / math.sqrt(qp.shape[-1])
        qk = jnp.einsum('bqd,bkd->bqk', qp, kp) * scale
        qk = qk + mask
        attn = jax.nn.softmax(qk, axis=-1)
        return jnp.einsum('bqk,bkd->bqd', attn, v1)

    def _L1_ffn_ref(x, Wr, br, W1, b1, g1, be1, W2, b2, g2, be2):
        import jax, jax.numpy as jnp
        import numpy as np
        E = 8
        K = 2
        D = 128
        F = 512
        EPS = 1e-05

        def _layernorm(h, g, b):
            mu = h.mean(axis=-1, keepdims=True)
            var = ((h - mu) ** 2).mean(axis=-1, keepdims=True)
            return (h - mu) * jax.lax.rsqrt(var + EPS) * g[:, None, :] + b[:, None, :]
        B, S, _ = x.shape
        xt = x.reshape(-1, D)
        logits = xt @ Wr + br
        p = jax.nn.softmax(logits, axis=-1)
        probs, idx = jax.lax.top_k(p, K)
        probs = probs / probs.sum(axis=-1, keepdims=True)
        h = jnp.einsum('td,edf->etf', xt, W1) + b1[:, None, :]
        h = _layernorm(jax.nn.relu(h), g1, be1)
        y = jnp.einsum('etf,efd->etd', h, W2) + b2[:, None, :]
        y = _layernorm(jax.nn.relu(y), g2, be2)
        gate = (jax.nn.one_hot(idx, E, dtype=x.dtype) * probs[..., None]).sum(axis=1)
        out = jnp.einsum('te,etd->td', gate, y)
        return out.reshape(B, S, D)
    x = x + _L0_xattn_ref(_layernorm(x, axis=-1), ctx_1024, mask_BxS2_bk0, L0_xattn_W_Q, L0_xattn_b_Q, L0_xattn_W_K, L0_xattn_b_K, L0_xattn_W_V, L0_xattn_b_V, L0_xattn_W_O, L0_xattn_b_O)
    x = x + _L0_ffn_ref(_layernorm(x, axis=-1), L0_ffn_uzman_embeddings, L0_ffn_W1, L0_ffn_b1, L0_ffn_W2, L0_ffn_b2, L0_ffn_onbellek_durumu)
    x = x + _L1_xattn_ref(_layernorm(x, axis=-1), ctx_1024, ctx_1024, fside_1xSxS2_0, L1_xattn_W1, L1_xattn_b1, L1_xattn_W2, L1_xattn_b2)
    x = x + _L1_ffn_ref(_layernorm(x, axis=-1), L1_ffn_Wr, L1_ffn_br, L1_ffn_W1, L1_ffn_b1, L1_ffn_g1, L1_ffn_be1, L1_ffn_W2, L1_ffn_b2, L1_ffn_g2, L1_ffn_be2)
    return x

_drawn_inputs = setup_inputs


def setup_inputs(seed=0):
    import zlib

    import numpy as np

    out = dict(_drawn_inputs(seed))
    spreads = {'L0_xattn_b_Q': (0.0, 0.1),
     'L0_xattn_b_K': (0.0, 0.8),
     'L0_xattn_b_V': (0.0, 0.1),
     'L0_xattn_b_O': (0.0, 0.1),
     'L0_ffn_onbellek_durumu': (1.0, 0.2),
     'L1_ffn_br': (0.0, 0.1),
     'L1_ffn_b1': (0.0, 0.1),
     'L1_ffn_g1': (1.0, 0.2),
     'L1_ffn_be1': (0.0, 0.1),
     'L1_ffn_b2': (0.0, 0.1),
     'L1_ffn_g2': (1.0, 0.2),
     'L1_ffn_be2': (0.0, 0.1)}
    factors = {'L0_ffn_b1': 3.177, 'L1_xattn_b1': 5.251, 'L1_xattn_b2': 3.207}
    for name, (base, spread) in spreads.items():
        noise = np.random.default_rng([zlib.crc32(name.encode()), seed]).standard_normal(out[name].shape)
        drawn = base * np.exp(spread * noise) if base else spread * noise
        out[name] = jnp.asarray(drawn.astype(out[name].dtype))
    for name, factor in factors.items():
        out[name] = (out[name] * factor).astype(out[name].dtype)
    return out
```

```python
from contextlib import ExitStack

import concourse.bass as bass
from concourse import mybir

F32, BF16, I32, U8 = mybir.dt.float32, mybir.dt.bfloat16, mybir.dt.int32, mybir.dt.uint8
ALU = mybir.AluOpType
ACT = mybir.ActivationFunctionType
AX = mybir.AxisListType

P = 128
B, S, D = 4, 512, 128
TOK = B * S
NT = TOK // P
G = B
TG = NT // G
KL = 77
H, DH = 16, 8
HK = H * KL
NBLK = -(-HK // P)
VC = DH + 1
E, F = 8, 512
FC = F // P
NS = (2 * TOK + E * (P - 1)) // P
SPARE = NS - 2 * TOK // P
REGION = TOK + P
RW = D + 4
XROWS = E * REGION + SPARE * P
YROWS = 2 * TOK + NS * P
LN_EPS = 1e-5
NORM_EPS = 1e-8
HIDE = -float(2 ** 100)
DROP = -1e30
RSQRT_SEED = 1597463007.0
XBUF = 4
DVE_GROUP, DVE_GROUP1, DVE_LAST = 75, 122, 2
DVE_TILE = (0, 6)


class Steps:

    def __init__(self, eng, sem):
        self.eng, self.sem, self.base, self.n = eng, sem, 0, 0

    def __call__(self, ins, consts_ready=None):
        ins.then_inc(self.sem, 1)
        self.n += 1
        if consts_ready is not None:
            return wait_alone(self.eng, consts_ready, (self.sem, self.base + self.n))
        self.eng.wait_ge(self.sem, self.base + self.n)

    def enter(self, i, per):
        self.outer = self.base + self.n
        self.base, self.n, self.per = self.outer + i * per, 0, per

    def leave(self, passes):
        assert self.n == self.per, (self.n, self.per)
        self.base, self.n = self.outer + passes * self.per, 0


def W(eng, sem, n):
    if not isinstance(n, int) or n > 0:
        eng.wait_ge(sem, n)


def wait_alone(eng, consts_ready, *waits):
    waits = [(sem, n if isinstance(n, int) else eng.to_reg(n)) for sem, n in waits]
    eng.wait_ge(consts_ready, 1)
    for sem, n in waits:
        W(eng, sem, n)


def two(tensor, j, w=D):
    return tensor[:, (j % 2) * w:(j % 2 + 1) * w]


def at(tensor, i, w, n=1):
    return tensor[:, bass.ds(i * w, n * w)]


def spread(ap, n, axis=2):
    ap = ap.unsqueeze(axis)
    shape = list(ap.shape)
    shape[axis] = n
    return ap.broadcast_to(shape)


def build(nc, d, out, xslots, yslots):
    ctx = ExitStack()

    def sb(name, width, dt=F32, rows=P):
        return ctx.enter_context(nc.sbuf_tensor(name, [rows, width], dt))

    def sem(name):
        return ctx.enter_context(nc.semaphore(name))

    with ctx:
        ident = sb("ident", P)
        ones = sb("ones", P)
        ones_b = sb("ones_b", P, BF16)
        below = sb("below", P, BF16)
        pick = sb("pick", E * P, BF16)
        head_of = sb("head_of", H)
        block_of = sb("block_of", NBLK * H)
        up8, down8 = sb("up8", E), sb("down8", E)
        region0 = sb("region0", E)
        ramp16 = sb("ramp16", TOK // P)
        ramp_s = sb("ramp_s", NS)
        token_id = sb("token_id", NT)
        dump_row = sb("dump_row", NS)
        eps = sb("eps", 1)
        x = sb("x", NT * D)
        ctx_n = sb("ctx_n", B * D)
        mask_u8 = sb("mask_u8", KL, U8, B)
        wq, wk, wv, wo = sb("wq", D), sb("wk", D), sb("wv", D), sb("wo", D)
        bq, bk, bv = sb("bq", 1), sb("bk", 1), sb("bv", 1)
        bo_all = sb("bo_all", D)
        emb = sb("emb", D, F32, E)
        cache_all = sb("cache_all", E)
        fside = sb("fside", TG * KL)
        u1, u2 = sb("u1", D), sb("u2", D)
        ub1, ub2 = sb("ub1", 1), sb("ub2", 1)
        router1 = sb("router1", E)
        br_all = sb("br_all", E)
        w1 = [sb(f"w1_{n}", E * F) for n in range(2)]
        zeros = w1[1][:, 0:REGION // P * RW]
        w2 = [sb(f"w2_{n}", E * FC * D) for n in range(2)]
        bias_f = [sb(f"bias_f{n}", F + D) for n in range(2)]
        bias_p = [sb(f"bias_p{n}", F + D, BF16) for n in range(2)]
        g1_n, be1_n = sb("g1_n", P, F32, E * FC), sb("be1_n", P, F32, E * FC)
        b2_n = sb("b2_n", D, F32, E)
        g1_t, be1_t = sb("g1_t", E * FC), sb("be1_t", E * FC)
        shift_t = sb("shift_t", P)
        ctx_t = sb("ctx_t", B * KL)
        k_t = sb("k_t", B * KL)
        ctx_rep = sb("ctx_rep", 2 * NBLK * P)
        g2_all, be2_all = ctx_rep[:, 0:E * D], ctx_rep[:, E * D:2 * E * D]
        k_heads = sb("k_heads", B * HK)
        v_heads = sb("v_heads", B * NBLK * H * VC)
        hide = sb("hide", HK, BF16)
        out_row = sb("out_row", D)
        bv_rep = sb("bv_rep", D)
        stats = sb("stats", NT * 6)
        mv = sb("mv", NT * 2)
        rstd = sb("rstd", NT)
        nw_v, nw_t = sb("nw_v", NT), sb("nw_t", NT)
        xn_both = sb("xn_both", 2 * NT * D)
        xn, xn_t = xn_both[:, 0:NT * D], xn_both[:, NT * D:]
        q_t = sb("q_t", 2 * D)
        neg_max = sb("neg_max", 2 * H)
        probs = sb("probs", 2 * NBLK * P)
        probs_t = sb("probs_t", NBLK * P)
        inv = sb("inv", H)
        heads_out = sb("heads_out", D)
        heads_t = sb("heads_t", D)
        mvg = sb("mvg", TG * 2)
        statg = sb("statg", TG * 6)
        rstdg = sb("rstdg", TG)
        norm2, inv_norm = sb("norm2", TG), sb("inv_norm", TG)
        rows1, rows2 = sb("rows1", TG * RW), sb("rows2", TG * RW)
        rt = sb("rt", 2 * E)
        xg_t = sb("xg_t", TG * D)
        logits = sb("logits", TG * 2 * E)
        sc = sb("sc", TG * E)
        hit, key = sb("hit", TG * E), sb("key", TG * E)
        oh1, oh2 = sb("oh1", TG * E), sb("oh2", TG * E)
        top1, top2, best = sb("top1", TG), sb("top2", TG), sb("best", TG)
        gap = sb("gap", TG)
        gate = sb("gate", NT * 2)
        chosen = sb("chosen", TG * E, BF16)
        before = sb("before", TG * E, BF16)
        running = sb("running", E, BF16)
        posn = sb("posn", TG * E)
        row1, row2 = sb("row1", TG, I32), sb("row2", TG, I32)
        count = sb("count", E + 1)
        tiles_e, ends = sb("tiles_e", E), sb("ends", E)
        gt = sb("gt", NS * E)
        gtw = sb("gtw", NS * E)
        coef = sb("coef", E)
        slot_e, slot_row = sb("slot_e", NS), sb("slot_row", NS)
        local, cnt_s, e_all = sb("local", NS), sb("cnt_s", NS), sb("e_all", NS)
        valid, pad_row = sb("valid", NS), sb("pad_row", NS)
        slot_e_i, slot_row_i = sb("slot_e_i", NS, I32), sb("slot_row_i", NS, I32)
        xs = sb("xs", XBUF * RW)
        xs_t = sb("xs_t", 2 * D)
        hid, hidn, hid_t = (v_heads[:, n * 2 * F:(n + 1) * 2 * F] for n in range(3))
        ys = sb("ys", 2 * D)
        ya = sb("ya", 2 * D)
        ret = sb("ret", 2, I32)
        hst, hmv, hrs = sb("hst", 6), sb("hmv", 2), sb("hrs", 2)
        yst, ymv, yrs = sb("yst", 6), sb("ymv", 2), sb("yrs", 2)
        back = xn_both[:]
        ctx_z = sb("ctx_z", B * D)
        bq1 = sb("bq1", 1)
        places = [0]

        def old_keys(width):
            a = places[0]
            places[0] += width
            return k_heads[:, a:a + width]

        xn1, xn1_t, sc1, pr1, pr1_t = (old_keys(n) for n in (TG * D, TG * D, TG * KL, TG * KL, TG * P))
        kp_a, kp_t, fold_u, fold, u1_t, u2_t, bq1_rep = (old_keys(n) for n in (*[B * KL] * 4, D, D, P))
        bias_r, bias_q = old_keys(F + D), old_keys((F + D) // 2).bitcast(BF16)
        nmax1, sum1, inv1 = sb("nmax1", TG), sb("sum1", TG), sb("inv1", TG)

        ps = ctx.enter_context(nc.psum_tensor("ps", [P, 8 * 512], F32))

        def bank(i, a=0, b=512):
            return ps[:, 512 * i + a:512 * i + b]

        zeros_ready, consts_ready = sem("zeros_ready"), sem("consts_ready")
        pool_step, dve_step, act_step = sem("pool_step"), sem("dve_step"), sem("act_step")
        in_x, in_attn0, in_ffn0, in_small1, in_ffn1 = (sem(n) for n in ("in_x", "in_attn0", "in_ffn0", "in_small1", "in_ffn1"))
        in_bias = sem("in_bias")
        bias_zeroed = sem("bias_zeroed")
        table_zeroed = sem("table_zeroed")
        pe_setup, dve_setup, act_setup = sem("pe_setup"), sem("dve_setup"), sem("act_setup")
        xn_ready, xt_done, xnt_ready, q_done, qt_ready = (sem(n) for n in ("xn_ready", "xt_done", "xnt_ready", "q_done", "qt_ready"))
        s_done, sub_done, exp_done, pt_done, ptr_ready, pv_done = (sem(n) for n in ("s_done", "sub_done", "exp_done", "pt_done", "ptr_ready", "pv_done"))
        o_ready, ot_done, ott_ready, proj_done, x_biased, added = (sem(n) for n in ("o_ready", "ot_done", "ott_ready", "proj_done", "x_biased", "added"))
        r = [dict((n, sem(f"{n}{k}")) for n in (
            "rows_ready", "rows2_ready", "xgt_done", "xgt_ready", "logits_done", "logits_read", "gap_ready", "gap_exp", "chosen_ready",
            "pos_done", "rows_placed", "scattered", "count_done", "tables_ready",
            "xst_done", "xst_ready", "h_done", "act_done", "ht_done", "ht_ready", "y_done",
            "y_read", "y_ready", "ret_ready", "combined")) for k in range(2)]
        for k in range(2):
            r[k]["loaded"] = [sem(f"loaded{k}_{n}") for n in range(XBUF)]
            r[k]["returned"] = [sem(f"returned{k}_{n}") for n in range(2)]
            r[k]["fetched"] = [sem(f"fetched{k}_{n}") for n in range(2)]
        hstat_ready, hsd_ready, hn_ready, ystat_ready, ysd_ready = (sem(n) for n in ("hstat_ready", "hsd_ready", "hn_ready", "ystat_ready", "ysd_ready"))
        folded = sem("folded")
        ln1_ready, x1t_done, x1t_ready, s1_done, s1_ready, e1_done, p1t_done, p1t_ready, pv1_done, added1 = (
            sem(n) for n in ("ln1_ready", "x1t_done", "x1t_ready", "s1_done", "s1_ready", "e1_done", "p1t_done", "p1t_ready", "pv1_done", "added1"))
        pe_setup1, act_setup1, dve_setup1 = sem("pe_setup1"), sem("act_setup1"), sem("dve_setup1")
        stored = sem("stored")

        block = ctx.enter_context(nc.Block())

        @block.sync
        def _(sp):
            for g in range(G):
                sp.dma_start(at(x, g * TG, D, TG).rearrange("p (t d) -> p t d", d=D),
                             d["x"][g].rearrange("(t p) d -> p t d", p=P)).then_inc(in_x, 16)
            sp.dma_start(ctx_n[0:KL, :].rearrange("k (b d) -> k b d", d=D),
                         d["ctx_1024"].rearrange("b k d -> k b d")).then_inc(in_attn0, 16)
            sp.dma_start(mask_u8[:], d["mask_BxS2_bk0"]).then_inc(in_attn0, 16)
            for t, n in ((wq, "W_Q"), (wk, "W_K"), (wv, "W_V"), (wo, "W_O")):
                sp.dma_start(t[:], d["L0_xattn_" + n]).then_inc(in_attn0, 16)
            for t, n in ((bq, "b_Q"), (bk, "b_K"), (bv, "b_V")):
                sp.dma_start(t[:], d["L0_xattn_" + n].rearrange("(p a) -> p a", a=1)).then_inc(in_attn0, 16)
            sp.dma_start(bo_all[:], d["L0_xattn_b_O"].partition_broadcast(P)).then_inc(in_attn0, 16)
            sp.dma_start(emb[:], d["L0_ffn_uzman_embeddings"]).then_inc(in_attn0, 16)
            sp.dma_start(cache_all[:], d["L0_ffn_onbellek_durumu"].partition_broadcast(P)).then_inc(in_attn0, 16)
            sp.wait_ge(zeros_ready, 1)
            span = REGION // P
            for e in range(E):
                sp.dma_start(xslots[e * REGION:(e + 1) * REGION, :].rearrange("(p a) w -> p (a w)", a=span),
                             zeros[:]).then_inc(table_zeroed, 16)
            sp.dma_start(xslots[E * REGION:XROWS, :].rearrange("(p a) w -> p (a w)", a=SPARE),
                         zeros[:, 0:SPARE * RW]).then_inc(table_zeroed, 16)
            sp.wait_ge(bias_zeroed, 2)
            for k in range(3):
                sp.dma_start(bias_f[0][32 * k:32 * k + E, 0:F], d["L0_ffn_b1"]).then_inc(in_bias, 16)
                sp.dma_start(bias_f[0][32 * k:32 * k + E, F:F + D], d["L0_ffn_b2"]).then_inc(in_bias, 16)
                sp.dma_start(bias_f[1][32 * k:32 * k + E, 0:F], d["L1_ffn_b1"]).then_inc(in_bias, 16)
            sp.dma_start(w1[0][:].rearrange("p (e f) -> p e f", e=E), d["L0_ffn_W1"].rearrange("e p f -> p e f")).then_inc(in_ffn0, 16)
            sp.dma_start(w2[0][:].rearrange("p (a n) -> p a n", n=D),
                         d["L0_ffn_W2"].rearrange("e (c p) n -> p (e c) n", p=P)).then_inc(in_ffn0, 16)
            sp.dma_start(fside[:].rearrange("p (t k) -> p t k", k=KL),
                         d["fside_1xSxS2_0"][0].rearrange("(t p) k -> p t k", p=P)).then_inc(in_small1, 16)
            sp.dma_start(u1[:], d["L1_xattn_W1"]).then_inc(in_small1, 16)
            sp.dma_start(u2[:], d["L1_xattn_W2"]).then_inc(in_small1, 16)
            sp.dma_start(ub1[:], d["L1_xattn_b1"].rearrange("(p a) -> p a", a=1)).then_inc(in_small1, 16)
            sp.dma_start(ub2[:], d["L1_xattn_b2"].rearrange("(p a) -> p a", a=1)).then_inc(in_small1, 16)
            sp.dma_start(router1[:], d["L1_ffn_Wr"]).then_inc(in_small1, 16)
            sp.dma_start(br_all[:], d["L1_ffn_br"].partition_broadcast(P)).then_inc(in_small1, 16)
            sp.dma_start(g1_n[:], d["L1_ffn_g1"].rearrange("e (c p) -> (e c) p", p=P)).then_inc(in_small1, 16)
            sp.dma_start(be1_n[:], d["L1_ffn_be1"].rearrange("e (c p) -> (e c) p", p=P)).then_inc(in_small1, 16)
            sp.dma_start(b2_n[:], d["L1_ffn_b2"]).then_inc(in_small1, 16)
            sp.wait_ge(table_zeroed, 16 * (E + 1))
            sp.dma_start(w1[1][:].rearrange("p (e f) -> p e f", e=E), d["L1_ffn_W1"].rearrange("e p f -> p e f")).then_inc(in_ffn1, 16)
            sp.dma_start(w2[1][:].rearrange("p (a n) -> p a n", n=D),
                         d["L1_ffn_W2"].rearrange("e (c p) n -> p (e c) n", p=P)).then_inc(in_ffn1, 16)
            sp.wait_ge(dve_setup, 4 + B)
            sp.dma_start(g2_all[:], d["L1_ffn_g2"].rearrange("e n -> (e n)").partition_broadcast(P)).then_inc(in_ffn1, 16)
            sp.dma_start(be2_all[:], d["L1_ffn_be2"].rearrange("e n -> (e n)").partition_broadcast(P)).then_inc(in_ffn1, 16)

            for k in range(2):
                m = r[k]

                def load(s, j):
                    W(sp, m["xst_done"], s - XBUF + 1)
                    W(sp, m["ret_ready"], s - XBUF + 1)
                    row = sp.value_load(slot_row_i[0:1, bass.ds(s, 1)], min_val=0, max_val=XROWS - P)
                    sp.dma_start(xs[:, j * RW:(j + 1) * RW], xslots[bass.ds(row, P), :]).then_inc(m["loaded"][j], 16)

                sp.wait_ge(m["tables_ready"], 1)
                sp.wait_ge(m["scattered"], 16 * 2 * NT)
                for s in range(XBUF):
                    load(s, s)
                with sp.Fori(1, NS // XBUF) as i:
                    for j in range(XBUF):
                        load(i * XBUF + j, j)
                for s in range(NS // XBUF * XBUF, NS):
                    load(s, s % XBUF)

                for n in range(2):
                    sp.wait_ge(m["returned"][n], 16 * ((NS + 1 - n) // 2))
                for g in range(G):
                    W(sp, m["combined"], g - 1)
                    for c in range(2):
                        sp.dma_start(back[:, ((g % 2) * 2 + c) * TG * D:][:, 0:TG * D].rearrange("p (t d) -> p t d", d=D),
                                     yslots[c * TOK + g * S:c * TOK + (g + 1) * S, :].rearrange("(t p) d -> p t d", p=P)
                                     ).then_inc(m["fetched"][g % 2], 16)
            for g in range(G):
                sp.wait_ge(r[1]["combined"], g + 1)
                sp.dma_start(out[g].rearrange("(t p) d -> p t d", p=P),
                             at(x, g * TG, D, TG).rearrange("p (t d) -> p t d", d=D)).then_inc(stored, 16)
            sp.wait_ge(stored, 16 * G)

        @block.gpsimd
        def _(pool):
            gp = nc.gpsimd
            chain = Steps(pool, pool_step)
            gp.memset(zeros[:], 0.0).then_inc(zeros_ready, 1)
            gp.memset(bias_f[0][:], 0.0).then_inc(bias_zeroed, 1)
            gp.memset(bias_f[1][:], 0.0).then_inc(bias_zeroed, 1)
            for t, v in ((ident, 0.0), (ones, 1.0), (ones_b, 1.0), (below, 1.0), (pick, 0.0), (head_of, 1.0),
                         (block_of, 1.0), (hide, 0.0), (running, 0.0), (rows1, 0.0), (rows2, 0.0), (eps, LN_EPS),
                         (ctx_z, 0.0), (shift_t, 0.0), (count, 0.0), (ctx_rep, 0.0)):
                gp.memset(t[:], v)
            chain(gp.memset(probs[:], 0.0))
            chain(gp.affine_select(out=ident[:], in_=ident[:], compare_op=ALU.not_equal, fill=1.0, base=0,
                                   pattern=[[-1, P]], channel_multiplier=1))
            chain(gp.affine_select(out=below[:], in_=below[:], compare_op=ALU.is_gt, fill=0.0, base=0,
                                   pattern=[[1, P]], channel_multiplier=-1))
            for k in range(3):
                chain(gp.affine_select(out=pick[:].rearrange("p (e m) -> p e m", e=E), in_=pick[:].rearrange("p (e m) -> p e m", e=E),
                                       compare_op=ALU.not_equal, fill=1.0, base=-32 * k,
                                       pattern=[[-1, E], [0, P]], channel_multiplier=1))
            chain(gp.affine_select(out=head_of[:], in_=head_of[:], compare_op=ALU.is_ge, fill=0.0, base=0,
                                   pattern=[[-DH, H]], channel_multiplier=1))
            chain(gp.affine_select(out=head_of[:], in_=head_of[:], compare_op=ALU.is_ge, fill=0.0, base=DH - 1,
                                   pattern=[[DH, H]], channel_multiplier=-1))
            bo = block_of[:].rearrange("p (c h) -> p c h", h=H)
            chain(gp.affine_select(out=bo, in_=bo, compare_op=ALU.is_ge, fill=0.0, base=0,
                                   pattern=[[P, NBLK], [-KL, H]], channel_multiplier=1))
            chain(gp.affine_select(out=bo, in_=bo, compare_op=ALU.is_ge, fill=0.0, base=KL - 1,
                                   pattern=[[-P, NBLK], [KL, H]], channel_multiplier=-1))
            for t, step, base, mult in ((up8, 1, 1, 0), (down8, -1, E, 0), (region0, REGION, 0, 0), (ramp16, P, 0, 0),
                                        (ramp_s, 1, 0, 0), (token_id, P, 0, 1), (dump_row, P, 2 * TOK, 1)):
                chain(gp.iota(t[:], [[step, t.shape[1]]], base=base, channel_multiplier=mult,
                              allow_small_or_imprecise_dtypes=True))
            gp.memset(neg_max[:], 0.0).then_inc(consts_ready, 1)

            pool.wait_ge(dve_setup, 3)
            pool.wait_ge(xn_ready, G)
            x3 = x[:].rearrange("p (t d) -> p t d", d=D)
            gp.tensor_tensor(x3, x3, spread(out_row[:], NT, 1), ALU.add).then_inc(x_biased, 1)

            def place_rows(k, g):
                m = r[k]
                wait_alone(pool, consts_ready, (m["rows_placed"], g + 1), (m["rows2_ready"], g + 1))
                for rows, idx in ((rows1, row1), (rows2, row2)):
                    for j in range(TG):
                        gp.indirect_dma_start(out=xslots[:, :], out_offset=bass.IndirectOffsetOnAxis(ap=idx[:, j:j + 1], axis=0),
                                              in_=rows[:, j * RW:(j + 1) * RW], in_offset=None).then_inc(m["scattered"], 16)

            def return_rows(k, s, j):
                m = r[k]
                wait_alone(pool, consts_ready, (m["y_ready"], s + 1), (m["ret_ready"], s + 1))
                gp.indirect_dma_start(out=yslots[:, :], out_offset=bass.IndirectOffsetOnAxis(ap=ret[:, j % 2:j % 2 + 1], axis=0),
                                      in_=two(ys, j), in_offset=None).then_inc(m["returned"][j % 2], 16)

            pool.wait_ge(table_zeroed, 16 * (E + 1))
            for k in range(2):
                if k == 1:
                    pool.wait_ge(act_setup1, 8)
                    pool.wait_ge(pe_setup1, 8)
                    w3 = w2[1][:].rearrange("p (a n) -> p a n", n=D)
                    gp.tensor_tensor(w3, w3, spread(g1_t[:], D), ALU.mult).then_inc(folded, 1)
                with pool.Fori(0, G) as g:
                    place_rows(k, g)
                with pool.Fori(0, NS // 2) as i:
                    for j in range(2):
                        return_rows(k, i * 2 + j, j)
                if NS % 2:
                    return_rows(k, NS - 1, 0)

        @block.tensor
        def _(pe):
            te = nc.tensor

            def mm(o, a, b, start=True, stop=True, **kw):
                return te.matmul(o, a, b, start=start, stop=stop, **kw)

            def tr(o, a, rows=P):
                return te.transpose(o, a, ident[0:rows, 0:rows])

            pe.wait_ge(consts_ready, 1)
            pe.wait_ge(in_attn0, 16 * 12)
            for b in range(B):
                last = tr(bank(0, b * KL, (b + 1) * KL), ctx_n[0:KL, b * D:(b + 1) * D], KL)
            last.then_inc(pe_setup, 1)
            pe.wait_ge(act_setup, 1)
            mm(bank(1, 0, B * KL), wk[:], ctx_t[:]).then_inc(pe_setup, 1)
            pe.wait_ge(dve_setup, 1)
            mm(bank(2, 0, D), bv_rep[:], wo[:]).then_inc(pe_setup, 1)
            pe.wait_ge(dve_setup, 2)
            tr(bank(3, 0, E), emb[:], E)
            tr(bank(3, E, 2 * E), rows1[0:E, 0:D], E).then_inc(pe_setup, 1)
            for g in range(G):
                pe.wait_ge(xn_ready, g + 1)
                for j in range(TG):
                    last = tr(bank(4 + g, j * P, (j + 1) * P), xn[:, (g * TG + j) * D:(g * TG + j + 1) * D])
                last.then_inc(xt_done, 1)
            pe.wait_ge(xnt_ready, G)
            for b in range(B):
                pe.wait_ge(act_setup, 2 + b)
                pe.wait_ge(dve_setup, 4 + max(b - 1, 0))
                for c in range(NBLK):
                    last = mm(bank(4 - b % 2 * 4, c * D, (c + 1) * D), two(ctx_rep, b, NBLK * P)[:, c * P:(c + 1) * P], wv[:])
                last.then_inc(pe_setup, 1)

            def queries(t, j):
                W(pe, qt_ready, t)
                mm(bank(6, 0, P), wq[:], at(xn_t, t, P)).then_inc(q_done, 1)

            def scores(t, j, g):
                pe.wait_ge(qt_ready, t + 1)
                W(pe, sub_done, t)
                for a in range(0, HK, 512):
                    n = min(512, HK - a)
                    mm(bank(a // 512, 0, n), two(q_t, j), k_heads[:, bass.ds(g * HK + a, n)], stop=False)
                    last = mm(bank(a // 512, 0, n), at(pick, g, P), hide[:, a:a + n], start=False)
                last.then_inc(s_done, 1)

            def turn_probs(t, j):
                pe.wait_ge(exp_done, t + 1)
                W(pe, ptr_ready, t)
                for c in range(NBLK):
                    last = tr(bank(3, c * P, (c + 1) * P), two(probs, j, NBLK * P)[:, c * P:(c + 1) * P])
                last.then_inc(pt_done, 1)

            def values(t, g):
                pe.wait_ge(ptr_ready, t + 1)
                W(pe, added, t)
                nothing = shift_t[:].bitcast(BF16)
                mm(bank(7, 0, H * VC), nothing[:, 0:P], nothing[:, 0:H * VC], stop=False, skip_group_check=True)
                for c in range(NBLK):
                    h0, h1 = c * P // KL, min(H, -(-(c + 1) * P // KL))
                    last = mm(bank(7, h0 * VC, h1 * VC), probs_t[:, c * P:(c + 1) * P],
                              v_heads[:, bass.ds(g * (NBLK * H * VC) + (c * H + h0) * VC, (h1 - h0) * VC)],
                              start=False, stop=(c == NBLK - 1), skip_group_check=True)
                last.then_inc(pv_done, 1)

            def turn_heads(t):
                pe.wait_ge(o_ready, t + 1)
                tr(bank(7, 256, 384), heads_out[:]).then_inc(ot_done, 1)

            def project(t):
                pe.wait_ge(ott_ready, t + 1)
                mm(bank(7, 384, 512), heads_t[:], wo[:]).then_inc(proj_done, 1)

            def route_turn(k, g, b):
                m = r[k]
                pe.wait_ge(m["rows_ready"], g + 1)
                for j in range(TG):
                    last = tr(bank(b, j * P, (j + 1) * P), rows1[:, j * RW:j * RW + D])
                last.then_inc(m["xgt_done"], 1)

            def route_logits(k, g, b):
                m = r[k]
                pe.wait_ge(m["xgt_ready"], g + 1)
                w, n = (rt, 2 * E) if k == 0 else (router1, E)
                for j in range(TG):
                    last = mm(bank(b, j * n, (j + 1) * n), xg_t[:, j * P:(j + 1) * P], w[:])
                last.then_inc(m["logits_done"], 1)

            def route_rank(k, g, b):
                m = r[k]
                pe.wait_ge(m["chosen_ready"], g + 1)
                mm(bank(b, 0, TG * E), below[:], chosen[:], stop=False)
                mm(bank(b, 0, TG * E), ones_b[:], before[:], start=False).then_inc(m["pos_done"], 1)

            def attend(g, first, final):
                for j in range(TG):
                    t = g * TG + j
                    if not (final and j == TG - 1):
                        scores(t + 1, j + 1, g + (j + 1) // TG)
                    if not (final and j >= TG - 2):
                        if not first and j in (2, 3):
                            pe.wait_ge(r[0]["xgt_ready" if j == 2 else "logits_read"], g)
                        queries(t + 2, j)
                    if not (first and j == 0):
                        turn_heads(t - 1)
                    turn_probs(t, j)
                    if not (first and j == 0):
                        project(t - 1)
                    if not first and j:
                        if not (final and j >= TG - 2):
                            pe.wait_ge(qt_ready, t + 3)
                        (None, route_turn, route_logits, route_rank)[j](0, g - 1, 6)
                    values(t, g)
                if not first:
                    pe.wait_ge(r[0]["rows_placed"], g)

            pe.wait_ge(dve_setup, 4 + B)
            queries(0, 0)
            scores(0, 0, 0)
            queries(1, 1)
            attend(0, True, False)
            with pe.Fori(1, G - 1) as g:
                attend(g, False, False)
            attend(G - 1, False, True)
            turn_heads(NT - 1)
            project(NT - 1)

            def route_all(k, g, banks):
                route_turn(k, g, banks[0])
                route_logits(k, g, banks[1])
                route_rank(k, g, banks[2])

            def route_count(k, b):
                mm(bank(b, 0, E), ones_b[:], running[:]).then_inc(r[k]["count_done"], 1)

            route_all(0, G - 1, (0, 1, 2))
            route_count(0, 3)

            pe.wait_ge(in_small1, 16 * 10)
            tr(bank(4, 0, P), u1[:])
            tr(bank(4, P, 2 * P), u2[:]).then_inc(pe_setup1, 1)
            pe.wait_ge(act_setup1, 1)
            mm(bank(5, 0, B * KL), u1_t[:], ctx_t[:]).then_inc(pe_setup1, 1)
            pe.wait_ge(act_setup1, 2)
            mm(bank(5, 0, B * KL), u2_t[:], kp_a[:]).then_inc(pe_setup1, 1)
            mm(bank(6, 0, 1), u2_t[:], ub1[:]).then_inc(pe_setup1, 1)
            pe.wait_ge(act_setup1, 3)
            mm(bank(5, 0, B * KL), u2[:], kp_t[:]).then_inc(pe_setup1, 1)
            pe.wait_ge(act_setup1, 4)
            mm(bank(5, 0, B * KL), u1[:], fold_u[:]).then_inc(pe_setup1, 1)
            pe.wait_ge(act_setup1, 6)

            def experts(k):
                m = r[k]

                def turn_x(s, j):
                    pe.wait_ge(m["loaded"][j % XBUF], (s - j + j // XBUF * XBUF) * (16 // XBUF) + 16)
                    W(pe, m["xst_ready"], s - 1)
                    tr(bank(6 + j % 2, 0, P), xs[:, (j % XBUF) * RW:(j % XBUF) * RW + D]).then_inc(m["xst_done"], 1)

                def hidden(s, j):
                    e = pe.value_load(slot_e_i[0:1, bass.ds(s, 1)], min_val=0, max_val=E - 1)
                    pe.wait_ge(m["xst_ready"], s + 1)
                    W(pe, m["act_done"], s - 1)
                    mm(bank(j % 2), xs_t[:, (j % 2) * D:(j % 2 + 1) * D], w1[k][:, bass.ds(e * F, F)], stop=False)
                    mm(bank(j % 2), at(pick, e, P), bias_p[k][:, 0:F], start=False).then_inc(m["h_done"], 1)

                def turn_h(s, j):
                    pe.wait_ge(m["act_done"] if k == 0 else hn_ready, s + 1)
                    W(pe, m["ht_ready"], s - 1)
                    src = hid if k == 0 else hidn
                    for c in range(FC):
                        last = tr(bank(2 + j % 2, c * P, (c + 1) * P), src[:, (j % 2) * F + c * P:][:, 0:P])
                    last.then_inc(m["ht_done"], 1)

                def output(s, j):
                    e = pe.value_load(slot_e_i[0:1, bass.ds(s, 1)], min_val=0, max_val=E - 1)
                    pe.wait_ge(m["ht_ready"], s + 1)
                    W(pe, m["y_ready" if k == 0 else "y_read"], s - 1)
                    for c in range(FC):
                        mm(bank(4 + j % 2, 0, D), hid_t[:, (j % 2) * F + c * P:][:, 0:P],
                           w2[k][:, bass.ds(e * F + c * D, D)], start=(c == 0), stop=False)
                    mm(bank(4 + j % 2, 0, D), at(pick, e, P), bias_p[k][:, F:F + D], start=False).then_inc(m["y_done"], 1)

                def tile(s, j, left):
                    turn_h(s, j)
                    if left > 2:
                        hidden(s + 2, j + 2)
                    output(s, j)
                    if left > 3:
                        turn_x(s + 3, j + 3)

                for s in range(3):
                    turn_x(s, s)
                for s in range(2):
                    hidden(s, s)
                U = XBUF
                for s in range(U):
                    tile(s, s, U)
                with pe.Fori(1, NS // U) as i:
                    for j in range(U):
                        tile(i * U + j, j, U)
                for s in range(NS // U * U, NS):
                    tile(s, s, NS - s)

            pe.wait_ge(in_ffn0, 32)
            pe.wait_ge(r[0]["tables_ready"], 1)
            experts(0)

            def attend1(g):
                m = r[1]
                pe.wait_ge(ln1_ready, g + 1)
                for j in range(TG):
                    last = tr(bank(0, j * P, (j + 1) * P), xn1[:, j * D:(j + 1) * D])
                last.then_inc(x1t_done, 1)
                pe.wait_ge(x1t_ready, g + 1)
                for j in range(TG):
                    mm(bank(1, j * KL, (j + 1) * KL), xn1_t[:, j * P:(j + 1) * P], fold[:, bass.ds(g * KL, KL)], stop=False)
                    last = mm(bank(1, j * KL, (j + 1) * KL), bq1_rep[:], kp_t[:, bass.ds(g * KL, KL)], start=False)
                last.then_inc(s1_done, 1)
                pe.wait_ge(e1_done, g + 1)
                for j in range(TG):
                    last = tr(bank(2, j * P, (j + 1) * P)[0:KL, :], pr1[:, j * KL:(j + 1) * KL])
                last.then_inc(p1t_done, 1)
                pe.wait_ge(p1t_ready, g + 1)
                for j in range(TG):
                    last = mm(bank(3, j * D, (j + 1) * D), pr1_t[:, j * P:(j + 1) * P], ctx_z[:, bass.ds(g * D, D)])
                last.then_inc(pv1_done, 1)
                route_all(1, g, (4, 5, 6))

            pe.wait_ge(in_ffn1, 64)
            tr(bank(7, 0, E * FC), g1_n[:], E * FC)
            tr(bank(7, E * FC, 2 * E * FC), be1_n[:], E * FC)
            tr(bank(7, 2 * E * FC, 2 * E * FC + E), b2_n[:], E).then_inc(pe_setup1, 1)
            pe.wait_ge(act_setup1, 8)
            for e in range(E):
                for c in range(FC):
                    a = e * FC + c
                    last = mm(bank(7, 128 + e, 129 + e), w2[1][:, a * D:(a + 1) * D], be1_t[:, a:a + 1],
                              start=(c == 0), stop=(c == FC - 1))
            last.then_inc(pe_setup1, 1)
            pe.wait_ge(dve_setup1, 1)
            tr(bank(7, 256, 384), shift_t[:]).then_inc(pe_setup1, 1)

            with pe.Fori(0, G) as g:
                attend1(g)
            route_count(1, 0)
            pe.wait_ge(r[1]["tables_ready"], 1)
            pe.wait_ge(folded, 1)
            experts(1)

        @block.scalar
        def _(act):
            sc_ = nc.scalar

            def copy(o, i, s=None):
                ins = sc_.activation(o, i, ACT.Copy)
                return ins.then_inc(s, 1) if s is not None else ins

            act.wait_ge(consts_ready, 1)
            act.wait_ge(pe_setup, 1)
            copy(ctx_t[:], bank(0, 0, B * KL), act_setup)
            act.wait_ge(act_setup, 1)
            def rep_ctx(b):
                if b >= 2:
                    act.wait_ge(pe_setup, 3 + b)
                copy(two(ctx_rep, b, NBLK * P)[:, 0:HK].rearrange("p (h k) -> p h k", k=KL),
                     spread(ctx_t[:, b * KL:(b + 1) * KL], H, 1), act_setup)

            rep_ctx(0)
            rep_ctx(1)
            for g in range(G):
                act.wait_ge(xt_done, g + 1)
                copy(at(xn_t, g, TG * P), bank(4 + g), xnt_ready)
            rep_ctx(2)
            rep_ctx(3)

            def queried(t, j):
                act.wait_ge(q_done, t + 1)
                W(act, s_done, t - 1)
                sc_.activation(two(q_t, j), bank(6, 0, P), ACT.Identity, bias=bq[:]).then_inc(qt_ready, 1)

            def exps(t, j):
                act.wait_ge(sub_done, t + 1)
                p = two(probs, j, NBLK * P)[:, 0:HK]
                sc_.activation(p, p, ACT.Exp, scale=DH ** -0.5).then_inc(exp_done, 1)

            def turned_probs(t):
                act.wait_ge(pt_done, t + 1)
                W(act, pv_done, t)
                copy(probs_t[:], bank(3, 0, NBLK * P), ptr_ready)

            def turned_heads(t):
                act.wait_ge(ot_done, t + 1)
                copy(heads_t[:], bank(7, 256, 384), ott_ready)

            def route_turned(k, g, b):
                m = r[k]
                act.wait_ge(m["xgt_done"], g + 1)
                copy(xg_t[:], bank(b), m["xgt_ready"])

            def route_rows2(k, g):
                m = r[k]
                act.wait_ge(m["rows_ready"], g + 1)
                copy(rows2[:].rearrange("p (t w) -> p t w", w=RW)[:, :, 0:D],
                     rows1[:].rearrange("p (t w) -> p t w", w=RW)[:, :, 0:D], m["rows2_ready"])

            def route_exp(k, g):
                m = r[k]
                act.wait_ge(m["gap_ready"], g + 1)
                sc_.activation(gap[:], gap[:], ACT.Exp).then_inc(m["gap_exp"], 1)

            def attend(g, first, final):
                for j in range(TG):
                    t = g * TG + j
                    exps(t, j)
                    if not (final and j >= TG - 2):
                        queried(t + 2, j)
                    if not (first and j == 0):
                        turned_heads(t - 1)
                    turned_probs(t)
                    if not first and j == 1:
                        route_rows2(0, g - 1)
                        route_turned(0, g - 1, 6)
                    if not first and j == 2:
                        route_exp(0, g - 1)

            queried(0, 0)
            queried(1, 1)
            attend(0, True, False)
            with act.Fori(1, G - 1) as g:
                attend(g, False, False)
            attend(G - 1, False, True)
            turned_heads(NT - 1)
            route_rows2(0, G - 1)
            route_turned(0, G - 1, 0)
            route_exp(0, G - 1)

            act.wait_ge(pe_setup1, 1)
            copy(u1_t[:], bank(4, 0, P))
            copy(u2_t[:], bank(4, P, 2 * P), act_setup1)
            act.wait_ge(pe_setup1, 2)
            sc_.activation(kp_a[:], bank(5, 0, B * KL), ACT.Identity, bias=ub1[:]).then_inc(act_setup1, 1)
            act.wait_ge(pe_setup1, 3)
            sc_.activation(kp_t[:], bank(5, 0, B * KL), ACT.Identity, bias=ub2[:]).then_inc(act_setup1, 1)
            act.wait_ge(pe_setup1, 5)
            copy(fold_u[:], bank(5, 0, B * KL), act_setup1)
            act.wait_ge(pe_setup1, 6)
            copy(fold[:], bank(5, 0, B * KL), act_setup1)
            sc_.activation(bq1[:], bank(6, 0, 1), ACT.Identity, bias=ub2[:]).then_inc(act_setup1, 1)
            act.wait_ge(act_setup1, 6)
            sc_.activation(bq1_rep[:], ones[:], ACT.Copy, scale=bq1[:]).then_inc(act_setup1, 1)

            def experts(k):
                m = r[k]

                def turned_x(s, j):
                    act.wait_ge(m["xst_done"], s + 1)
                    W(act, m["h_done"], s - 1)
                    copy(xs_t[:, (j % 2) * D:(j % 2 + 1) * D], bank(6 + j % 2, 0, P), m["xst_ready"])

                def turned_h(s, j):
                    act.wait_ge(m["ht_done"], s + 1)
                    W(act, m["y_done"], s - 1)
                    copy(two(hid_t, j, F), bank(2 + j % 2), m["ht_ready"])

                def activate(s, j):
                    act.wait_ge(m["h_done"], s + 1)
                    if k == 0:
                        W(act, m["ht_done"], s - 1)
                        sc_.activation(hid[:, (j % 2) * F:(j % 2 + 1) * F], bank(j % 2), ACT.Gelu).then_inc(m["act_done"], 1)
                    else:
                        W(act, hn_ready, s - 1)
                        sc_.activation(hid[:, (j % 2) * F:(j % 2 + 1) * F], bank(j % 2), ACT.Relu).then_inc(m["act_done"], 1)
                        act.wait_ge(hstat_ready, s + 1)
                        sc_.activation(hrs[:, 0:1], hmv[:, 1:2], ACT.Sqrt, bias=eps[:]).then_inc(hsd_ready, 1)

                def finish(s, j):
                    if k == 0:
                        return
                    act.wait_ge(m["y_done"], s + 1)
                    W(act, m["y_ready"], s - 1)
                    sc_.activation(ya[:, (j % 2) * D:(j % 2 + 1) * D], bank(4 + j % 2, 0, D), ACT.Relu).then_inc(m["y_read"], 1)
                    act.wait_ge(ystat_ready, s + 1)
                    sc_.activation(yrs[:, 0:1], ymv[:, 1:2], ACT.Sqrt, bias=eps[:]).then_inc(ysd_ready, 1)

                def tile(s, j, left):
                    if k == 1:
                        turned_h(s, j)
                    if left > 2:
                        activate(s + 2, j + 2)
                    finish(s, j)
                    if left > 3:
                        turned_x(s + 3, j + 3)

                turned_x(0, 0)
                turned_x(1, 1)
                activate(0, 0)
                turned_x(2, 2)
                activate(1, 1)
                U = XBUF
                for s in range(U):
                    tile(s, s, U)
                with act.Fori(1, NS // U) as i:
                    for j in range(U):
                        tile(i * U + j, j, U)
                for s in range(NS // U * U, NS):
                    tile(s, s, NS - s)

            experts(0)

            act.wait_ge(pe_setup1, 7)
            copy(g1_t[:], bank(7, 0, E * FC))
            copy(be1_t[:], bank(7, E * FC, 2 * E * FC), act_setup1)

            def attend1(g):
                act.wait_ge(x1t_done, g + 1)
                copy(xn1_t[:], bank(0), x1t_ready)
                act.wait_ge(s1_ready, g + 1)
                for j in range(TG):
                    last = sc_.activation(pr1[:, j * KL:(j + 1) * KL], sc1[:, j * KL:(j + 1) * KL], ACT.Exp,
                                          bias=nmax1[:, j:j + 1], accum_out=sum1[:, j:j + 1])
                last.then_inc(e1_done, 1)
                act.wait_ge(p1t_done, g + 1)
                copy(pr1_t[0:KL, :], bank(2)[0:KL, :], p1t_ready)
                route_rows2(1, g)
                route_turned(1, g, 4)
                route_exp(1, g)

            with act.Fori(0, G) as g:
                attend1(g)
            experts(1)

        @block.vector
        def _(dve):
            v = nc.vector
            chain = Steps(dve, dve_step)
            var_g = mvg[:].rearrange("p (t s) -> p t s", s=2)[:, :, 1]

            def rsqrt(y, a, t):
                chain(v.tensor_scalar(y.bitcast(I32), a.bitcast(I32), -0.5, RSQRT_SEED, ALU.mult, ALU.add))
                for _ in range(3):
                    chain(v.tensor_tensor(t, y, y, ALU.mult))
                    chain(v.tensor_tensor(t, t, a, ALU.mult))
                    chain(v.tensor_scalar(t, t, -0.5, 1.5, ALU.mult, ALU.add))
                    chain(v.tensor_tensor(y, y, t, ALU.mult))

            dve.wait_ge(in_x, 16 * G)
            for t in range(NT):
                last = v.bn_stats(stats[:, t * 6:(t + 1) * 6], x[:, t * D:(t + 1) * D])
            chain(last)
            for t in range(NT):
                last = v.bn_aggr(mv[:, t * 2:(t + 1) * 2], stats[:, t * 6:(t + 1) * 6])
            chain(last)
            chain(v.tensor_scalar(nw_v[:], mv[:].rearrange("p (t s) -> p t s", s=2)[:, :, 1], LN_EPS, None, ALU.add))
            rsqrt(rstd[:], nw_v[:], nw_t[:])
            for g in range(G):
                for t in range(g * TG, (g + 1) * TG):
                    last = v.tensor_scalar(xn[:, t * D:(t + 1) * D], x[:, t * D:(t + 1) * D], mv[:, 2 * t:2 * t + 1],
                                           rstd[:, t:t + 1], ALU.subtract, ALU.mult)
                last.then_inc(xn_ready, 1)

            dve.wait_ge(consts_ready, 1)
            dve.wait_ge(in_attn0, 16 * 12)
            v.tensor_scalar(bv_rep[:], ones[:], bv[:], None, ALU.mult).then_inc(dve_setup, 1)
            chain(v.tensor_tensor(rows2[0:E, 0:D], emb[:], emb[:], ALU.mult))
            chain(v.reduce_sum(nw_v[0:E, 0:1], rows2[0:E, 0:D], AX.X))
            rsqrt(norm2[0:E, 0:1], nw_v[0:E, 0:1], nw_t[0:E, 0:1])
            chain(v.tensor_tensor(nw_v[0:E, 0:1], nw_v[0:E, 0:1], norm2[0:E, 0:1], ALU.mult))
            chain(v.tensor_scalar(nw_v[0:E, 0:1], nw_v[0:E, 0:1], NORM_EPS, None, ALU.add))
            chain(v.reciprocal(nw_t[0:E, 0:1], nw_v[0:E, 0:1]))
            v.tensor_scalar(rows1[0:E, 0:D], emb[:], nw_t[0:E, 0:1], None, ALU.mult).then_inc(dve_setup, 1)
            dve.wait_ge(pe_setup, 3)
            v.tensor_tensor(out_row[:], bank(2, 0, D), bo_all[:], ALU.add).then_inc(dve_setup, 1)
            chain(v.tensor_scalar(k_t[:], bank(1, 0, B * KL), bk[:], None, ALU.add))
            dve.wait_ge(pe_setup, 4)
            v.tensor_copy(rt[:], bank(3, 0, 2 * E))
            v.tensor_scalar(cache_all[:], cache_all[:], 0.1, None, ALU.mult)
            v.tensor_scalar(hide[0:B, :].rearrange("b (h k) -> b h k", k=KL), spread(mask_u8[:], H, 1), HIDE, None, ALU.mult)
            for b in range(B):
                last = v.tensor_tensor(k_heads[:, b * HK:(b + 1) * HK].rearrange("p (h k) -> p h k", k=KL),
                                       spread(k_t[:, b * KL:(b + 1) * KL], H, 1), spread(head_of[:], KL), ALU.mult)
            last.then_inc(dve_setup, 1)
            for b in range(B):
                vh = v_heads[:, b * NBLK * H * VC:(b + 1) * NBLK * H * VC].rearrange("p (c v) -> p c v", v=VC)
                v.tensor_copy(vh[:, :, DH], block_of[:])
                dve.wait_ge(pe_setup, 5 + b)
                v.tensor_tensor(vh[:, :, 0:DH], bank(4 - b % 2 * 4, 0, NBLK * D).rearrange("p (c v) -> p c v", v=DH),
                                spread(block_of[:], DH), ALU.mult).then_inc(dve_setup, 1)

            def maxima(t, j):
                dve.wait_ge(s_done, t + 1)
                nm = two(neg_max, j, H)
                chain(v.tensor_reduce(nm, bank(0, 0, HK).rearrange("p (h k) -> p h k", k=KL), AX.X, ALU.max, negate=True))

            def subtract(t, j):
                W(dve, pt_done, t - 1)
                nm = two(neg_max, j, H)
                v.tensor_tensor(two(probs, j, NBLK * P)[:, 0:HK].rearrange("p (h k) -> p h k", k=KL),
                                bank(0, 0, HK).rearrange("p (h k) -> p h k", k=KL), spread(nm, KL), ALU.add).then_inc(sub_done, 1)

            def divide(t):
                dve.wait_ge(pv_done, t + 1)
                o = bank(7, 0, H * VC).rearrange("p (h v) -> p h v", v=VC)
                chain(v.reciprocal(inv[:], o[:, :, DH]))
                W(dve, ot_done, t)
                v.tensor_tensor(heads_out[:].rearrange("p (h v) -> p h v", v=DH), o[:, :, 0:DH], spread(inv[:], DH),
                                ALU.mult).then_inc(o_ready, 1)

            def add(t):
                dve.wait_ge(proj_done, t + 1)
                dve.wait_ge(x_biased, 1)
                v.tensor_tensor(at(x, t, D), bank(7, 384, 512), at(x, t, D), ALU.add).then_inc(added, 1)

            def group_stats(g):
                for j in range(TG):
                    last = v.bn_stats(statg[:, j * 6:(j + 1) * 6], at(x, g * TG + j, D))
                chain(last, consts_ready)
                for j in range(TG):
                    last = v.bn_aggr(mvg[:, j * 2:(j + 1) * 2], statg[:, j * 6:(j + 1) * 6])
                chain(last)
                chain(v.tensor_scalar(nw_v[:, 0:TG], var_g, LN_EPS, None, ALU.add))
                rsqrt(rstdg[:], nw_v[:, 0:TG], nw_t[:, 0:TG])

            def route_norm(k, g):
                m = r[k]
                wait_alone(dve, consts_ready, (m["scattered"], g * (16 * 2 * TG)),
                           (added, (g + 1) * TG) if k == 0 else (m["combined"], 0))
                group_stats(g)
                for j in range(TG):
                    last = v.tensor_scalar(rows1[:, j * RW:j * RW + D], at(x, g * TG + j, D), mvg[:, 2 * j:2 * j + 1],
                                           rstdg[:, j:j + 1], ALU.subtract, ALU.mult)
                for rows, base in ((rows1, 0.0), (rows2, float(TOK))):
                    last = v.tensor_scalar(rows[:].rearrange("p (t w) -> p t w", w=RW)[:, :, D], at(token_id, g, TG),
                                           base, None, ALU.add)
                last.then_inc(m["rows_ready"], 1)
                if k == 0:
                    chain(v.tensor_tensor(norm2[:], var_g, rstdg[:], ALU.mult))
                    chain(v.tensor_tensor(norm2[:], norm2[:], rstdg[:], ALU.mult))
                    chain(v.tensor_scalar(norm2[:], norm2[:], float(D), None, ALU.mult))
                    rsqrt(inv_norm[:], norm2[:], nw_t[:, 0:TG])
                    chain(v.tensor_tensor(norm2[:], norm2[:], inv_norm[:], ALU.mult))
                    chain(v.tensor_scalar(norm2[:], norm2[:], NORM_EPS, None, ALU.add))
                    chain(v.reciprocal(inv_norm[:], norm2[:]))

            def by_e(t):
                return t[:].rearrange("p (t e) -> p t e", e=E)

            def route_read(k, g, b):
                m = r[k]
                n = (2 if k == 0 else 1) * TG * E
                dve.wait_ge(m["logits_done"], g + 1)
                v.tensor_copy(logits[:, 0:n], bank(b, 0, n)).then_inc(m["logits_read"], 1)

            def pick_one(values, value, ramp, onehot, op):
                chain(v.tensor_reduce(value, values, AX.X, op))
                chain(v.tensor_tensor(by_e(hit), values, spread(value, E), ALU.is_equal))
                chain(v.tensor_tensor(by_e(key), by_e(hit), spread(ramp[:], TG, 1), ALU.mult))
                chain(v.tensor_reduce(best[:], by_e(key), AX.X, ALU.max))
                chain(v.tensor_tensor(by_e(onehot), by_e(key), spread(best[:], E), ALU.is_equal))

            def route_choose(k, g):
                m = r[k]
                dve.wait_ge(m["logits_read"], g + 1)
                if k == 0:
                    pair = logits[:].rearrange("p (t e) -> p t e", e=2 * E)
                    pick_one(pair[:, :, 0:E], top1[:], up8, oh1, ALU.min)
                    chain(v.tensor_tensor(by_e(sc), pair[:, :, E:2 * E], spread(inv_norm[:], E), ALU.mult))
                    chain(v.tensor_tensor(by_e(sc), by_e(sc), spread(cache_all[:], TG, 1), ALU.add))
                    chain(v.scalar_tensor_tensor(sc[:], oh1[:], DROP, sc[:], ALU.mult, ALU.add))
                else:
                    chain(v.tensor_tensor(by_e(sc), logits[:, 0:TG * E].rearrange("p (t e) -> p t e", e=E),
                                          spread(br_all[:], TG, 1), ALU.add))
                pick_one(by_e(sc), top1[:], down8, oh1, ALU.max)
                chain(v.scalar_tensor_tensor(sc[:], oh1[:], 2 * DROP, sc[:], ALU.mult, ALU.add))
                pick_one(by_e(sc), top2[:], down8, oh2, ALU.max)
                v.tensor_tensor(gap[:], top2[:], top1[:], ALU.subtract).then_inc(m["gap_ready"], 1)
                chain(v.tensor_tensor(chosen[:], oh1[:], oh2[:], ALU.add))
                chain(v.tensor_copy(before[:, 0:E], running[:]))
                for j in range(1, TG):
                    chain(v.tensor_tensor(before[:, j * E:(j + 1) * E], before[:, (j - 1) * E:j * E],
                                          chosen[:, (j - 1) * E:j * E], ALU.add))
                v.tensor_tensor(running[:], before[:, (TG - 1) * E:], chosen[:, (TG - 1) * E:], ALU.add).then_inc(m["chosen_ready"], 1)

            def route_gates(k, g):
                m = r[k]
                dve.wait_ge(m["gap_exp"], g + 1)
                chain(v.tensor_scalar(top1[:], gap[:], 1.0, None, ALU.add))
                gg = at(gate, g, 2 * TG).rearrange("p (t c) -> p t c", c=2)
                chain(v.reciprocal(best[:], top1[:]))
                v.tensor_copy(gg[:, :, 0], best[:])
                chain(v.tensor_tensor(gg[:, :, 1], best[:], gap[:], ALU.mult))

            def route_place(k, g, b):
                m = r[k]
                dve.wait_ge(m["pos_done"], g + 1)
                chain(v.tensor_tensor(by_e(posn), bank(b, 0, TG * E).rearrange("p (t e) -> p t e", e=E), spread(region0[:], TG, 1), ALU.add))
                for oh, row, part in ((oh1, row1, top1), (oh2, row2, top2)):
                    chain(v.tensor_tensor(key[:], oh[:], posn[:], ALU.mult))
                    chain(v.tensor_reduce(part[:], by_e(key), AX.X, ALU.add))
                    last = v.tensor_copy(row[:], part[:])
                last.then_inc(m["rows_placed"], 1)

            def tables(k, b):
                m = r[k]
                dve.wait_ge(m["count_done"], 1)
                chain(v.tensor_copy(count[:, 0:E], bank(b, 0, E)))
                n16 = TOK // P
                g16 = gt[:, 0:E * n16].rearrange("p (e n) -> p e n", n=n16)
                chain(v.tensor_tensor(g16, spread(count[:, 0:E], n16), spread(ramp16[:], E, 1), ALU.is_gt))
                chain(v.tensor_reduce(tiles_e[:], g16, AX.X, ALU.add))
                chain(v.tensor_copy(ends[:, 0:1], tiles_e[:, 0:1]))
                for e in range(1, E):
                    chain(v.tensor_tensor(ends[:, e:e + 1], ends[:, e - 1:e], tiles_e[:, e:e + 1], ALU.add))
                g3, w3 = (t[:].rearrange("p (s e) -> p s e", e=E) for t in (gt, gtw))
                chain(v.tensor_tensor(g3, spread(ramp_s[:], E), spread(ends[:], NS, 1), ALU.is_ge))
                chain(v.tensor_reduce(slot_e[:], g3[:, :, 0:E - 1], AX.X, ALU.add))
                v.tensor_copy(slot_e_i[:], slot_e[:])
                chain(v.tensor_scalar(coef[:], tiles_e[:], -float(P), float(REGION), ALU.mult, ALU.add))
                chain(v.tensor_tensor(w3, g3, spread(coef[:], NS, 1), ALU.mult))
                chain(v.tensor_reduce(slot_row[:], w3, AX.X, ALU.add))
                chain(v.scalar_tensor_tensor(slot_row[:], ramp_s[:], float(P), slot_row[:], ALU.mult, ALU.add))
                v.tensor_copy(slot_row_i[:], slot_row[:])
                chain(v.tensor_reduce(e_all[:], g3, AX.X, ALU.add))
                chain(v.scalar_tensor_tensor(local[:], e_all[:], -float(REGION), slot_row[:], ALU.mult, ALU.add))
                chain(v.tensor_tensor(coef[:], count[:, 1:E + 1], count[:, 0:E], ALU.subtract))
                chain(v.tensor_tensor(w3, g3, spread(coef[:], NS, 1), ALU.mult))
                chain(v.tensor_reduce(cnt_s[:], w3, AX.X, ALU.add))
                chain(v.tensor_scalar(cnt_s[:], cnt_s[:], count[:, 0:1], token_id[:, 0:1], ALU.add, ALU.subtract))
                chain(v.tensor_tensor(valid[:], local[:], cnt_s[:], ALU.is_lt))
                chain(v.tensor_scalar(pad_row[:], valid[:], -1.0, 1.0, ALU.mult, ALU.add))
                v.tensor_tensor(pad_row[:], pad_row[:], dump_row[:], ALU.mult).then_inc(m["tables_ready"], 1)
                dve.wait_ge(m["tables_ready"], 1)

            def bias_parts(k):
                chain(v.tensor_copy(bias_p[k][:], bias_f[k][:]))
                chain(v.tensor_tensor(bias_r[:], bias_f[k][:], bias_p[k][:], ALU.subtract))
                chain(v.tensor_copy(bias_q[:], bias_r[:]))
                chain(v.tensor_tensor(bias_r[:], bias_r[:], bias_q[:], ALU.subtract))
                chain(v.tensor_copy(bias_p[k][32:64, :], bias_q[32:64, :]))
                chain(v.tensor_copy(bias_p[k][64:96, :], bias_r[64:96, :]))

            def attend(g, first, final):
                for j in range(TG):
                    t = g * TG + j
                    if not (first and j == 0):
                        divide(t - 1)
                    if not (final and j == TG - 1):
                        maxima(t + 1, j + 1)
                    if not (first and j == 0):
                        add(t - 1)
                    if not first and j == 2:
                        route_read(0, g - 1, 6)
                    if not first and j == 3:
                        route_gates(0, g - 1)
                        route_place(0, g - 1, 6)
                    if not (final and j == TG - 1):
                        subtract(t + 1, j + 1)
                    if not first and j == 0:
                        route_norm(0, g - 1)
                    if not first and j == 2:
                        route_choose(0, g - 1)

            maxima(0, 0)
            subtract(0, 0)
            attend(0, True, False)
            with dve.Fori(1, G - 1) as g:
                chain.enter(g - 1, DVE_GROUP)
                attend(g, False, False)
                chain.leave(G - 2)
            attend(G - 1, False, True)
            divide(NT - 1)
            add(NT - 1)
            route_norm(0, G - 1)
            route_read(0, G - 1, 1)
            route_choose(0, G - 1)
            route_gates(0, G - 1)
            route_place(0, G - 1, 2)
            dve.wait_ge(in_bias, 16 * 9)
            bias_parts(0)
            tables(0, 3)

            def experts(k):
                m = r[k]

                def returns(s, j):
                    dve.wait_ge(m["loaded"][j % XBUF], (s - j + j // XBUF * XBUF) * (16 // XBUF) + 16)
                    W(dve, m["returned"][j % 2], (s - j) * 8 + j // 2 * 16)
                    v.tensor_scalar(ret[:, j % 2:j % 2 + 1], xs[:, (j % XBUF) * RW + D:][:, 0:1], at(valid, s, 1), at(pad_row, s, 1),
                                    ALU.mult, ALU.add).then_inc(m["ret_ready"], 1)

                def turned_h(s, j):
                    dve.wait_ge(m["ht_done"], s + 1)
                    W(dve, m["y_done"], s - 1)
                    v.tensor_copy(hid_t[:, (j % 2) * F:(j % 2 + 1) * F], bank(2 + j % 2)).then_inc(m["ht_ready"], 1)

                def normalise_h(s, j):
                    dve.wait_ge(m["act_done"], s + 1)
                    h = hid[:, (j % 2) * F:(j % 2 + 1) * F]
                    chain(v.bn_stats(hst[:], h), consts_ready)
                    v.bn_aggr(hmv[:], hst[:]).then_inc(hstat_ready, 1)
                    dve.wait_ge(hsd_ready, s + 1)
                    chain(v.reciprocal(hrs[:, 1:2], hrs[:, 0:1]))
                    W(dve, m["ht_done"], s - 1)
                    v.tensor_scalar(hidn[:, (j % 2) * F:(j % 2 + 1) * F], h, hmv[:, 0:1], hrs[:, 1:2],
                                    ALU.subtract, ALU.mult).then_inc(hn_ready, 1)

                def finish(s, j):
                    o = ys[:, (j % 2) * D:(j % 2 + 1) * D]
                    if k == 0:
                        dve.wait_ge(m["y_done"], s + 1)
                        W(dve, m["returned"][j % 2], (s - j) * 8 + j // 2 * 16)
                        v.tensor_copy(o, bank(4 + j % 2, 0, D)).then_inc(m["y_ready"], 1)
                        return
                    a = ya[:, (j % 2) * D:(j % 2 + 1) * D]
                    dve.wait_ge(m["y_read"], s + 1)
                    chain(v.bn_stats(yst[:], a), consts_ready)
                    v.bn_aggr(ymv[:], yst[:]).then_inc(ystat_ready, 1)
                    dve.wait_ge(ysd_ready, s + 1)
                    chain(v.reciprocal(yrs[:, 1:2], yrs[:, 0:1]))
                    chain(v.tensor_scalar(a, a, ymv[:, 0:1], yrs[:, 1:2], ALU.subtract, ALU.mult))
                    e = dve.value_load(slot_e_i[0:1, bass.ds(s, 1)], min_val=0, max_val=E - 1)
                    chain(v.tensor_tensor(a, a, at(g2_all, e, D), ALU.mult))
                    W(dve, m["returned"][j % 2], (s - j) * 8 + j // 2 * 16)
                    v.tensor_tensor(o, a, at(be2_all, e, D), ALU.add).then_inc(m["y_ready"], 1)

                def tile(s, j, left):
                    returns(s, j)
                    if k == 0:
                        turned_h(s, j)
                    if k == 1 and left > 2:
                        normalise_h(s + 2, j + 2)
                    finish(s, j)

                if k == 1:
                    normalise_h(0, 0)
                    normalise_h(1, 1)
                U = XBUF
                for s in range(U):
                    tile(s, s, U)
                with dve.Fori(1, NS // U) as i:
                    chain.enter(i - 1, U * DVE_TILE[k])
                    for j in range(U):
                        tile(i * U + j, j, U)
                    chain.leave(NS // U - 1)
                for s in range(NS // U * U, NS):
                    tile(s, s, NS - s)

            experts(0)

            def combine(k, g, j):
                m = r[k]
                dve.wait_ge(m["fetched"][j], (g - j) * 16 + 32)
                for c in range(2):
                    for i in range(TG):
                        last = v.scalar_tensor_tensor(at(x, g * TG + i, D), back[:, ((j * 2 + c) * TG + i) * D:][:, 0:D],
                                                      gate[:, bass.ds((g * TG + i) * 2 + c, 1)], at(x, g * TG + i, D), ALU.mult, ALU.add)
                    if c == 0:
                        chain(last)
                last.then_inc(m["combined"], 1)
                wait_alone(dve, consts_ready, (m["combined"], g + 1))

            dve.wait_ge(pe_setup1, 8)
            chain(v.tensor_copy(coef[:], bank(7, 2 * E * FC, 2 * E * FC + E)))
            for n in range(3):
                ins = v.tensor_tensor(shift_t[:, 32 * n:32 * n + E], bank(7, 128, 128 + E), coef[:], ALU.add)
            ins.then_inc(dve_setup1, 1)
            dve.wait_ge(pe_setup1, 9)
            chain(v.tensor_copy(bias_f[1][:, F:F + D], bank(7, 256, 384)))
            bias_parts(1)
            v.memset(running[:], 0.0)
            v.memset(pr1_t[:], 0.0)
            chain(v.tensor_copy(ctx_z[0:KL, :], ctx_n[0:KL, :]))

            def attend1(g, j):
                combine(0, g, j)
                group_stats(g)
                for i in range(TG):
                    last = v.tensor_scalar(xn1[:, i * D:(i + 1) * D], at(x, g * TG + i, D), mvg[:, 2 * i:2 * i + 1],
                                           rstdg[:, i:i + 1], ALU.subtract, ALU.mult)
                last.then_inc(ln1_ready, 1)
                dve.wait_ge(s1_done, g + 1)
                chain(v.scalar_tensor_tensor(sc1[:], bank(1, 0, TG * KL), D ** -0.5, fside[:], ALU.mult, ALU.add))
                v.tensor_reduce(nmax1[:], sc1[:].rearrange("p (t k) -> p t k", k=KL), AX.X, ALU.max, negate=True).then_inc(s1_ready, 1)
                dve.wait_ge(e1_done, g + 1)
                chain(v.reciprocal(inv1[:], sum1[:]))
                dve.wait_ge(pv1_done, g + 1)
                for i in range(TG):
                    last = v.scalar_tensor_tensor(at(x, g * TG + i, D), bank(3, i * D, (i + 1) * D), inv1[:, i:i + 1],
                                                  at(x, g * TG + i, D), ALU.mult, ALU.add)
                chain(last)
                route_norm(1, g)
                route_read(1, g, 5)
                route_choose(1, g)
                route_gates(1, g)
                route_place(1, g, 6)

            with dve.Fori(0, G // 2) as i:
                chain.enter(i, DVE_GROUP1)
                for j in range(2):
                    attend1(i * 2 + j, j)
                chain.leave(G // 2)
            tables(1, 0)
            experts(1)
            with dve.Fori(0, G // 2) as i:
                chain.enter(i, DVE_LAST)
                for j in range(2):
                    combine(1, i * 2 + j, j)
                chain.leave(G // 2)


INPUTS = ["x", "ctx_1024", "fside_1xSxS2_0", "mask_BxS2_bk0", "L0_xattn_W_Q", "L0_xattn_b_Q", "L0_xattn_W_K", "L0_xattn_b_K",
          "L0_xattn_W_V", "L0_xattn_b_V", "L0_xattn_W_O", "L0_xattn_b_O", "L0_ffn_uzman_embeddings", "L0_ffn_W1", "L0_ffn_b1",
          "L0_ffn_W2", "L0_ffn_b2", "L0_ffn_onbellek_durumu", "L1_xattn_W1", "L1_xattn_b1", "L1_xattn_W2", "L1_xattn_b2",
          "L1_ffn_Wr", "L1_ffn_br", "L1_ffn_W1", "L1_ffn_b1", "L1_ffn_g1", "L1_ffn_be1", "L1_ffn_W2", "L1_ffn_b2",
          "L1_ffn_g2", "L1_ffn_be2"]


def kernel(**inputs):
    import numpy as np
    import concourse.bacc as bacc
    from concourse.bass_utils import run_bass_kernel_spmd

    nc = bacc.Bacc("TRN2", target_bir_lowering=False, num_devices=1)
    arrays, d = {}, {}
    for name in INPUTS:
        a = np.ascontiguousarray(inputs[name])
        arrays["in_" + name] = a
        d[name] = nc.dram_tensor("in_" + name, a.shape, mybir.dt.from_np(a.dtype), kind="ExternalInput").ap()
    out = nc.dram_tensor("out", (B, S, D), F32, kind="ExternalOutput").ap()
    xslots = nc.dram_tensor("xslots", (XROWS, RW), F32, kind="Internal").ap()
    yslots = nc.dram_tensor("yslots", (YROWS, D), F32, kind="Internal").ap()
    build(nc, d, out, xslots, yslots)
    return run_bass_kernel_spmd(nc, [arrays], core_ids=[0]).results[0]["out"]
```

```python
from contextlib import ExitStack

import concourse.bass as bass
from concourse import mybir

F32, BF16, I32, U8 = mybir.dt.float32, mybir.dt.bfloat16, mybir.dt.int32, mybir.dt.uint8
ALU = mybir.AluOpType
ACT = mybir.ActivationFunctionType
AX = mybir.AxisListType

P = 128
B, S, D = 4, 512, 128
TOK = B * S
NT = TOK // P
G = B
TG = NT // G
KL = 77
H, DH = 16, 8
HK = H * KL
NBLK = -(-HK // P)
VC = DH + 1
E, F = 8, 512
FC = F // P
NS = (2 * TOK + E * (P - 1)) // P
SPARE = NS - 2 * TOK // P
REGION = TOK + P
RW = D + 4
XROWS = E * REGION + SPARE * P
YROWS = 2 * TOK + NS * P
LN_EPS = 1e-5
NORM_EPS = 1e-8
HIDE = -float(2 ** 100)
DROP = -1e30
RSQRT_SEED = 1597463007.0
XBUF = 4
DVE_GROUP, DVE_GROUP1, DVE_LAST = 69, 43, 1
DVE_TILE = (0, 4)


class Steps:

    def __init__(self, eng, sem):
        self.eng, self.sem, self.base, self.n = eng, sem, 0, 0

    def __call__(self, ins, consts_ready=None):
        ins.then_inc(self.sem, 1)
        self.n += 1
        if consts_ready is not None:
            return wait_alone(self.eng, consts_ready, (self.sem, self.base + self.n))
        self.eng.wait_ge(self.sem, self.base + self.n)

    def enter(self, i, per):
        self.outer = self.base + self.n
        self.base, self.n, self.per = self.outer + i * per, 0, per

    def leave(self, passes):
        assert self.n == self.per, (self.n, self.per)
        self.base, self.n = self.outer + passes * self.per, 0


def W(eng, sem, n):
    if not isinstance(n, int) or n > 0:
        eng.wait_ge(sem, n)


def wait_alone(eng, consts_ready, *waits):
    waits = [(sem, n if isinstance(n, int) else eng.to_reg(n)) for sem, n in waits]
    eng.wait_ge(consts_ready, 1)
    for sem, n in waits:
        W(eng, sem, n)


def two(tensor, j, w=D):
    return tensor[:, (j % 2) * w:(j % 2 + 1) * w]


def uses(s, j, n=XBUF):
    return (s - j % n) * (16 // n)


def at(tensor, i, w, n=1):
    return tensor[:, bass.ds(i * w, n * w)]


def spread(ap, n, axis=2):
    ap = ap.unsqueeze(axis)
    shape = list(ap.shape)
    shape[axis] = n
    return ap.broadcast_to(shape)


def build(nc, d, out, xslots, yslots):
    ctx = ExitStack()

    def sb(name, width, dt=F32, rows=P):
        return ctx.enter_context(nc.sbuf_tensor(name, [rows, width], dt))

    def sem(name):
        return ctx.enter_context(nc.semaphore(name))

    with ctx:
        ident = sb("ident", P)
        ones = sb("ones", P)
        ones_b = sb("ones_b", P, BF16)
        below = sb("below", P, BF16)
        pick = sb("pick", E * P, BF16)
        head_of = sb("head_of", H)
        block_of = sb("block_of", NBLK * H)
        up8, down8 = sb("up8", E), sb("down8", E)
        region0 = sb("region0", E)
        ramp16 = sb("ramp16", TOK // P)
        ramp_s = sb("ramp_s", NS)
        token_id = sb("token_id", NT)
        dump_row = sb("dump_row", NS)
        eps = sb("eps", 1)
        x = sb("x", NT * D)
        ctx_n = sb("ctx_n", B * D)
        mask_u8 = sb("mask_u8", KL, U8, B)
        wq, wk, wv, wo = sb("wq", D), sb("wk", D), sb("wv", D), sb("wo", D)
        bq, bk, bv = sb("bq", 1), sb("bk", 1), sb("bv", 1)
        bo_all = sb("bo_all", D)
        emb = sb("emb", D, F32, E)
        cache_all = sb("cache_all", E)
        fside = sb("fside", TG * KL)
        u1, u2 = sb("u1", D), sb("u2", D)
        ub1, ub2 = sb("ub1", 1), sb("ub2", 1)
        router1 = sb("router1", E)
        br_all = sb("br_all", E)
        w1 = [sb(f"w1_{n}", E * F) for n in range(2)]
        zeros = w1[1][:, 0:REGION // P * RW]
        w2 = [sb(f"w2_{n}", E * FC * D) for n in range(2)]
        bias_f = [sb(f"bias_f{n}", F + D) for n in range(2)]
        bias_p = [sb(f"bias_p{n}", F + D, BF16) for n in range(2)]
        g1_n, be1_n = sb("g1_n", P, F32, E * FC), sb("be1_n", P, F32, E * FC)
        b2_n = sb("b2_n", D, F32, E)
        g1_t, be1_t = sb("g1_t", E * FC), sb("be1_t", E * FC)
        shift_t = sb("shift_t", P)
        ctx_t = sb("ctx_t", B * KL)
        k_t = sb("k_t", B * KL)
        ctx_rep = sb("ctx_rep", 2 * NBLK * P)
        g2_all, be2_all = ctx_rep[:, 0:E * D], ctx_rep[:, E * D:2 * E * D]
        k_heads = sb("k_heads", B * HK)
        v_heads = sb("v_heads", B * NBLK * H * VC)
        hide = sb("hide", HK, BF16)
        out_row = sb("out_row", D)
        bv_rep = sb("bv_rep", D)
        stats = sb("stats", NT * 6)
        mv = sb("mv", NT * 2)
        rstd = sb("rstd", NT)
        nw_v, nw_t = sb("nw_v", NT), sb("nw_t", NT)
        xn_both = sb("xn_both", 2 * NT * D)
        xn, xn_t = xn_both[:, 0:NT * D], xn_both[:, NT * D:]
        q_t = sb("q_t", 2 * D)
        neg_max = sb("neg_max", 2 * H)
        probs = sb("probs", 2 * NBLK * P)
        probs_t = sb("probs_t", NBLK * P)
        inv = sb("inv", H)
        heads_out = sb("heads_out", D)
        heads_t = sb("heads_t", D)
        mvg = sb("mvg", 2 * TG * 2)
        statg = sb("statg", 2 * TG * 6)
        rstdg = sb("rstdg", 2 * TG)
        norm2, inv_norm = sb("norm2", TG), sb("inv_norm", TG)
        rows1, rows2 = sb("rows1", TG * RW), sb("rows2", TG * RW)
        rt = sb("rt", 2 * E)
        xg_t = sb("xg_t", TG * D)
        logits = sb("logits", TG * 2 * E)
        sc = sb("sc", TG * E)
        hit, key = sb("hit", TG * E), sb("key", TG * E)
        oh1, oh2 = sb("oh1", TG * E), sb("oh2", TG * E)
        top1, top2, best = sb("top1", TG), sb("top2", TG), sb("best", TG)
        gap = sb("gap", TG)
        gate = sb("gate", NT * 2)
        chosen = sb("chosen", TG * E, BF16)
        before = sb("before", TG * E, BF16)
        running = sb("running", E, BF16)
        posn = sb("posn", TG * E)
        row1, row2 = sb("row1", TG, I32), sb("row2", TG, I32)
        count = sb("count", E + 1)
        tiles_e, ends = sb("tiles_e", E), sb("ends", E)
        gt = sb("gt", NS * E)
        gtw = sb("gtw", NS * E)
        coef = sb("coef", E)
        slot_e, slot_row = sb("slot_e", NS), sb("slot_row", NS)
        local, cnt_s, e_all = sb("local", NS), sb("cnt_s", NS), sb("e_all", NS)
        valid, pad_row = sb("valid", NS), sb("pad_row", NS)
        slot_e_i, slot_row_i = sb("slot_e_i", NS, I32), sb("slot_row_i", NS, I32)
        xs = sb("xs", XBUF * RW)
        xs_t = sb("xs_t", 2 * D)
        hid, hidn, hid_t = (v_heads[:, n * 2 * F:(n + 1) * 2 * F] for n in range(3))
        ys = v_heads[:, 6 * F:6 * F + XBUF * D]
        ya = v_heads[:, 7 * F:7 * F + 2 * D]
        ret = sb("ret", XBUF, I32)
        hst, hmv, hrs = sb("hst", 6), sb("hmv", 2), sb("hrs", 2)
        yst, ymv, yrs = sb("yst", 6), sb("ymv", 2), sb("yrs", 2)
        back = xn_both[:]
        rows_all = v_heads[:, 0:G * 2 * TG * RW]
        ctx_z = sb("ctx_z", B * D)
        bq1 = sb("bq1", 1)
        places = [0]

        def old_keys(width):
            a = places[0]
            places[0] += width
            return k_heads[:, a:a + width]

        xn1, xn1_t, sc1, pr1, pr1_t = (old_keys(n) for n in (TG * D, TG * D, TG * KL, TG * KL, TG * P))
        kp_a, kp_t, fold_u, fold, u1_t, u2_t, bq1_rep = (old_keys(n) for n in (*[B * KL] * 4, D, D, P))
        bias_r, bias_q = old_keys(F + D), old_keys((F + D) // 2).bitcast(BF16)
        q_row, fside_q = kp_a, fold_u
        nmax1, sum1, inv1 = sb("nmax1", TG), sb("sum1", TG), sb("inv1", TG)

        ps = ctx.enter_context(nc.psum_tensor("ps", [P, 8 * 512], F32))

        def bank(i, a=0, b=512):
            return ps[:, 512 * i + a:512 * i + b]

        zeros_ready, consts_ready = sem("zeros_ready"), sem("consts_ready")
        pool_step, dve_step, act_step = sem("pool_step"), sem("dve_step"), sem("act_step")
        in_x, in_attn0, in_ffn0, in_small1, in_ffn1 = (sem(n) for n in ("in_x", "in_attn0", "in_ffn0", "in_small1", "in_ffn1"))
        in_bias = sem("in_bias")
        bias_zeroed = sem("bias_zeroed")
        table_zeroed = sem("table_zeroed")
        pe_setup, dve_setup, act_setup = sem("pe_setup"), sem("dve_setup"), sem("act_setup")
        xn_ready, xt_done, xnt_ready, q_done, qt_ready = (sem(n) for n in ("xn_ready", "xt_done", "xnt_ready", "q_done", "qt_ready"))
        s_done, sub_done, exp_done, pt_done, ptr_ready, pv_done = (sem(n) for n in ("s_done", "sub_done", "exp_done", "pt_done", "ptr_ready", "pv_done"))
        o_ready, ot_done, ott_ready, proj_done, x_biased, added = (sem(n) for n in ("o_ready", "ot_done", "ott_ready", "proj_done", "x_biased", "added"))
        r = [dict((n, sem(f"{n}{k}")) for n in (
            "rows_ready", "rows2_ready", "xgt_done", "xgt_ready", "logits_done", "logits_read", "gap_ready", "gap_exp", "chosen_ready",
            "pos_done", "rows_placed", "scattered", "count_done", "tables_ready",
            "xst_done", "xst_ready", "h_done", "act_done", "ht_done", "ht_ready", "y_done",
            "y_read", "y_ready", "ret_ready", "combined")) for k in range(2)]
        for k in range(2):
            r[k]["loaded"] = [sem(f"loaded{k}_{n}") for n in range(XBUF)]
            r[k]["returned"] = [sem(f"returned{k}_{n}") for n in range(XBUF)]
            r[k]["fetched"] = sem(f"fetched{k}")
        hstat_ready, hsd_ready, hn_ready, ystat_ready, ysd_ready = (sem(n) for n in ("hstat_ready", "hsd_ready", "hn_ready", "ystat_ready", "ysd_ready"))
        folded = sem("folded")
        y_scaled, y_shifted = sem("y_scaled"), sem("y_shifted")
        ln1_ready, x1t_done, x1t_ready, s1_done, s1_ready, e1_done, p1t_done, p1t_ready, pv1_done, added1 = (
            sem(n) for n in ("ln1_ready", "x1t_done", "x1t_ready", "s1_done", "s1_ready", "e1_done", "p1t_done", "p1t_ready", "pv1_done", "added1"))
        pe_setup1, act_setup1, dve_setup1 = sem("pe_setup1"), sem("act_setup1"), sem("dve_setup1")
        stored = sem("stored")

        block = ctx.enter_context(nc.Block())

        @block.sync
        def _(sp):
            for g in range(G):
                sp.dma_start(at(x, g * TG, D, TG).rearrange("p (t d) -> p t d", d=D),
                             d["x"][g].rearrange("(t p) d -> p t d", p=P)).then_inc(in_x, 16)
            sp.dma_start(ctx_n[0:KL, :].rearrange("k (b d) -> k b d", d=D),
                         d["ctx_1024"].rearrange("b k d -> k b d")).then_inc(in_attn0, 16)
            sp.dma_start(mask_u8[:], d["mask_BxS2_bk0"]).then_inc(in_attn0, 16)
            for t, n in ((wq, "W_Q"), (wk, "W_K"), (wv, "W_V"), (wo, "W_O")):
                sp.dma_start(t[:], d["L0_xattn_" + n]).then_inc(in_attn0, 16)
            for t, n in ((bq, "b_Q"), (bk, "b_K"), (bv, "b_V")):
                sp.dma_start(t[:], d["L0_xattn_" + n].rearrange("(p a) -> p a", a=1)).then_inc(in_attn0, 16)
            sp.dma_start(bo_all[:], d["L0_xattn_b_O"].partition_broadcast(P)).then_inc(in_attn0, 16)
            sp.dma_start(emb[:], d["L0_ffn_uzman_embeddings"]).then_inc(in_attn0, 16)
            sp.dma_start(cache_all[:], d["L0_ffn_onbellek_durumu"].partition_broadcast(P)).then_inc(in_attn0, 16)
            sp.wait_ge(zeros_ready, 1)
            span = REGION // P
            for e in range(E):
                sp.dma_start(xslots[e * REGION:(e + 1) * REGION, :].rearrange("(p a) w -> p (a w)", a=span),
                             zeros[:]).then_inc(table_zeroed, 16)
            sp.dma_start(xslots[E * REGION:XROWS, :].rearrange("(p a) w -> p (a w)", a=SPARE),
                         zeros[:, 0:SPARE * RW]).then_inc(table_zeroed, 16)
            sp.wait_ge(bias_zeroed, 2)
            for k in range(3):
                sp.dma_start(bias_f[0][32 * k:32 * k + E, 0:F], d["L0_ffn_b1"]).then_inc(in_bias, 16)
                sp.dma_start(bias_f[0][32 * k:32 * k + E, F:F + D], d["L0_ffn_b2"]).then_inc(in_bias, 16)
                sp.dma_start(bias_f[1][32 * k:32 * k + E, 0:F], d["L1_ffn_b1"]).then_inc(in_bias, 16)
            sp.dma_start(w1[0][:].rearrange("p (e f) -> p e f", e=E), d["L0_ffn_W1"].rearrange("e p f -> p e f")).then_inc(in_ffn0, 16)
            sp.dma_start(w2[0][:].rearrange("p (a n) -> p a n", n=D),
                         d["L0_ffn_W2"].rearrange("e (c p) n -> p (e c) n", p=P)).then_inc(in_ffn0, 16)
            sp.dma_start(fside[:].rearrange("p (t k) -> p t k", k=KL),
                         d["fside_1xSxS2_0"][0].rearrange("(t p) k -> p t k", p=P)).then_inc(in_small1, 16)
            sp.dma_start(u1[:], d["L1_xattn_W1"]).then_inc(in_small1, 16)
            sp.dma_start(u2[:], d["L1_xattn_W2"]).then_inc(in_small1, 16)
            sp.dma_start(ub1[:], d["L1_xattn_b1"].rearrange("(p a) -> p a", a=1)).then_inc(in_small1, 16)
            sp.dma_start(ub2[:], d["L1_xattn_b2"].rearrange("(p a) -> p a", a=1)).then_inc(in_small1, 16)
            sp.dma_start(router1[:], d["L1_ffn_Wr"]).then_inc(in_small1, 16)
            sp.dma_start(br_all[:], d["L1_ffn_br"].partition_broadcast(P)).then_inc(in_small1, 16)
            sp.dma_start(g1_n[:], d["L1_ffn_g1"].rearrange("e (c p) -> (e c) p", p=P)).then_inc(in_small1, 16)
            sp.dma_start(be1_n[:], d["L1_ffn_be1"].rearrange("e (c p) -> (e c) p", p=P)).then_inc(in_small1, 16)
            sp.dma_start(b2_n[:], d["L1_ffn_b2"]).then_inc(in_small1, 16)
            sp.wait_ge(table_zeroed, 16 * (E + 1))
            sp.dma_start(w1[1][:].rearrange("p (e f) -> p e f", e=E), d["L1_ffn_W1"].rearrange("e p f -> p e f")).then_inc(in_ffn1, 16)
            sp.dma_start(w2[1][:].rearrange("p (a n) -> p a n", n=D),
                         d["L1_ffn_W2"].rearrange("e (c p) n -> p (e c) n", p=P)).then_inc(in_ffn1, 16)
            sp.wait_ge(dve_setup, 4 + B)
            sp.dma_start(g2_all[:], d["L1_ffn_g2"].rearrange("e n -> (e n)").partition_broadcast(P)).then_inc(in_ffn1, 16)
            sp.dma_start(be2_all[:], d["L1_ffn_be2"].rearrange("e n -> (e n)").partition_broadcast(P)).then_inc(in_ffn1, 16)

            for k in range(2):
                m = r[k]

                def load(s, j):
                    W(sp, m["xst_done"], s - XBUF + 1)
                    W(sp, m["ret_ready"], s - XBUF + 1)
                    row = sp.value_load(slot_row_i[0:1, bass.ds(s, 1)], min_val=0, max_val=XROWS - P)
                    sp.dma_start(xs[:, j * RW:(j + 1) * RW], xslots[bass.ds(row, P), :]).then_inc(m["loaded"][j], 16)

                sp.wait_ge(m["tables_ready"], 1)
                sp.wait_ge(m["scattered"], 16 * 2 * NT)
                for s in range(XBUF):
                    load(s, s)
                with sp.Fori(1, NS // XBUF) as i:
                    for j in range(XBUF):
                        load(i * XBUF + j, j)
                for s in range(NS // XBUF * XBUF, NS):
                    load(s, s % XBUF)

                for n in range(XBUF):
                    sp.wait_ge(m["returned"][n], 16 * len(range(n, NS, XBUF)))
                for g in range(G):
                    W(sp, m["fetched"], 32 * g)
                    for c in range(2):
                        sp.dma_start(at(back, g * 2 + c, TG * D).rearrange("p (t d) -> p t d", d=D),
                                     yslots[c * TOK + g * S:c * TOK + (g + 1) * S, :].rearrange("(t p) d -> p t d", p=P)
                                     ).then_inc(m["fetched"], 16)
            for g in range(G):
                sp.wait_ge(r[1]["combined"], g + 1)
                sp.dma_start(out[g].rearrange("(t p) d -> p t d", p=P),
                             at(x, g * TG, D, TG).rearrange("p (t d) -> p t d", d=D)).then_inc(stored, 16)
            sp.wait_ge(stored, 16 * G)

        @block.gpsimd
        def _(pool):
            gp = nc.gpsimd
            chain = Steps(pool, pool_step)
            gp.memset(zeros[:], 0.0).then_inc(zeros_ready, 1)
            gp.memset(bias_f[0][:], 0.0).then_inc(bias_zeroed, 1)
            gp.memset(bias_f[1][:], 0.0).then_inc(bias_zeroed, 1)
            for t, v in ((ident, 0.0), (ones, 1.0), (ones_b, 1.0), (below, 1.0), (pick, 0.0), (head_of, 1.0),
                         (block_of, 1.0), (hide, 0.0), (running, 0.0), (rows1, 0.0), (rows2, 0.0), (eps, LN_EPS),
                         (ctx_z, 0.0), (shift_t, 0.0), (count, 0.0), (ctx_rep, 0.0)):
                gp.memset(t[:], v)
            chain(gp.memset(probs[:], 0.0))
            chain(gp.affine_select(out=ident[:], in_=ident[:], compare_op=ALU.not_equal, fill=1.0, base=0,
                                   pattern=[[-1, P]], channel_multiplier=1))
            chain(gp.affine_select(out=below[:], in_=below[:], compare_op=ALU.is_gt, fill=0.0, base=0,
                                   pattern=[[1, P]], channel_multiplier=-1))
            for k in range(3):
                chain(gp.affine_select(out=pick[:].rearrange("p (e m) -> p e m", e=E), in_=pick[:].rearrange("p (e m) -> p e m", e=E),
                                       compare_op=ALU.not_equal, fill=1.0, base=-32 * k,
                                       pattern=[[-1, E], [0, P]], channel_multiplier=1))
            chain(gp.affine_select(out=head_of[:], in_=head_of[:], compare_op=ALU.is_ge, fill=0.0, base=0,
                                   pattern=[[-DH, H]], channel_multiplier=1))
            chain(gp.affine_select(out=head_of[:], in_=head_of[:], compare_op=ALU.is_ge, fill=0.0, base=DH - 1,
                                   pattern=[[DH, H]], channel_multiplier=-1))
            bo = block_of[:].rearrange("p (c h) -> p c h", h=H)
            chain(gp.affine_select(out=bo, in_=bo, compare_op=ALU.is_ge, fill=0.0, base=0,
                                   pattern=[[P, NBLK], [-KL, H]], channel_multiplier=1))
            chain(gp.affine_select(out=bo, in_=bo, compare_op=ALU.is_ge, fill=0.0, base=KL - 1,
                                   pattern=[[-P, NBLK], [KL, H]], channel_multiplier=-1))
            for t, step, base, mult in ((up8, 1, 1, 0), (down8, -1, E, 0), (region0, REGION, 0, 0), (ramp16, P, 0, 0),
                                        (ramp_s, 1, 0, 0), (token_id, P, 0, 1), (dump_row, P, 2 * TOK, 1)):
                chain(gp.iota(t[:], [[step, t.shape[1]]], base=base, channel_multiplier=mult,
                              allow_small_or_imprecise_dtypes=True))
            gp.memset(neg_max[:], 0.0).then_inc(consts_ready, 1)

            pool.wait_ge(dve_setup, 3)
            pool.wait_ge(xn_ready, G)
            x3 = x[:].rearrange("p (t d) -> p t d", d=D)
            gp.tensor_tensor(x3, x3, spread(out_row[:], NT, 1), ALU.add).then_inc(x_biased, 1)

            def place_rows(k, g):
                m = r[k]
                wait_alone(pool, consts_ready, (m["rows_placed"], g + 1), (m["rows2_ready"], g + 1))
                for c, idx in enumerate((row1, row2)):
                    for j in range(TG):
                        row = (rows1, rows2)[c][:, j * RW:(j + 1) * RW] if k == 0 else at(rows_all, (g * 2 + c) * TG + j, RW)
                        gp.indirect_dma_start(out=xslots[:, :], out_offset=bass.IndirectOffsetOnAxis(ap=idx[:, j:j + 1], axis=0),
                                              in_=row, in_offset=None).then_inc(m["scattered"], 16)

            def return_rows(k, s, j):
                m = r[k]
                n = j % XBUF
                o = ys[:, n * D:(n + 1) * D]
                if k == 1:
                    e = pool.value_load(slot_e_i[0:1, bass.ds(s, 1)], min_val=0, max_val=E - 1)
                    pool.wait_ge(m["y_ready"], s + 1)
                    W(pool, m["returned"][n], uses(s, j))
                    gp.tensor_tensor(o, two(ya, j), at(g2_all, e, D), ALU.mult).then_inc(y_scaled, 1)
                    pool.wait_ge(y_scaled, s + 1)
                    gp.tensor_tensor(o, o, at(be2_all, e, D), ALU.add).then_inc(y_shifted, 1)
                wait_alone(pool, consts_ready, (m["y_ready"] if k == 0 else y_shifted, s + 1), (m["ret_ready"], s + 1))
                gp.indirect_dma_start(out=yslots[:, :], out_offset=bass.IndirectOffsetOnAxis(ap=ret[:, n:n + 1], axis=0),
                                      in_=o, in_offset=None).then_inc(m["returned"][n], 16)

            pool.wait_ge(table_zeroed, 16 * (E + 1))
            for k in range(2):
                if k == 0:
                    with pool.Fori(0, G) as g:
                        place_rows(k, g)
                    pool.wait_ge(act_setup1, 1)
                    pool.wait_ge(pe_setup1, 2)
                    w3 = w2[1][:].rearrange("p (a n) -> p a n", n=D)
                    gp.tensor_tensor(w3, w3, spread(g1_t[:], D), ALU.mult).then_inc(folded, 1)
                else:
                    for g in range(G):
                        place_rows(k, g)
                pool.wait_ge(r[k]["tables_ready"], 1)
                for s in range(XBUF):
                    return_rows(k, s, s)
                with pool.Fori(1, NS // XBUF) as i:
                    for j in range(XBUF):
                        return_rows(k, i * XBUF + j, j)
                for s in range(NS // XBUF * XBUF, NS):
                    return_rows(k, s, s)

        @block.tensor
        def _(pe):
            te = nc.tensor

            def mm(o, a, b, start=True, stop=True, **kw):
                return te.matmul(o, a, b, start=start, stop=stop, **kw)

            def tr(o, a, rows=P):
                return te.transpose(o, a, ident[0:rows, 0:rows])

            pe.wait_ge(consts_ready, 1)
            pe.wait_ge(in_attn0, 16 * 12)
            for b in range(B):
                last = tr(bank(0, b * KL, (b + 1) * KL), ctx_n[0:KL, b * D:(b + 1) * D], KL)
            last.then_inc(pe_setup, 1)
            pe.wait_ge(act_setup, 1)
            mm(bank(1, 0, B * KL), wk[:], ctx_t[:]).then_inc(pe_setup, 1)
            pe.wait_ge(dve_setup, 1)
            mm(bank(2, 0, D), bv_rep[:], wo[:]).then_inc(pe_setup, 1)
            pe.wait_ge(dve_setup, 2)
            tr(bank(3, 0, E), emb[:], E)
            tr(bank(3, E, 2 * E), rows1[0:E, 0:D], E).then_inc(pe_setup, 1)
            for g in range(G):
                pe.wait_ge(xn_ready, g + 1)
                for j in range(TG):
                    last = tr(bank(4 + g, j * P, (j + 1) * P), xn[:, (g * TG + j) * D:(g * TG + j + 1) * D])
                last.then_inc(xt_done, 1)
            pe.wait_ge(xnt_ready, G)
            for b in range(B):
                pe.wait_ge(act_setup, 2 + b)
                pe.wait_ge(dve_setup, 4 + max(b - 1, 0))
                for c in range(NBLK):
                    last = mm(bank(4 - b % 2 * 4, c * D, (c + 1) * D), two(ctx_rep, b, NBLK * P)[:, c * P:(c + 1) * P], wv[:])
                last.then_inc(pe_setup, 1)

            def queries(t, j):
                W(pe, qt_ready, t)
                mm(bank(6, 0, P), wq[:], at(xn_t, t, P)).then_inc(q_done, 1)

            def scores(t, j, g):
                pe.wait_ge(qt_ready, t + 1)
                W(pe, sub_done, t)
                for a in range(0, HK, 512):
                    n = min(512, HK - a)
                    mm(bank(a // 512, 0, n), two(q_t, j), k_heads[:, bass.ds(g * HK + a, n)], stop=False)
                    last = mm(bank(a // 512, 0, n), at(pick, g, P), hide[:, a:a + n], start=False)
                last.then_inc(s_done, 1)

            def turn_probs(t, j):
                pe.wait_ge(exp_done, t + 1)
                W(pe, ptr_ready, t)
                for c in range(NBLK):
                    last = tr(bank(3, c * P, (c + 1) * P), two(probs, j, NBLK * P)[:, c * P:(c + 1) * P])
                last.then_inc(pt_done, 1)

            def values(t, g):
                pe.wait_ge(ptr_ready, t + 1)
                W(pe, added, t)
                nothing = shift_t[:].bitcast(BF16)
                mm(bank(7, 0, H * VC), nothing[:, 0:P], nothing[:, 0:H * VC], stop=False, skip_group_check=True)
                for c in range(NBLK):
                    h0, h1 = c * P // KL, min(H, -(-(c + 1) * P // KL))
                    last = mm(bank(7, h0 * VC, h1 * VC), probs_t[:, c * P:(c + 1) * P],
                              v_heads[:, bass.ds(g * (NBLK * H * VC) + (c * H + h0) * VC, (h1 - h0) * VC)],
                              start=False, stop=(c == NBLK - 1), skip_group_check=True)
                last.then_inc(pv_done, 1)

            def turn_heads(t):
                pe.wait_ge(o_ready, t + 1)
                tr(bank(7, 256, 384), heads_out[:]).then_inc(ot_done, 1)

            def project(t):
                pe.wait_ge(ott_ready, t + 1)
                mm(bank(7, 384, 512), heads_t[:], wo[:]).then_inc(proj_done, 1)

            def route_turn(k, g, b):
                m = r[k]
                pe.wait_ge(m["rows_ready"], g + 1)
                for j in range(TG):
                    last = tr(bank(b, j * P, (j + 1) * P), rows1[:, j * RW:j * RW + D])
                last.then_inc(m["xgt_done"], 1)

            def route_logits(k, g, b):
                m = r[k]
                pe.wait_ge(m["xgt_ready"], g + 1)
                w, n = (rt, 2 * E) if k == 0 else (router1, E)
                for j in range(TG):
                    last = mm(bank(b, j * n, (j + 1) * n), xg_t[:, j * P:(j + 1) * P], w[:])
                last.then_inc(m["logits_done"], 1)

            def route_rank(k, g, b):
                m = r[k]
                pe.wait_ge(m["chosen_ready"], g + 1)
                mm(bank(b, 0, TG * E), below[:], chosen[:], stop=False)
                mm(bank(b, 0, TG * E), ones_b[:], before[:], start=False).then_inc(m["pos_done"], 1)

            def attend(g, first, final):
                for j in range(TG):
                    t = g * TG + j
                    if not (final and j == TG - 1):
                        scores(t + 1, j + 1, g + (j + 1) // TG)
                    if not (final and j >= TG - 2):
                        if not first and j in (2, 3):
                            pe.wait_ge(r[0]["xgt_ready" if j == 2 else "logits_read"], g)
                        queries(t + 2, j)
                    if not (first and j == 0):
                        turn_heads(t - 1)
                    turn_probs(t, j)
                    if not (first and j == 0):
                        project(t - 1)
                    if not first and j:
                        if not (final and j >= TG - 2):
                            pe.wait_ge(qt_ready, t + 3)
                        (None, route_turn, route_logits, route_rank)[j](0, g - 1, 6)
                    values(t, g)
                if not first:
                    pe.wait_ge(r[0]["rows_placed"], g)

            pe.wait_ge(dve_setup, 4 + B)
            queries(0, 0)
            scores(0, 0, 0)
            queries(1, 1)
            attend(0, True, False)
            with pe.Fori(1, G - 1) as g:
                attend(g, False, False)
            attend(G - 1, False, True)
            turn_heads(NT - 1)
            project(NT - 1)

            def route_all(k, g, banks):
                route_turn(k, g, banks[0])
                route_logits(k, g, banks[1])
                route_rank(k, g, banks[2])

            def route_count(k, b):
                mm(bank(b, 0, E), ones_b[:], running[:]).then_inc(r[k]["count_done"], 1)

            pe.wait_ge(added, NT)
            pe.wait_ge(in_ffn1, 64)
            tr(bank(7, 0, E * FC), g1_n[:], E * FC)
            tr(bank(7, E * FC, 2 * E * FC), be1_n[:], E * FC)
            tr(bank(7, 2 * E * FC, 2 * E * FC + E), b2_n[:], E).then_inc(pe_setup1, 1)
            pe.wait_ge(act_setup1, 1)
            for e in range(E):
                for c in range(FC):
                    a = e * FC + c
                    last = mm(bank(7, 128 + e, 129 + e), w2[1][:, a * D:(a + 1) * D], be1_t[:, a:a + 1],
                              start=(c == 0), stop=(c == FC - 1))
            last.then_inc(pe_setup1, 1)
            route_all(0, G - 1, (0, 1, 2))
            route_count(0, 3)

            pe.wait_ge(in_small1, 16 * 10)
            tr(bank(4, 0, P), u1[:])
            tr(bank(4, P, 2 * P), u2[:]).then_inc(pe_setup1, 1)
            pe.wait_ge(act_setup1, 2)
            mm(bank(5, 0, B * KL), u1_t[:], ctx_t[:]).then_inc(pe_setup1, 1)
            pe.wait_ge(act_setup1, 3)
            mm(bank(5, 0, B * KL), u2_t[:], kp_a[:]).then_inc(pe_setup1, 1)
            mm(bank(6, 0, 1), u2_t[:], ub1[:]).then_inc(pe_setup1, 1)
            pe.wait_ge(act_setup1, 4)
            mm(bank(5, 0, B * KL), u2[:], kp_t[:]).then_inc(pe_setup1, 1)
            pe.wait_ge(act_setup1, 5)
            mm(bank(5, 0, B * KL), u1[:], fold_u[:]).then_inc(pe_setup1, 1)
            pe.wait_ge(act_setup1, 8)
            mm(bank(5, 0, B * KL), bq1_rep[:], kp_t[:]).then_inc(pe_setup1, 1)

            pe.wait_ge(dve_setup1, 1)
            tr(bank(7, 256, 384), shift_t[:]).then_inc(pe_setup1, 1)

            def experts(k):
                m = r[k]

                def turn_x(s, j):
                    pe.wait_ge(m["loaded"][j % XBUF], uses(s, j) + 16)
                    W(pe, m["xst_ready"], s - 1)
                    tr(bank(6 + j % 2, 0, P), xs[:, (j % XBUF) * RW:(j % XBUF) * RW + D]).then_inc(m["xst_done"], 1)

                def experts_of(s, n):
                    return nc.values_load_multi_w_load_instructions(slot_e_i[0:1, bass.ds(s, n)], [mybir.EngineType.PE],
                                                                    min_val=0, max_val=E - 1)[1]

                def hidden(s, j, e):
                    pe.wait_ge(m["xst_ready"], s + 1)
                    W(pe, m["act_done"], s - 1)
                    mm(bank(j % 2), xs_t[:, (j % 2) * D:(j % 2 + 1) * D], w1[k][:, bass.ds(e * F, F)], stop=False)
                    mm(bank(j % 2), at(pick, e, P), bias_p[k][:, 0:F], start=False).then_inc(m["h_done"], 1)

                def turn_h(s, j):
                    pe.wait_ge(m["act_done"] if k == 0 else hn_ready, s + 1)
                    W(pe, m["ht_ready"], s - 1)
                    src = hid if k == 0 else hidn
                    for c in range(FC):
                        last = tr(bank(2 + j % 2, c * P, (c + 1) * P), src[:, (j % 2) * F + c * P:][:, 0:P])
                    last.then_inc(m["ht_done"], 1)

                def output(s, j, e):
                    pe.wait_ge(m["ht_ready"], s + 1)
                    W(pe, m["y_ready" if k == 0 else "y_read"], s - 1)
                    for c in range(FC):
                        mm(bank(4 + j % 2, 0, D), hid_t[:, (j % 2) * F + c * P:][:, 0:P],
                           w2[k][:, bass.ds(e * F + c * D, D)], start=(c == 0), stop=False)
                    mm(bank(4 + j % 2, 0, D), at(pick, e, P), bias_p[k][:, F:F + D], start=False).then_inc(m["y_done"], 1)

                def tile(s, j, left, e):
                    turn_h(s, j)
                    if left > 2:
                        hidden(s + 2, j + 2, e[j + 2])
                    output(s, j, e[j])
                    if left > 3:
                        turn_x(s + 3, j + 3)

                for s in range(3):
                    turn_x(s, s)
                U = XBUF
                e = experts_of(0, U + 2)
                for s in range(2):
                    hidden(s, s, e[s])
                for s in range(U):
                    tile(s, s, U, e)
                with pe.Fori(1, NS // U) as i:
                    e = experts_of(i * U, U + 2)
                    for j in range(U):
                        tile(i * U + j, j, U, e)
                done = NS // U * U
                e = experts_of(done, NS - done)
                for s in range(done, NS):
                    tile(s, s - done, NS - s, e)

            pe.wait_ge(dve_setup1, 2)
            pe.wait_ge(in_ffn0, 32)
            pe.wait_ge(r[0]["tables_ready"], 1)
            experts(0)

            def attend1(g, attends=True, routes=True):
                if attends:
                    pe.wait_ge(ln1_ready, g + 1)
                    for j in range(TG):
                        last = tr(bank(0, j * P, (j + 1) * P), xn1[:, j * D:(j + 1) * D])
                    last.then_inc(x1t_done, 1)
                if routes:
                    route_turn(1, g - 1, 4)
                if attends:
                    pe.wait_ge(x1t_ready, g + 1)
                    for j in range(TG):
                        last = mm(bank(1, j * KL, (j + 1) * KL), xn1_t[:, j * P:(j + 1) * P], fold[:, bass.ds(g * KL, KL)])
                    last.then_inc(s1_done, 1)
                if routes:
                    route_logits(1, g - 1, 5)
                if attends:
                    pe.wait_ge(e1_done, g + 1)
                    for j in range(TG):
                        last = tr(bank(2, j * P, (j + 1) * P)[0:KL, :], pr1[:, j * KL:(j + 1) * KL])
                    last.then_inc(p1t_done, 1)
                    pe.wait_ge(p1t_ready, g + 1)
                    for j in range(TG):
                        last = mm(bank(3, j * D, (j + 1) * D), pr1_t[:, j * P:(j + 1) * P], ctx_z[:, bass.ds(g * D, D)])
                    last.then_inc(pv1_done, 1)
                if routes:
                    route_rank(1, g - 1, 6)

            attend1(0, routes=False)
            with pe.Fori(1, G) as g:
                attend1(g)
            attend1(G, attends=False)
            route_count(1, 0)
            pe.wait_ge(r[1]["tables_ready"], 1)
            pe.wait_ge(folded, 1)
            experts(1)

        @block.scalar
        def _(act):
            sc_ = nc.scalar

            def copy(o, i, s=None):
                ins = sc_.activation(o, i, ACT.Copy)
                return ins.then_inc(s, 1) if s is not None else ins

            act.wait_ge(consts_ready, 1)
            act.wait_ge(pe_setup, 1)
            copy(ctx_t[:], bank(0, 0, B * KL), act_setup)
            act.wait_ge(act_setup, 1)
            def rep_ctx(b):
                if b >= 2:
                    act.wait_ge(pe_setup, 3 + b)
                copy(two(ctx_rep, b, NBLK * P)[:, 0:HK].rearrange("p (h k) -> p h k", k=KL),
                     spread(ctx_t[:, b * KL:(b + 1) * KL], H, 1), act_setup)

            rep_ctx(0)
            rep_ctx(1)
            for g in range(G):
                act.wait_ge(xt_done, g + 1)
                copy(at(xn_t, g, TG * P), bank(4 + g), xnt_ready)
            rep_ctx(2)
            rep_ctx(3)

            def queried(t, j):
                act.wait_ge(q_done, t + 1)
                W(act, s_done, t - 1)
                sc_.activation(two(q_t, j), bank(6, 0, P), ACT.Identity, bias=bq[:]).then_inc(qt_ready, 1)

            def exps(t, j):
                act.wait_ge(sub_done, t + 1)
                p = two(probs, j, NBLK * P)[:, 0:HK]
                sc_.activation(p, p, ACT.Exp, scale=DH ** -0.5).then_inc(exp_done, 1)

            def turned_probs(t):
                act.wait_ge(pt_done, t + 1)
                W(act, pv_done, t)
                copy(probs_t[:], bank(3, 0, NBLK * P), ptr_ready)

            def turned_heads(t):
                act.wait_ge(ot_done, t + 1)
                copy(heads_t[:], bank(7, 256, 384), ott_ready)

            def route_turned(k, g, b):
                m = r[k]
                act.wait_ge(m["xgt_done"], g + 1)
                copy(xg_t[:], bank(b), m["xgt_ready"])

            def route_rows2(k, g):
                m = r[k]
                act.wait_ge(m["rows_ready"], g + 1)
                for rows in (rows2[:],) if k == 0 else (at(rows_all, g * 2 + c, TG * RW) for c in range(2)):
                    last = copy(rows.rearrange("p (t w) -> p t w", w=RW)[:, :, 0:D],
                                rows1[:].rearrange("p (t w) -> p t w", w=RW)[:, :, 0:D])
                last.then_inc(m["rows2_ready"], 1)

            def route_exp(k, g):
                m = r[k]
                act.wait_ge(m["gap_ready"], g + 1)
                sc_.activation(gap[:], gap[:], ACT.Exp).then_inc(m["gap_exp"], 1)

            def attend(g, first, final):
                for j in range(TG):
                    t = g * TG + j
                    exps(t, j)
                    if not (final and j >= TG - 2):
                        queried(t + 2, j)
                    if not (first and j == 0):
                        turned_heads(t - 1)
                    turned_probs(t)
                    if not first and j == 1:
                        route_rows2(0, g - 1)
                        route_turned(0, g - 1, 6)
                    if not first and j == 2:
                        route_exp(0, g - 1)

            queried(0, 0)
            queried(1, 1)
            attend(0, True, False)
            with act.Fori(1, G - 1) as g:
                attend(g, False, False)
            attend(G - 1, False, True)
            turned_heads(NT - 1)
            act.wait_ge(pe_setup1, 1)
            copy(g1_t[:], bank(7, 0, E * FC))
            copy(be1_t[:], bank(7, E * FC, 2 * E * FC), act_setup1)
            route_rows2(0, G - 1)
            route_turned(0, G - 1, 0)
            route_exp(0, G - 1)

            act.wait_ge(pe_setup1, 3)
            copy(u1_t[:], bank(4, 0, P))
            copy(u2_t[:], bank(4, P, 2 * P), act_setup1)
            act.wait_ge(pe_setup1, 4)
            sc_.activation(kp_a[:], bank(5, 0, B * KL), ACT.Identity, bias=ub1[:]).then_inc(act_setup1, 1)
            act.wait_ge(pe_setup1, 5)
            sc_.activation(kp_t[:], bank(5, 0, B * KL), ACT.Identity, bias=ub2[:]).then_inc(act_setup1, 1)
            act.wait_ge(pe_setup1, 7)
            copy(fold_u[:], bank(5, 0, B * KL), act_setup1)
            act.wait_ge(pe_setup1, 8)
            copy(fold[:], bank(5, 0, B * KL), act_setup1)
            sc_.activation(bq1[:], bank(6, 0, 1), ACT.Identity, bias=ub2[:]).then_inc(act_setup1, 1)
            act.wait_ge(act_setup1, 7)
            sc_.activation(bq1_rep[:], ones[:], ACT.Copy, scale=bq1[:]).then_inc(act_setup1, 1)
            act.wait_ge(pe_setup1, 9)
            copy(q_row[:], bank(5, 0, B * KL), act_setup1)

            def experts(k):
                m = r[k]

                def turned_x(s, j):
                    act.wait_ge(m["xst_done"], s + 1)
                    W(act, m["h_done"], s - 1)
                    copy(xs_t[:, (j % 2) * D:(j % 2 + 1) * D], bank(6 + j % 2, 0, P), m["xst_ready"])

                def turned_h(s, j):
                    act.wait_ge(m["ht_done"], s + 1)
                    W(act, m["y_done"], s - 1)
                    copy(two(hid_t, j, F), bank(2 + j % 2), m["ht_ready"])

                def activate(s, j):
                    act.wait_ge(m["h_done"], s + 1)
                    if k == 0:
                        W(act, m["ht_done"], s - 1)
                        sc_.activation(hid[:, (j % 2) * F:(j % 2 + 1) * F], bank(j % 2), ACT.Gelu).then_inc(m["act_done"], 1)
                    else:
                        W(act, hn_ready, s - 1)
                        sc_.activation(hid[:, (j % 2) * F:(j % 2 + 1) * F], bank(j % 2), ACT.Relu).then_inc(m["act_done"], 1)

                def deviation_h(s):
                    act.wait_ge(hstat_ready, s + 1)
                    sc_.activation(hrs[:, 0:1], hmv[:, 1:2], ACT.Sqrt, bias=eps[:]).then_inc(hsd_ready, 1)

                def activate_y(s, j):
                    act.wait_ge(m["y_done"], s + 1)
                    W(act, y_scaled, s - 1)
                    sc_.activation(ya[:, (j % 2) * D:(j % 2 + 1) * D], bank(4 + j % 2, 0, D), ACT.Relu).then_inc(m["y_read"], 1)

                def deviation_y(s):
                    act.wait_ge(ystat_ready, s + 1)
                    sc_.activation(yrs[:, 0:1], ymv[:, 1:2], ACT.Sqrt, bias=eps[:]).then_inc(ysd_ready, 1)

                def tile(s, j, left, first=False):
                    if k == 1:
                        turned_h(s, j)
                        if left > 1:
                            deviation_h(s + 1)
                        if not first:
                            deviation_y(s - 1)
                    if left > 2:
                        activate(s + 2, j + 2)
                    if k == 1:
                        activate_y(s, j)
                    if left > 3:
                        turned_x(s + 3, j + 3)

                turned_x(0, 0)
                turned_x(1, 1)
                activate(0, 0)
                turned_x(2, 2)
                activate(1, 1)
                if k == 1:
                    deviation_h(0)
                U = XBUF
                for s in range(U):
                    tile(s, s, U, s == 0)
                with act.Fori(1, NS // U) as i:
                    for j in range(U):
                        tile(i * U + j, j, U)
                for s in range(NS // U * U, NS):
                    tile(s, s, NS - s)
                if k == 1:
                    deviation_y(NS - 1)

            experts(0)

            def attend1(g, attends=True, routes=True):
                if attends:
                    act.wait_ge(x1t_done, g + 1)
                    copy(xn1_t[:], bank(0), x1t_ready)
                if routes:
                    route_turned(1, g - 1, 4)
                if attends:
                    act.wait_ge(s1_ready, g + 1)
                    for j in range(TG):
                        last = sc_.activation(pr1[:, j * KL:(j + 1) * KL], sc1[:, j * KL:(j + 1) * KL], ACT.Exp,
                                              bias=nmax1[:, j:j + 1], accum_out=sum1[:, j:j + 1])
                    last.then_inc(e1_done, 1)
                    act.wait_ge(p1t_done, g + 1)
                    copy(pr1_t[0:KL, :], bank(2)[0:KL, :], p1t_ready)
                if routes:
                    route_rows2(1, g - 1)
                    route_exp(1, g - 1)

            attend1(0, routes=False)
            with act.Fori(1, G) as g:
                attend1(g)
            attend1(G, attends=False)
            experts(1)

        @block.vector
        def _(dve):
            v = nc.vector
            chain = Steps(dve, dve_step)
            var_g = mvg[:].rearrange("p (t s) -> p t s", s=2)[:, :, 1]

            def rsqrt(y, a, t):
                chain(v.tensor_scalar(y.bitcast(I32), a.bitcast(I32), -0.5, RSQRT_SEED, ALU.mult, ALU.add))
                for _ in range(3):
                    chain(v.scalar_tensor_tensor(t, y, -0.5, y, ALU.mult, ALU.mult))
                    chain(v.tensor_tensor(t, t, a, ALU.mult))
                    chain(v.scalar_tensor_tensor(y, t, 1.5, y, ALU.add, ALU.mult))

            dve.wait_ge(in_x, 16 * G)
            for t in range(NT):
                last = v.bn_stats(stats[:, t * 6:(t + 1) * 6], x[:, t * D:(t + 1) * D])
            chain(last)
            for t in range(NT):
                last = v.bn_aggr(mv[:, t * 2:(t + 1) * 2], stats[:, t * 6:(t + 1) * 6])
            chain(last)
            chain(v.tensor_scalar(nw_v[:], mv[:].rearrange("p (t s) -> p t s", s=2)[:, :, 1], LN_EPS, None, ALU.add))
            rsqrt(rstd[:], nw_v[:], nw_t[:])
            for g in range(G):
                for t in range(g * TG, (g + 1) * TG):
                    last = v.tensor_scalar(xn[:, t * D:(t + 1) * D], x[:, t * D:(t + 1) * D], mv[:, 2 * t:2 * t + 1],
                                           rstd[:, t:t + 1], ALU.subtract, ALU.mult)
                last.then_inc(xn_ready, 1)

            dve.wait_ge(consts_ready, 1)
            dve.wait_ge(in_attn0, 16 * 12)
            v.tensor_scalar(bv_rep[:], ones[:], bv[:], None, ALU.mult).then_inc(dve_setup, 1)
            chain(v.tensor_tensor(rows2[0:E, 0:D], emb[:], emb[:], ALU.mult))
            chain(v.reduce_sum(nw_v[0:E, 0:1], rows2[0:E, 0:D], AX.X))
            rsqrt(norm2[0:E, 0:1], nw_v[0:E, 0:1], nw_t[0:E, 0:1])
            chain(v.tensor_tensor(nw_v[0:E, 0:1], nw_v[0:E, 0:1], norm2[0:E, 0:1], ALU.mult))
            chain(v.tensor_scalar(nw_v[0:E, 0:1], nw_v[0:E, 0:1], NORM_EPS, None, ALU.add))
            chain(v.reciprocal(nw_t[0:E, 0:1], nw_v[0:E, 0:1]))
            v.tensor_scalar(rows1[0:E, 0:D], emb[:], nw_t[0:E, 0:1], None, ALU.mult).then_inc(dve_setup, 1)
            dve.wait_ge(pe_setup, 3)
            v.tensor_tensor(out_row[:], bank(2, 0, D), bo_all[:], ALU.add).then_inc(dve_setup, 1)
            chain(v.tensor_scalar(k_t[:], bank(1, 0, B * KL), bk[:], None, ALU.add))
            dve.wait_ge(pe_setup, 4)
            v.tensor_copy(rt[:], bank(3, 0, 2 * E))
            v.tensor_scalar(cache_all[:], cache_all[:], 0.1, None, ALU.mult)
            v.tensor_scalar(hide[0:B, :].rearrange("b (h k) -> b h k", k=KL), spread(mask_u8[:], H, 1), HIDE, None, ALU.mult)
            for b in range(B):
                last = v.tensor_tensor(k_heads[:, b * HK:(b + 1) * HK].rearrange("p (h k) -> p h k", k=KL),
                                       spread(k_t[:, b * KL:(b + 1) * KL], H, 1), spread(head_of[:], KL), ALU.mult)
            last.then_inc(dve_setup, 1)
            for b in range(B):
                vh = v_heads[:, b * NBLK * H * VC:(b + 1) * NBLK * H * VC].rearrange("p (c v) -> p c v", v=VC)
                v.tensor_copy(vh[:, :, DH], block_of[:])
                dve.wait_ge(pe_setup, 5 + b)
                v.tensor_tensor(vh[:, :, 0:DH], bank(4 - b % 2 * 4, 0, NBLK * D).rearrange("p (c v) -> p c v", v=DH),
                                spread(block_of[:], DH), ALU.mult).then_inc(dve_setup, 1)

            def maxima(t, j):
                dve.wait_ge(s_done, t + 1)
                nm = two(neg_max, j, H)
                chain(v.tensor_reduce(nm, bank(0, 0, HK).rearrange("p (h k) -> p h k", k=KL), AX.X, ALU.max, negate=True))

            def subtract(t, j):
                W(dve, pt_done, t - 1)
                nm = two(neg_max, j, H)
                v.tensor_tensor(two(probs, j, NBLK * P)[:, 0:HK].rearrange("p (h k) -> p h k", k=KL),
                                bank(0, 0, HK).rearrange("p (h k) -> p h k", k=KL), spread(nm, KL), ALU.add).then_inc(sub_done, 1)

            def divide(t):
                dve.wait_ge(pv_done, t + 1)
                o = bank(7, 0, H * VC).rearrange("p (h v) -> p h v", v=VC)
                chain(v.reciprocal(inv[:], o[:, :, DH]))
                W(dve, ot_done, t)
                v.tensor_tensor(heads_out[:].rearrange("p (h v) -> p h v", v=DH), o[:, :, 0:DH], spread(inv[:], DH),
                                ALU.mult).then_inc(o_ready, 1)

            def add(t):
                dve.wait_ge(proj_done, t + 1)
                dve.wait_ge(x_biased, 1)
                v.tensor_tensor(at(x, t, D), bank(7, 384, 512), at(x, t, D), ALU.add).then_inc(added, 1)

            def group_stats(groups):
                for g, n in groups:
                    for i in range(TG):
                        j = n * TG + i
                        last = v.bn_stats(statg[:, j * 6:(j + 1) * 6], at(x, g * TG + i, D))
                chain(last, consts_ready)
                for g, n in groups:
                    for j in range(n * TG, (n + 1) * TG):
                        last = v.bn_aggr(mvg[:, j * 2:(j + 1) * 2], statg[:, j * 6:(j + 1) * 6])
                chain(last)
                lo, hi = min(n for g, n in groups) * TG, max(n + 1 for g, n in groups) * TG
                chain(v.tensor_scalar(nw_v[:, lo:hi], var_g[:, lo:hi], LN_EPS, None, ALU.add))
                rsqrt(rstdg[:, lo:hi], nw_v[:, lo:hi], nw_t[:, lo:hi])

            def normalise(o, w, g, n):
                for i in range(TG):
                    j = n * TG + i
                    last = v.tensor_scalar(o[:, i * w:i * w + D], at(x, g * TG + i, D), mvg[:, 2 * j:2 * j + 1],
                                           rstdg[:, j:j + 1], ALU.subtract, ALU.mult)
                return last

            def route_norm(k, g):
                m = r[k]
                if k == 0:
                    wait_alone(dve, consts_ready, (m["scattered"], g * (16 * 2 * TG)), (added, (g + 1) * TG))
                    group_stats([(g, 0)])
                else:
                    W(dve, m["rows2_ready"], g)
                normalise(rows1, RW, g, k)
                for c, base in enumerate((0.0, float(TOK))):
                    rows = (rows1, rows2)[c][:] if k == 0 else at(rows_all, g * 2 + c, TG * RW)
                    last = v.tensor_scalar(rows.rearrange("p (t w) -> p t w", w=RW)[:, :, D], at(token_id, g, TG),
                                           base, None, ALU.add)
                last.then_inc(m["rows_ready"], 1)
                if k == 0:
                    chain(v.tensor_tensor(norm2[:], var_g[:, 0:TG], rstdg[:, 0:TG], ALU.mult))
                    chain(v.tensor_tensor(norm2[:], norm2[:], rstdg[:, 0:TG], ALU.mult))
                    chain(v.tensor_scalar(norm2[:], norm2[:], float(D), None, ALU.mult))
                    rsqrt(inv_norm[:], norm2[:], nw_t[:, 0:TG])
                    chain(v.tensor_tensor(norm2[:], norm2[:], inv_norm[:], ALU.mult))
                    chain(v.tensor_scalar(norm2[:], norm2[:], NORM_EPS, None, ALU.add))
                    chain(v.reciprocal(inv_norm[:], norm2[:]))

            def by_e(t):
                return t[:].rearrange("p (t e) -> p t e", e=E)

            def route_read(k, g, b):
                m = r[k]
                n = (2 if k == 0 else 1) * TG * E
                dve.wait_ge(m["logits_done"], g + 1)
                v.tensor_copy(logits[:, 0:n], bank(b, 0, n)).then_inc(m["logits_read"], 1)

            def pick_one(values, value, ramp, onehot, op):
                chain(v.tensor_reduce(value, values, AX.X, op))
                chain(v.tensor_tensor(by_e(hit), values, spread(value, E), ALU.is_equal))
                chain(v.tensor_tensor(by_e(key), by_e(hit), spread(ramp[:], TG, 1), ALU.mult))
                chain(v.tensor_reduce(best[:], by_e(key), AX.X, ALU.max))
                chain(v.tensor_tensor(by_e(onehot), by_e(key), spread(best[:], E), ALU.is_equal))

            def route_choose(k, g):
                m = r[k]
                dve.wait_ge(m["logits_read"], g + 1)
                if k == 0:
                    pair = logits[:].rearrange("p (t e) -> p t e", e=2 * E)
                    pick_one(pair[:, :, 0:E], top1[:], up8, oh1, ALU.min)
                    chain(v.tensor_tensor(by_e(sc), pair[:, :, E:2 * E], spread(inv_norm[:], E), ALU.mult))
                    chain(v.tensor_tensor(by_e(sc), by_e(sc), spread(cache_all[:], TG, 1), ALU.add))
                    chain(v.scalar_tensor_tensor(sc[:], oh1[:], DROP, sc[:], ALU.mult, ALU.add))
                else:
                    chain(v.tensor_tensor(by_e(sc), logits[:, 0:TG * E].rearrange("p (t e) -> p t e", e=E),
                                          spread(br_all[:], TG, 1), ALU.add))
                pick_one(by_e(sc), top1[:], down8, oh1, ALU.max)
                chain(v.scalar_tensor_tensor(sc[:], oh1[:], 2 * DROP, sc[:], ALU.mult, ALU.add))
                pick_one(by_e(sc), top2[:], down8, oh2, ALU.max)
                v.tensor_tensor(gap[:], top2[:], top1[:], ALU.subtract).then_inc(m["gap_ready"], 1)
                chain(v.tensor_tensor(chosen[:], oh1[:], oh2[:], ALU.add))
                chain(v.tensor_copy(before[:, 0:E], running[:]))
                for j in range(1, TG):
                    chain(v.tensor_tensor(before[:, j * E:(j + 1) * E], before[:, (j - 1) * E:j * E],
                                          chosen[:, (j - 1) * E:j * E], ALU.add))
                v.tensor_tensor(running[:], before[:, (TG - 1) * E:], chosen[:, (TG - 1) * E:], ALU.add).then_inc(m["chosen_ready"], 1)

            def route_gates(k, g):
                m = r[k]
                dve.wait_ge(m["gap_exp"], g + 1)
                chain(v.tensor_scalar(top1[:], gap[:], 1.0, None, ALU.add))
                gg = at(gate, g, 2 * TG).rearrange("p (t c) -> p t c", c=2)
                chain(v.reciprocal(best[:], top1[:]))
                v.tensor_copy(gg[:, :, 0], best[:])
                chain(v.tensor_tensor(gg[:, :, 1], best[:], gap[:], ALU.mult))

            def route_place(k, g, b):
                m = r[k]
                dve.wait_ge(m["pos_done"], g + 1)
                chain(v.tensor_tensor(by_e(posn), bank(b, 0, TG * E).rearrange("p (t e) -> p t e", e=E), spread(region0[:], TG, 1), ALU.add))
                if k == 1:
                    W(dve, m["scattered"], g * (16 * 2 * TG))
                for oh, row, part in ((oh1, row1, top1), (oh2, row2, top2)):
                    chain(v.tensor_tensor(key[:], oh[:], posn[:], ALU.mult))
                    chain(v.tensor_reduce(part[:], by_e(key), AX.X, ALU.add))
                    last = v.tensor_copy(row[:], part[:])
                last.then_inc(m["rows_placed"], 1)

            def tables(k, b):
                m = r[k]
                dve.wait_ge(m["count_done"], 1)
                chain(v.tensor_copy(count[:, 0:E], bank(b, 0, E)))
                n16 = TOK // P
                g16 = gt[:, 0:E * n16].rearrange("p (e n) -> p e n", n=n16)
                chain(v.tensor_tensor(g16, spread(count[:, 0:E], n16), spread(ramp16[:], E, 1), ALU.is_gt))
                chain(v.tensor_reduce(tiles_e[:], g16, AX.X, ALU.add))
                chain(v.tensor_copy(ends[:, 0:1], tiles_e[:, 0:1]))
                for e in range(1, E):
                    chain(v.tensor_tensor(ends[:, e:e + 1], ends[:, e - 1:e], tiles_e[:, e:e + 1], ALU.add))
                g3, w3 = (t[:].rearrange("p (s e) -> p s e", e=E) for t in (gt, gtw))
                chain(v.tensor_tensor(g3, spread(ramp_s[:], E), spread(ends[:], NS, 1), ALU.is_ge))
                chain(v.tensor_reduce(slot_e[:], g3[:, :, 0:E - 1], AX.X, ALU.add))
                v.tensor_copy(slot_e_i[:], slot_e[:])
                chain(v.tensor_scalar(coef[:], tiles_e[:], -float(P), float(REGION), ALU.mult, ALU.add))
                chain(v.tensor_tensor(w3, g3, spread(coef[:], NS, 1), ALU.mult))
                chain(v.tensor_reduce(slot_row[:], w3, AX.X, ALU.add))
                chain(v.scalar_tensor_tensor(slot_row[:], ramp_s[:], float(P), slot_row[:], ALU.mult, ALU.add))
                v.tensor_copy(slot_row_i[:], slot_row[:])
                chain(v.tensor_reduce(e_all[:], g3, AX.X, ALU.add))
                chain(v.scalar_tensor_tensor(local[:], e_all[:], -float(REGION), slot_row[:], ALU.mult, ALU.add))
                chain(v.tensor_tensor(coef[:], count[:, 1:E + 1], count[:, 0:E], ALU.subtract))
                chain(v.tensor_tensor(w3, g3, spread(coef[:], NS, 1), ALU.mult))
                chain(v.tensor_reduce(cnt_s[:], w3, AX.X, ALU.add))
                chain(v.tensor_scalar(cnt_s[:], cnt_s[:], count[:, 0:1], token_id[:, 0:1], ALU.add, ALU.subtract))
                chain(v.tensor_tensor(valid[:], local[:], cnt_s[:], ALU.is_lt))
                chain(v.tensor_scalar(pad_row[:], valid[:], -1.0, 1.0, ALU.mult, ALU.add))
                v.tensor_tensor(pad_row[:], pad_row[:], dump_row[:], ALU.mult).then_inc(m["tables_ready"], 1)
                dve.wait_ge(m["tables_ready"], 1)

            def bias_parts(k):
                chain(v.tensor_copy(bias_p[k][:], bias_f[k][:]))
                chain(v.tensor_tensor(bias_r[:], bias_f[k][:], bias_p[k][:], ALU.subtract))
                chain(v.tensor_copy(bias_q[:], bias_r[:]))
                chain(v.tensor_tensor(bias_r[:], bias_r[:], bias_q[:], ALU.subtract))
                chain(v.tensor_copy(bias_p[k][32:64, :], bias_q[32:64, :]))
                chain(v.tensor_copy(bias_p[k][64:96, :], bias_r[64:96, :]))

            def attend(g, first, final):
                for j in range(TG):
                    t = g * TG + j
                    if not (first and j == 0):
                        divide(t - 1)
                    if not (final and j == TG - 1):
                        maxima(t + 1, j + 1)
                    if not (first and j == 0):
                        add(t - 1)
                    if not first and j == 2:
                        route_read(0, g - 1, 6)
                    if not first and j == 3:
                        route_gates(0, g - 1)
                        route_place(0, g - 1, 6)
                    if not (final and j == TG - 1):
                        subtract(t + 1, j + 1)
                    if not first and j == 0:
                        route_norm(0, g - 1)
                    if not first and j == 2:
                        route_choose(0, g - 1)

            maxima(0, 0)
            subtract(0, 0)
            attend(0, True, False)
            with dve.Fori(1, G - 1) as g:
                chain.enter(g - 1, DVE_GROUP)
                attend(g, False, False)
                chain.leave(G - 2)
            attend(G - 1, False, True)
            divide(NT - 1)
            add(NT - 1)
            route_norm(0, G - 1)
            route_read(0, G - 1, 1)
            route_choose(0, G - 1)
            route_gates(0, G - 1)
            route_place(0, G - 1, 2)
            dve.wait_ge(in_bias, 16 * 9)
            bias_parts(0)
            tables(0, 3)

            dve.wait_ge(pe_setup1, 2)
            chain(v.tensor_copy(coef[:], bank(7, 2 * E * FC, 2 * E * FC + E)))
            for n in range(3):
                ins = v.tensor_tensor(shift_t[:, 32 * n:32 * n + E], bank(7, 128, 128 + E), coef[:], ALU.add)
            ins.then_inc(dve_setup1, 1)
            v.memset(running[:], 0.0)
            v.memset(pr1_t[:], 0.0)
            chain(v.tensor_copy(ctx_z[0:KL, :], ctx_n[0:KL, :]))
            dve.wait_ge(pe_setup1, 10)
            v.tensor_copy(bias_f[1][:, F:F + D], bank(7, 256, 384)).then_inc(dve_setup1, 1)
            dve.wait_ge(dve_setup1, 2)
            bias_parts(1)

            def experts(k):
                m = r[k]

                def return_row(s, j):
                    n = j % XBUF
                    dve.wait_ge(m["loaded"][n], uses(s, j) + 16)
                    W(dve, m["returned"][n], uses(s, j))
                    v.tensor_scalar(ret[:, n:n + 1], xs[:, n * RW + D:][:, 0:1], at(valid, s, 1), at(pad_row, s, 1),
                                    ALU.mult, ALU.add).then_inc(m["ret_ready"], 1)

                def turned_h(s, j):
                    dve.wait_ge(m["ht_done"], s + 1)
                    W(dve, m["y_done"], s - 1)
                    v.tensor_copy(hid_t[:, (j % 2) * F:(j % 2 + 1) * F], bank(2 + j % 2)).then_inc(m["ht_ready"], 1)

                def stats_h(s, j):
                    dve.wait_ge(m["act_done"], s + 1)
                    chain(v.bn_stats(hst[:], two(hid, j, F)), consts_ready)
                    v.bn_aggr(hmv[:], hst[:]).then_inc(hstat_ready, 1)

                def normalise_h(s, j):
                    dve.wait_ge(hsd_ready, s + 1)
                    chain(v.reciprocal(hrs[:, 1:2], hrs[:, 0:1]))
                    W(dve, m["ht_done"], s - 1)
                    v.tensor_scalar(two(hidn, j, F), two(hid, j, F), hmv[:, 0:1], hrs[:, 1:2],
                                    ALU.subtract, ALU.mult).then_inc(hn_ready, 1)

                def stats_y(s, j):
                    dve.wait_ge(m["y_read"], s + 1)
                    chain(v.bn_stats(yst[:], two(ya, j)), consts_ready)
                    v.bn_aggr(ymv[:], yst[:]).then_inc(ystat_ready, 1)

                def finish(s, j):
                    n = j % XBUF
                    if k == 0:
                        dve.wait_ge(m["y_done"], s + 1)
                        W(dve, m["returned"][n], uses(s, j))
                        v.tensor_copy(ys[:, n * D:(n + 1) * D], bank(4 + j % 2, 0, D)).then_inc(m["y_ready"], 1)
                        return
                    dve.wait_ge(ysd_ready, s + 1)
                    chain(v.reciprocal(yrs[:, 1:2], yrs[:, 0:1]))
                    v.tensor_scalar(two(ya, j), two(ya, j), ymv[:, 0:1], yrs[:, 1:2], ALU.subtract, ALU.mult).then_inc(m["y_ready"], 1)

                def tile(s, j, left, first=False):
                    if k == 0:
                        turned_h(s, j)
                        if left > 1:
                            return_row(s + 1, j + 1)
                        finish(s, j)
                        return
                    if left > 1:
                        stats_h(s + 1, j + 1)
                    if not first:
                        stats_y(s - 1, j - 1)
                    if left > 1:
                        return_row(s + 1, j + 1)
                        normalise_h(s + 1, j + 1)
                    if not first:
                        finish(s - 1, j - 1)

                return_row(0, 0)
                if k == 1:
                    stats_h(0, 0)
                    normalise_h(0, 0)
                U = XBUF
                for s in range(U):
                    tile(s, s, U, s == 0)
                with dve.Fori(1, NS // U) as i:
                    chain.enter(i - 1, U * DVE_TILE[k])
                    for j in range(U):
                        tile(i * U + j, j, U)
                    chain.leave(NS // U - 1)
                for s in range(NS // U * U, NS):
                    tile(s, s, NS - s)
                if k == 1:
                    stats_y(NS - 1, NS - 1)
                    finish(NS - 1, NS - 1)

            experts(0)

            def combine(k, g):
                m = r[k]
                dve.wait_ge(m["fetched"], g * 32 + 32)
                for c in range(2):
                    for i in range(TG):
                        last = v.scalar_tensor_tensor(at(x, g * TG + i, D), at(back, (g * 2 + c) * TG + i, D),
                                                      gate[:, bass.ds((g * TG + i) * 2 + c, 1)], at(x, g * TG + i, D), ALU.mult, ALU.add)
                    if c == 0:
                        chain(last)
                last.then_inc(m["combined"], 1)

            def attend1(g, attends=True, routes=True, final=False):
                if attends:
                    wait_alone(dve, consts_ready, (r[0]["combined"], g + 1))
                group_stats([(g, 0)] * attends + [(g - 1, 1)] * routes)
                if attends:
                    normalise(xn1, D, g, 0).then_inc(ln1_ready, 1)
                if routes:
                    route_norm(1, g - 1)
                if attends:
                    chain(v.scalar_tensor_tensor(fside_q[:].rearrange("p (t k) -> p t k", k=KL), spread(at(q_row, g, KL), TG, 1), D ** -0.5,
                                                 fside[:].rearrange("p (t k) -> p t k", k=KL), ALU.mult, ALU.add))
                    if not final:
                        combine(0, g + 1)
                    dve.wait_ge(s1_done, g + 1)
                    chain(v.scalar_tensor_tensor(sc1[:], bank(1, 0, TG * KL), D ** -0.5, fside_q[:], ALU.mult, ALU.add))
                    v.tensor_reduce(nmax1[:], sc1[:].rearrange("p (t k) -> p t k", k=KL), AX.X, ALU.max, negate=True).then_inc(s1_ready, 1)
                if routes:
                    route_read(1, g - 1, 5)
                    route_choose(1, g - 1)
                    route_gates(1, g - 1)
                    route_place(1, g - 1, 6)
                if attends:
                    dve.wait_ge(e1_done, g + 1)
                    chain(v.reciprocal(inv1[:], sum1[:]))
                    dve.wait_ge(pv1_done, g + 1)
                    for i in range(TG):
                        last = v.scalar_tensor_tensor(at(x, g * TG + i, D), bank(3, i * D, (i + 1) * D), inv1[:, i:i + 1],
                                                      at(x, g * TG + i, D), ALU.mult, ALU.add)
                    chain(last)

            combine(0, 0)
            attend1(0, routes=False)
            with dve.Fori(1, G - 1) as g:
                chain.enter(g - 1, DVE_GROUP1)
                attend1(g)
                chain.leave(G - 2)
            attend1(G - 1, final=True)
            attend1(G, attends=False)
            tables(1, 0)
            experts(1)
            with dve.Fori(0, G) as g:
                chain.enter(g, DVE_LAST)
                combine(1, g)
                chain.leave(G)


INPUTS = ["x", "ctx_1024", "fside_1xSxS2_0", "mask_BxS2_bk0", "L0_xattn_W_Q", "L0_xattn_b_Q", "L0_xattn_W_K", "L0_xattn_b_K",
          "L0_xattn_W_V", "L0_xattn_b_V", "L0_xattn_W_O", "L0_xattn_b_O", "L0_ffn_uzman_embeddings", "L0_ffn_W1", "L0_ffn_b1",
          "L0_ffn_W2", "L0_ffn_b2", "L0_ffn_onbellek_durumu", "L1_xattn_W1", "L1_xattn_b1", "L1_xattn_W2", "L1_xattn_b2",
          "L1_ffn_Wr", "L1_ffn_br", "L1_ffn_W1", "L1_ffn_b1", "L1_ffn_g1", "L1_ffn_be1", "L1_ffn_W2", "L1_ffn_b2",
          "L1_ffn_g2", "L1_ffn_be2"]


def kernel(**inputs):
    import numpy as np
    import concourse.bacc as bacc
    from concourse.bass_utils import run_bass_kernel_spmd

    nc = bacc.Bacc("TRN2", target_bir_lowering=False, num_devices=1)
    arrays, d = {}, {}
    for name in INPUTS:
        a = np.ascontiguousarray(inputs[name])
        arrays["in_" + name] = a
        d[name] = nc.dram_tensor("in_" + name, a.shape, mybir.dt.from_np(a.dtype), kind="ExternalInput").ap()
    out = nc.dram_tensor("out", (B, S, D), F32, kind="ExternalOutput").ap()
    xslots = nc.dram_tensor("xslots", (XROWS, RW), F32, kind="Internal").ap()
    yslots = nc.dram_tensor("yslots", (YROWS, D), F32, kind="Internal").ap()
    build(nc, d, out, xslots, yslots)
    return run_bass_kernel_spmd(nc, [arrays], core_ids=[0]).results[0]["out"]
```

```python
from contextlib import ExitStack

import concourse.bass as bass
from concourse import mybir

F32, BF16, I32, U8 = mybir.dt.float32, mybir.dt.bfloat16, mybir.dt.int32, mybir.dt.uint8
ALU = mybir.AluOpType
ACT = mybir.ActivationFunctionType
AX = mybir.AxisListType

P = 128
B, S, D = 4, 512, 128
TOK = B * S
NT = TOK // P
G = B
TG = NT // G
KL = 77
H, DH = 16, 8
HK = H * KL
NBLK = -(-HK // P)
PARTS = ((0, 6), (6, 11), (11, 16))
VC = DH + 1
E, F = 8, 512
FC = F // P
NS = (2 * TOK + E * (P - 1)) // P
EBITS = 3
SPARE = NS - 2 * TOK // P
REGION = TOK + P
RW = D + 4
XROWS = E * REGION + SPARE * P
YROWS = 2 * TOK + NS * P
LN_EPS = 1e-5
NORM_EPS = 1e-8
HIDE = -float(2 ** 100)
DROP = -1e30
RSQRT_SEED = 1597463007.0
XBUF = 4
NPASS = -(-NS // XBUF)
DVE_GROUP, DVE_GROUP1 = 51, 32
DVE_TILE = (0, 4)


class Steps:

    def __init__(self, eng, sem):
        self.eng, self.sem, self.base, self.n = eng, sem, 0, 0

    def __call__(self, ins, consts_ready=None):
        ins.then_inc(self.sem, 1)
        self.n += 1
        if consts_ready is not None:
            return wait_alone(self.eng, consts_ready, (self.sem, self.base + self.n))
        self.eng.wait_ge(self.sem, self.base + self.n)

    def start(self, ins):
        ins.then_inc(self.sem, 1)
        self.n += 1
        return self.base + self.n

    def until(self, count):
        self.eng.wait_ge(self.sem, count)

    def enter(self, i, per):
        self.outer = self.base + self.n
        self.base, self.n, self.per = self.outer + i * per, 0, per

    def leave(self, passes):
        assert self.n == self.per, (self.n, self.per)
        self.base, self.n = self.outer + passes * self.per, 0


def W(eng, sem, n):
    if not isinstance(n, int) or n > 0:
        eng.wait_ge(sem, n)


def wait_alone(eng, consts_ready, *waits):
    waits = [(sem, n if isinstance(n, int) else eng.to_reg(n)) for sem, n in waits]
    eng.wait_ge(consts_ready, 1)
    for sem, n in waits:
        W(eng, sem, n)


def two(tensor, j, w=D):
    return tensor[:, (j % 2) * w:(j % 2 + 1) * w]


def uses(s, j, n=XBUF):
    return (s - j % n) * (16 // n)


def at(tensor, i, w, n=1):
    return tensor[:, bass.ds(i * w, n * w)]


def spread(ap, n, axis=2):
    ap = ap.unsqueeze(axis)
    shape = list(ap.shape)
    shape[axis] = n
    return ap.broadcast_to(shape)


def build(nc, d, out, xslots, yslots):
    ctx = ExitStack()

    def sb(name, width, dt=F32, rows=P):
        return ctx.enter_context(nc.sbuf_tensor(name, [rows, width], dt))

    def sem(name):
        return ctx.enter_context(nc.semaphore(name))

    with ctx:
        ident = sb("ident", P)
        ones = sb("ones", P)
        ones_b = sb("ones_b", P, BF16)
        below = sb("below", P, BF16)
        pick = sb("pick", E * P, BF16)
        pick_row = sb("pick_row", E)
        head_of = sb("head_of", H)
        block_of = sb("block_of", NBLK * H)
        up8, down8 = sb("up8", E), sb("down8", E)
        region0 = sb("region0", E)
        ramp16 = sb("ramp16", TOK // P)
        ramp_s = sb("ramp_s", NS)
        token_id = sb("token_id", NT)
        dump_row = sb("dump_row", NS)
        eps = sb("eps", 1)
        unused = sb("unused", 1)
        x = sb("x", NT * D)
        ctx_n = sb("ctx_n", B * D)
        mask_u8 = sb("mask_u8", KL, U8, B)
        wq, wk, wv, wo = sb("wq", D), sb("wk", D), sb("wv", D), sb("wo", D)
        bq, bk, bv = sb("bq", 1), sb("bk", 1), sb("bv", 1)
        bq_scaled = sb("bq_scaled", 1)
        bo_all = sb("bo_all", D)
        emb = sb("emb", D, F32, E)
        cache_all = sb("cache_all", E)
        fside = sb("fside", TG * KL)
        u1, u2 = sb("u1", D), sb("u2", D)
        ub1, ub2 = sb("ub1", 1), sb("ub2", 1)
        router1 = sb("router1", E)
        br_all = sb("br_all", E)
        w1 = [sb(f"w1_{n}", E * F) for n in range(2)]
        zeros = w1[1][:, 0:REGION // P * RW]
        w2 = [sb(f"w2_{n}", E * FC * D) for n in range(2)]
        bias_f = [sb(f"bias_f{n}", F + D) for n in range(2)]
        bias_p = [sb(f"bias_p{n}", F + D, BF16) for n in range(2)]
        g1_n, be1_n = sb("g1_n", P, F32, E * FC), sb("be1_n", P, F32, E * FC)
        b2_n = sb("b2_n", D, F32, E)
        g1_t, be1_t = sb("g1_t", E * FC), sb("be1_t", E * FC)
        shift_t = sb("shift_t", P)
        ctx_t = sb("ctx_t", B * KL)
        k_t = sb("k_t", B * KL)
        setup_buf = sb("setup_buf", 2 * E * D)
        place = setup_buf[:, 0:NBLK * P // 2].bitcast(BF16)
        v_rest = setup_buf[:, NBLK * P // 2:NBLK * P // 2 + B * D]
        v_parts = setup_buf[:, NBLK * P // 2 + B * D:][:, 0:3 * B * D // 2].bitcast(BF16)
        g2_all, be2_all = setup_buf[:, 0:E * D], setup_buf[:, E * D:2 * E * D]
        k_heads = sb("k_heads", B * HK)
        v_heads = sb("v_heads", B * NBLK * H * VC)
        hide = sb("hide", HK, BF16)
        out_row = sb("out_row", D)
        bv_rep = sb("bv_rep", D)
        stats = sb("stats", NT * 6)
        mv = sb("mv", NT * 2)
        rstd = sb("rstd", NT)
        nw_v, nw_t, nw_y = sb("nw_v", NT), sb("nw_t", NT), sb("nw_y", NT)
        xn_both = sb("xn_both", 2 * NT * D)
        xn, xn_t = xn_both[:, 0:NT * D], xn_both[:, NT * D:]
        q_t = sb("q_t", 2 * D)
        neg_max = sb("neg_max", 2 * H)
        probs = sb("probs", 2 * NBLK * P)
        probs_t = sb("probs_t", NBLK * P)
        inv = sb("inv", H)
        heads_out = sb("heads_out", D)
        heads_t = sb("heads_t", D)
        mvg = sb("mvg", 2 * TG * 2)
        statg = sb("statg", 2 * TG * 6)
        rstdg = sb("rstdg", 2 * TG)
        norm2, inv_norm = sb("norm2", TG), sb("inv_norm", TG)
        rows1, rows2 = sb("rows1", TG * RW), sb("rows2", TG * RW)
        rt = sb("rt", 2 * E)
        xg_t = sb("xg_t", TG * D)
        logits = sb("logits", TG * 2 * E)
        sc = sb("sc", TG * E)
        hit, key = sb("hit", TG * E), sb("key", TG * E)
        oh_both = sb("oh_both", 2 * TG * E)
        oh1, oh2 = oh_both[:, 0:TG * E], oh_both[:, TG * E:]
        key_both = sb("key_both", 2 * TG * E)
        row_f, row_both = sb("row_f", 2 * TG), sb("row_both", 2 * TG, I32)
        row1, row2 = row_both[:, 0:TG], row_both[:, TG:]
        top1, top2, best = sb("top1", TG), sb("top2", TG), sb("best", TG)
        gap = sb("gap", TG)
        gate = sb("gate", NT * 2)
        chosen = sb("chosen", TG * E, BF16)
        running = sb("running", TG * E, BF16)
        added_up = sb("added_up", E)
        posn = sb("posn", TG * E)
        count = sb("count", E + 1)
        ends = [sb(f"ends{n}", 2 * E) for n in range(4)]
        gt = sb("gt", NS * E)
        gtw = sb("gtw", NS * E)
        coef = sb("coef", E)
        slot_e, slot_row = sb("slot_e", NPASS * XBUF + 8), sb("slot_row", NS)
        packed, packed_i = sb("packed", NPASS), sb("packed_i", NPASS, I32)
        local, cnt_s, e_all = sb("local", NS), sb("cnt_s", NS), sb("e_all", NS)
        valid, pad_row = sb("valid", NS), sb("pad_row", NS)
        slot_e_i, slot_row_i = sb("slot_e_i", NS, I32), sb("slot_row_i", NS, I32)
        xs = sb("xs", XBUF * RW)
        xs_t = sb("xs_t", 2 * D)
        hid, hidn, hid_t = (v_heads[:, n * 2 * F:(n + 1) * 2 * F] for n in range(3))
        ys = v_heads[:, 6 * F:6 * F + XBUF * D]
        ya = v_heads[:, 7 * F:7 * F + 2 * D]
        ret = sb("ret", XBUF, I32)
        hst, hmv, hrs = sb("hst", 6), sb("hmv", 2), sb("hrs", 2)
        yst, ymv, yrs = sb("yst", 6), sb("ymv", 2), sb("yrs", 2)
        back = xn_both[:]
        rows_all = v_heads[:, 0:G * 2 * TG * RW]
        ctx_z = sb("ctx_z", B * D)
        bq1 = sb("bq1", 1)
        places = [0]

        def old_keys(width):
            a = places[0]
            places[0] += width
            return k_heads[:, a:a + width]

        xn1, xn1_t, sc1, pr1, pr1_t = (old_keys(n) for n in (TG * D, TG * D, TG * KL, TG * KL, TG * P))
        kp_a, kp_t, fold_u, fold, u1_t, u2_t, bq1_rep = (old_keys(n) for n in (*[B * KL] * 4, D, D, P))
        bias_r, bias_q = old_keys(F + D), old_keys((F + D) // 2).bitcast(BF16)
        q_row, fside_q = kp_a, fold_u
        nmax1, sum1, inv1 = sb("nmax1", TG), sb("sum1", TG), sb("inv1", TG)

        ps = ctx.enter_context(nc.psum_tensor("ps", [P, 8 * 512], F32))

        def bank(i, a=0, b=512):
            return ps[:, 512 * i + a:512 * i + b]

        zeros_ready, consts_ready = sem("zeros_ready"), sem("consts_ready")
        pool_step, dve_step, act_step = sem("pool_step"), sem("dve_step"), sem("act_step")
        in_x, in_attn0, in_ffn0, in_small1, in_ffn1 = (sem(n) for n in ("in_x", "in_attn0", "in_ffn0", "in_small1", "in_ffn1"))
        in_bias = sem("in_bias")
        bias_zeroed = sem("bias_zeroed")
        table_zeroed = sem("table_zeroed")
        ident_ready, keys_ready = sem("ident_ready"), sem("keys_ready")
        blanks_ready = sem("blanks_ready")
        pool_combined = sem("pool_combined")
        pe_setup, dve_setup, act_setup = sem("pe_setup"), sem("dve_setup"), sem("act_setup")
        xn_ready, xt_done, xnt_ready, q_done, qt_ready = (sem(n) for n in ("xn_ready", "xt_done", "xnt_ready", "q_done", "qt_ready"))
        max_done = sem("max_done")
        s_done, sub_done, exp_done, pt_done, ptr_ready, pv_done = (sem(n) for n in ("s_done", "sub_done", "exp_done", "pt_done", "ptr_ready", "pv_done"))
        o_ready, ot_done, ott_ready, proj_done, x_biased, added = (sem(n) for n in ("o_ready", "ot_done", "ott_ready", "proj_done", "x_biased", "added"))
        r = [dict((n, sem(f"{n}{k}")) for n in (
            "rows_ready", "rows2_ready", "xgt_done", "xgt_ready", "logits_done", "logits_read", "gap_ready", "gap_exp", "chosen_ready",
            "pos_done", "pos_read", "rows_placed", "scattered", "slots_ready", "tables_ready",
            "xst_done", "xst_ready", "h_done", "act_done", "ht_done", "ht_ready", "y_done",
            "y_read", "y_ready", "ret_ready", "combined")) for k in range(2)]
        for k in range(2):
            r[k]["loaded"] = [sem(f"loaded{k}_{n}") for n in range(XBUF)]
            r[k]["returned"] = [sem(f"returned{k}_{n}") for n in range(XBUF)]
            r[k]["fetched"] = [sem(f"fetched{k}_{g}") for g in range(G)]
        hstat_ready, hsd_ready, hn_ready, ystat_ready, ysd_ready = (sem(n) for n in ("hstat_ready", "hsd_ready", "hn_ready", "ystat_ready", "ysd_ready"))
        folded = sem("folded")
        y_scaled, y_shifted = sem("y_scaled"), sem("y_shifted")
        ln1_ready, x1t_done, x1t_ready, s1_done, s1_ready, e1_done, p1t_done, p1t_ready, pv1_done, added1 = (
            sem(n) for n in ("ln1_ready", "x1t_done", "x1t_ready", "s1_done", "s1_ready", "e1_done", "p1t_done", "p1t_ready", "pv1_done", "added1"))
        pe_setup1, act_setup1, dve_setup1 = sem("pe_setup1"), sem("act_setup1"), sem("dve_setup1")
        stored = sem("stored")

        block = ctx.enter_context(nc.Block())

        @block.sync
        def _(sp):
            for g in range(G):
                sp.dma_start(at(x, g * TG, D, TG).rearrange("p (t d) -> p t d", d=D),
                             d["x"][g].rearrange("(t p) d -> p t d", p=P)).then_inc(in_x, 16)
            sp.dma_start(ctx_n[0:KL, :].rearrange("k (b d) -> k b d", d=D),
                         d["ctx_1024"].rearrange("b k d -> k b d")).then_inc(in_attn0, 16)
            sp.dma_start(mask_u8[:], d["mask_BxS2_bk0"]).then_inc(in_attn0, 16)
            for t, n in ((wq, "W_Q"), (wk, "W_K"), (wv, "W_V"), (wo, "W_O")):
                sp.dma_start(t[:], d["L0_xattn_" + n]).then_inc(in_attn0, 16)
            for t, n in ((bq, "b_Q"), (bk, "b_K"), (bv, "b_V")):
                sp.dma_start(t[:], d["L0_xattn_" + n].rearrange("(p a) -> p a", a=1)).then_inc(in_attn0, 16)
            sp.dma_start(bo_all[:], d["L0_xattn_b_O"].partition_broadcast(P)).then_inc(in_attn0, 16)
            sp.dma_start(emb[:], d["L0_ffn_uzman_embeddings"]).then_inc(in_attn0, 16)
            sp.dma_start(cache_all[:], d["L0_ffn_onbellek_durumu"].partition_broadcast(P)).then_inc(in_attn0, 16)
            sp.wait_ge(zeros_ready, 1)
            span = REGION // P
            for e in range(E):
                sp.dma_start(xslots[e * REGION:(e + 1) * REGION, :].rearrange("(p a) w -> p (a w)", a=span),
                             zeros[:]).then_inc(table_zeroed, 16)
            sp.dma_start(xslots[E * REGION:XROWS, :].rearrange("(p a) w -> p (a w)", a=SPARE),
                         zeros[:, 0:SPARE * RW]).then_inc(table_zeroed, 16)
            sp.wait_ge(bias_zeroed, 2)
            for k in range(3):
                sp.dma_start(bias_f[0][32 * k:32 * k + E, 0:F], d["L0_ffn_b1"]).then_inc(in_bias, 16)
                sp.dma_start(bias_f[0][32 * k:32 * k + E, F:F + D], d["L0_ffn_b2"]).then_inc(in_bias, 16)
                sp.dma_start(bias_f[1][32 * k:32 * k + E, 0:F], d["L1_ffn_b1"]).then_inc(in_bias, 16)
            sp.dma_start(w1[0][:].rearrange("p (e f) -> p e f", e=E), d["L0_ffn_W1"].rearrange("e p f -> p e f")).then_inc(in_ffn0, 16)
            sp.dma_start(w2[0][:].rearrange("p (a n) -> p a n", n=D),
                         d["L0_ffn_W2"].rearrange("e (c p) n -> p (e c) n", p=P)).then_inc(in_ffn0, 16)
            sp.dma_start(fside[:].rearrange("p (t k) -> p t k", k=KL),
                         d["fside_1xSxS2_0"][0].rearrange("(t p) k -> p t k", p=P)).then_inc(in_small1, 16)
            sp.dma_start(u1[:], d["L1_xattn_W1"]).then_inc(in_small1, 16)
            sp.dma_start(u2[:], d["L1_xattn_W2"]).then_inc(in_small1, 16)
            sp.dma_start(ub1[:], d["L1_xattn_b1"].rearrange("(p a) -> p a", a=1)).then_inc(in_small1, 16)
            sp.dma_start(ub2[:], d["L1_xattn_b2"].rearrange("(p a) -> p a", a=1)).then_inc(in_small1, 16)
            sp.dma_start(router1[:], d["L1_ffn_Wr"]).then_inc(in_small1, 16)
            sp.dma_start(br_all[:], d["L1_ffn_br"].partition_broadcast(P)).then_inc(in_small1, 16)
            sp.dma_start(g1_n[:], d["L1_ffn_g1"].rearrange("e (c p) -> (e c) p", p=P)).then_inc(in_small1, 16)
            sp.dma_start(be1_n[:], d["L1_ffn_be1"].rearrange("e (c p) -> (e c) p", p=P)).then_inc(in_small1, 16)
            sp.dma_start(b2_n[:], d["L1_ffn_b2"]).then_inc(in_small1, 16)
            sp.wait_ge(table_zeroed, 16 * (E + 1))
            sp.dma_start(w1[1][:].rearrange("p (e f) -> p e f", e=E), d["L1_ffn_W1"].rearrange("e p f -> p e f")).then_inc(in_ffn1, 16)
            sp.dma_start(w2[1][:].rearrange("p (a n) -> p a n", n=D),
                         d["L1_ffn_W2"].rearrange("e (c p) n -> p (e c) n", p=P)).then_inc(in_ffn1, 16)
            sp.wait_ge(dve_setup, 4 + NBLK)
            sp.dma_start(g2_all[:], d["L1_ffn_g2"].rearrange("e n -> (e n)").partition_broadcast(P)).then_inc(in_ffn1, 16)
            sp.dma_start(be2_all[:], d["L1_ffn_be2"].rearrange("e n -> (e n)").partition_broadcast(P)).then_inc(in_ffn1, 16)

            for k in range(2):
                m = r[k]

                def load(s, j):
                    W(sp, m["xst_done"], s - XBUF + 1)
                    W(sp, m["ret_ready"], s - XBUF + 1)
                    row = sp.value_load(slot_row_i[0:1, bass.ds(s, 1)], min_val=0, max_val=XROWS - P)
                    sp.dma_start(xs[:, j * RW:(j + 1) * RW], xslots[bass.ds(row, P), :]).then_inc(m["loaded"][j], 16)

                sp.wait_ge(m["slots_ready"], 1)
                sp.wait_ge(m["scattered"], 16 * 2 * NT)
                for s in range(XBUF):
                    load(s, s)
                with sp.Fori(1, NS // XBUF) as i:
                    for j in range(XBUF):
                        load(i * XBUF + j, j)
                for s in range(NS // XBUF * XBUF, NS):
                    load(s, s % XBUF)

                for n in range(XBUF):
                    sp.wait_ge(m["returned"][n], 16 * len(range(n, NS, XBUF)))
                for g in range(G):
                    for c in range(2):
                        sp.dma_start(at(back, g * 2 + c, TG * D).rearrange("p (t d) -> p t d", d=D),
                                     yslots[c * TOK + g * S:c * TOK + (g + 1) * S, :].rearrange("(t p) d -> p t d", p=P)
                                     ).then_inc(m["fetched"][g], 16)
            vector_sums = 0
            for g in (0, 2, 1, 3):
                if g == 1:
                    sp.wait_ge(pool_combined, G - G // 2 + 1)
                else:
                    vector_sums += 1
                    sp.wait_ge(r[1]["combined"], vector_sums)
                sp.dma_start(out[g].rearrange("(t p) d -> p t d", p=P),
                             at(x, g * TG, D, TG).rearrange("p (t d) -> p t d", d=D)).then_inc(stored, 16)
            sp.wait_ge(stored, 16 * G)

        @block.gpsimd
        def _(pool):
            gp = nc.gpsimd
            chain = Steps(pool, pool_step)
            gp.memset(zeros[:], 0.0).then_inc(zeros_ready, 1)
            gp.memset(bias_f[0][:], 0.0).then_inc(bias_zeroed, 1)
            gp.memset(bias_f[1][:], 0.0).then_inc(bias_zeroed, 1)
            gp.memset(ones[:], 1.0)
            chain(gp.memset(ident[:], 0.0))
            gp.affine_select(out=ident[:], in_=ident[:], compare_op=ALU.not_equal, fill=1.0, base=0,
                             pattern=[[-1, P]], channel_multiplier=1).then_inc(ident_ready, 1)
            for t in (place, hide, rows1, rows2, probs, ctx_z, slot_e, *ends):
                gp.memset(t[:] if t is not place else t, 0.0)
            gp.memset(v_parts, 0.0).then_inc(blanks_ready, 1)
            for t, v in ((ones_b, 1.0), (below, 1.0), (pick_row, 0.0), (head_of, 1.0), (block_of, 1.0), (running, 0.0),
                         (eps, LN_EPS), (shift_t, 0.0)):
                gp.memset(t[:], v)
            chain(gp.memset(count[:], 0.0))
            chain(gp.affine_select(out=below[:], in_=below[:], compare_op=ALU.is_gt, fill=0.0, base=0,
                                   pattern=[[1, P]], channel_multiplier=-1))
            for k in range(3):
                chain(gp.affine_select(out=pick_row[:], in_=pick_row[:], compare_op=ALU.not_equal, fill=1.0, base=-32 * k,
                                       pattern=[[-1, E]], channel_multiplier=1))
            chain(gp.affine_select(out=head_of[:], in_=head_of[:], compare_op=ALU.is_ge, fill=0.0, base=0,
                                   pattern=[[-DH, H]], channel_multiplier=1))
            chain(gp.affine_select(out=head_of[:], in_=head_of[:], compare_op=ALU.is_ge, fill=0.0, base=DH - 1,
                                   pattern=[[DH, H]], channel_multiplier=-1))
            bo = block_of[:].rearrange("p (c h) -> p c h", h=H)
            chain(gp.affine_select(out=bo, in_=bo, compare_op=ALU.is_ge, fill=0.0, base=0,
                                   pattern=[[P, NBLK], [-KL, H]], channel_multiplier=1))
            chain(gp.affine_select(out=bo, in_=bo, compare_op=ALU.is_ge, fill=0.0, base=KL - 1,
                                   pattern=[[-P, NBLK], [KL, H]], channel_multiplier=-1))
            for t, step, base, mult in ((up8, 1, 1, 0), (down8, -1, E, 0), (region0, REGION, 0, 0), (ramp16, P, 0, 0),
                                        (ramp_s, 1, 0, 0), (token_id, P, 0, 1), (dump_row, P, 2 * TOK, 1)):
                chain(gp.iota(t[:], [[step, t.shape[1]]], base=base, channel_multiplier=mult,
                              allow_small_or_imprecise_dtypes=True))
            gp.memset(neg_max[:], 0.0).then_inc(consts_ready, 1)

            def keys(b):
                gp.tensor_tensor(k_heads[:, b * HK:(b + 1) * HK].rearrange("p (h k) -> p h k", k=KL),
                                 spread(k_t[:, b * KL:(b + 1) * KL], H, 1), spread(head_of[:], KL), ALU.mult).then_inc(keys_ready, 1)

            pool.wait_ge(dve_setup, 4)
            keys(0)
            pool.wait_ge(xn_ready, G)
            x3 = x[:].rearrange("p (t d) -> p t d", d=D)
            gp.tensor_tensor(x3, x3, spread(out_row[:], NT, 1), ALU.add).then_inc(x_biased, 1)
            for b in range(1, B):
                keys(b)

            def place_rows(k, g):
                m = r[k]
                wait_alone(pool, consts_ready, (m["rows_placed"], g + 1), (m["rows2_ready"], g + 1))
                for c, idx in enumerate((row1, row2)):
                    for j in range(TG):
                        row = (rows1, rows2)[c][:, j * RW:(j + 1) * RW] if k == 0 else at(rows_all, (g * 2 + c) * TG + j, RW)
                        gp.indirect_dma_start(out=xslots[:, :], out_offset=bass.IndirectOffsetOnAxis(ap=idx[:, j:j + 1], axis=0),
                                              in_=row, in_offset=None).then_inc(m["scattered"], 16)

            def combine(k, g):
                m = r[k]
                pool.wait_ge(m["fetched"][g], 32)
                weights = at(gate, g, 2 * TG).rearrange("p (t c) -> p t c", c=2)
                xg = at(x, g, TG * D)
                for c in range(2):
                    part = at(back, g * 2 + c, TG * D)
                    chain(gp.tensor_tensor(part.rearrange("p (t d) -> p t d", d=D), part.rearrange("p (t d) -> p t d", d=D),
                                           spread(weights[:, :, c], D), ALU.mult))
                    ins = gp.tensor_tensor(xg, xg, part, ALU.add)
                    if c == 0:
                        chain(ins)
                ins.then_inc(pool_combined, 1)

            def return_rows(k, s, j):
                m = r[k]
                n = j % XBUF
                o = ys[:, n * D:(n + 1) * D]
                if k == 1:
                    e = pool.value_load(slot_e_i[0:1, bass.ds(s, 1)], min_val=0, max_val=E - 1)
                    pool.wait_ge(m["y_ready"], s + 1)
                    W(pool, m["returned"][n], uses(s, j))
                    gp.tensor_tensor(o, two(ya, j), at(g2_all, e, D), ALU.mult).then_inc(y_scaled, 1)
                    pool.wait_ge(y_scaled, s + 1)
                    gp.tensor_tensor(o, o, at(be2_all, e, D), ALU.add).then_inc(y_shifted, 1)
                wait_alone(pool, consts_ready, (m["y_ready"] if k == 0 else y_shifted, s + 1), (m["ret_ready"], s + 1))
                gp.indirect_dma_start(out=yslots[:, :], out_offset=bass.IndirectOffsetOnAxis(ap=ret[:, n:n + 1], axis=0),
                                      in_=o, in_offset=None).then_inc(m["returned"][n], 16)

            pool.wait_ge(table_zeroed, 16 * (E + 1))
            for k in range(2):
                if k == 0:
                    with pool.Fori(0, G) as g:
                        place_rows(k, g)
                    pool.wait_ge(act_setup1, 2)
                    pool.wait_ge(pe_setup1, 9)
                    w3 = w2[1][:].rearrange("p (a n) -> p a n", n=D)
                    gp.tensor_tensor(w3, w3, spread(g1_t[:], D), ALU.mult).then_inc(folded, 1)
                else:
                    for g in range(G // 2, G):
                        combine(0, g)
                    for g in range(G):
                        place_rows(k, g)
                pool.wait_ge(r[k]["tables_ready"], 1)
                for s in range(XBUF):
                    return_rows(k, s, s)
                with pool.Fori(1, NS // XBUF) as i:
                    for j in range(XBUF):
                        return_rows(k, i * XBUF + j, j)
                for s in range(NS // XBUF * XBUF, NS):
                    return_rows(k, s, s)
            combine(1, 1)

        @block.tensor
        def _(pe):
            te = nc.tensor

            def mm(o, a, b, start=True, stop=True, **kw):
                return te.matmul(o, a, b, start=start, stop=stop, **kw)

            def tr(o, a, rows=P):
                return te.transpose(o, a, ident[0:rows, 0:rows])

            pe.wait_ge(ident_ready, 1)
            pe.wait_ge(in_attn0, 16 * 12)
            for b in range(B):
                last = tr(bank(0, b * KL, (b + 1) * KL), ctx_n[0:KL, b * D:(b + 1) * D], KL)
            last.then_inc(pe_setup, 1)
            for g in range(G):
                pe.wait_ge(xn_ready, g + 1)
                for j in range(TG):
                    last = tr(bank(4 + g, j * P, (j + 1) * P), xn[:, (g * TG + j) * D:(g * TG + j + 1) * D])
                last.then_inc(xt_done, 1)
                if g == 0:
                    pe.wait_ge(act_setup, 1)
                    mm(bank(1, 0, B * KL), wk[:], ctx_t[:]).then_inc(pe_setup, 1)
                    for b in range(B):
                        last = mm(bank(0, b * D, (b + 1) * D)[0:KL, :], ctx_t[:, b * KL:(b + 1) * KL], wv[:])
                    last.then_inc(pe_setup, 1)
            pe.wait_ge(dve_setup, 1)
            mm(bank(2, 0, D), bv_rep[:], wo[:]).then_inc(pe_setup, 1)
            pe.wait_ge(dve_setup, 2)
            tr(bank(3, 0, E), emb[:], E)
            tr(bank(3, E, 2 * E), rows1[0:E, 0:D], E).then_inc(pe_setup, 1)
            pe.wait_ge(xnt_ready, G)
            pe.wait_ge(dve_setup, 4)
            for c in range(NBLK):
                if c >= 8:
                    pe.wait_ge(dve_setup, 4 + c - 7)
                for n in range(3):
                    last = mm(bank((4 + c) % 8), place[:, c * P:(c + 1) * P], v_parts[:, n * B * D:(n + 1) * B * D],
                              start=(n == 0), stop=(n == 2))
                last.then_inc(pe_setup, 1)

            def queries(t, j):
                W(pe, qt_ready, t)
                mm(bank(6, 0, P), wq[:], at(xn_t, t, P)).then_inc(q_done, 1)

            def scores(t, j, g, part):
                if part == 0 and j == TG:
                    pe.wait_ge(keys_ready, g + 1)
                pe.wait_ge(qt_ready, t + 1)
                if part < 2:
                    W(pe, sub_done, (t - 1) * 2 + part + 1)
                else:
                    W(pe, exp_done, t * len(PARTS))
                a, n = PARTS[part][0] * KL, (PARTS[part][1] - PARTS[part][0]) * KL
                mm(bank(part, 0, n), two(q_t, j), k_heads[:, bass.ds(g * HK + a, n)], stop=False)
                mm(bank(part, 0, n), at(pick, g, P), hide[:, a:a + n], start=False).then_inc(s_done, 1)

            def turn_probs(t, j):
                W(pe, ptr_ready, t)
                c = 0
                for part, (_, h1) in enumerate(PARTS):
                    pe.wait_ge(exp_done, t * len(PARTS) + part + 1)
                    while (c + 1) * P <= h1 * KL or (h1 == H and c < NBLK):
                        last = tr(bank(3, c * P, (c + 1) * P), two(probs, j, NBLK * P)[:, c * P:(c + 1) * P])
                        c += 1
                last.then_inc(pt_done, 1)

            def values(t, g):
                pe.wait_ge(ptr_ready, t + 1)
                W(pe, added, t)
                nothing = shift_t[:].bitcast(BF16)
                mm(bank(7, 0, H * VC), nothing[:, 0:P], nothing[:, 0:H * VC], stop=False, skip_group_check=True)
                for c in range(NBLK):
                    h0, h1 = c * P // KL, min(H, -(-(c + 1) * P // KL))
                    last = mm(bank(7, h0 * VC, h1 * VC), probs_t[:, c * P:(c + 1) * P],
                              v_heads[:, bass.ds(g * (NBLK * H * VC) + (c * H + h0) * VC, (h1 - h0) * VC)],
                              start=False, stop=(c == NBLK - 1), skip_group_check=True)
                last.then_inc(pv_done, 1)

            def turn_heads(t):
                pe.wait_ge(o_ready, t + 1)
                tr(bank(7, 256, 384), heads_out[:]).then_inc(ot_done, 1)

            def project(t):
                pe.wait_ge(ott_ready, t + 1)
                mm(bank(7, 384, 512), heads_t[:], wo[:]).then_inc(proj_done, 1)

            def route_turn(k, g, b):
                m = r[k]
                pe.wait_ge(m["rows_ready"], g + 1)
                for j in range(TG):
                    last = tr(bank(b, j * P, (j + 1) * P), rows1[:, j * RW:j * RW + D])
                last.then_inc(m["xgt_done"], 1)

            def route_logits(k, g, b):
                m = r[k]
                pe.wait_ge(m["xgt_ready"], g + 1)
                w, n = (rt, 2 * E) if k == 0 else (router1, E)
                for j in range(TG):
                    last = mm(bank(b, j * n, (j + 1) * n), xg_t[:, j * P:(j + 1) * P], w[:])
                last.then_inc(m["logits_done"], 1)

            def route_rank(k, g, b):
                m = r[k]
                pe.wait_ge(m["chosen_ready"], g + 1)
                mm(bank(b, 0, TG * E), below[:], chosen[:], stop=False)
                for i in range(1, TG):
                    mm(bank(b, i * E, TG * E), ones_b[:], chosen[:, 0:(TG - i) * E], start=False, stop=False)
                mm(bank(b, 0, TG * E), ones_b[:], running[:], start=False)
                for i in range(TG):
                    mm(bank(b, TG * E, TG * E + E), ones_b[:], chosen[:, i * E:(i + 1) * E], start=(i == 0), stop=False)
                mm(bank(b, TG * E, TG * E + E), ones_b[:], running[:, 0:E], start=False).then_inc(m["pos_done"], 1)

            def attend(g, first, final):
                for j in range(TG):
                    t = g * TG + j
                    behind = not (first and j == 0)
                    ahead = not (final and j == TG - 1)
                    turn_probs(t, j)
                    if ahead:
                        scores(t + 1, j + 1, g + (j + 1) // TG, 0)
                    if not first and j == 1:
                        pe.wait_ge(qt_ready, t + 2)
                        route_turn(0, g - 1, 6)
                    if behind:
                        turn_heads(t - 1)
                    if ahead:
                        scores(t + 1, j + 1, g + (j + 1) // TG, 1)
                    if behind:
                        project(t - 1)
                    if ahead:
                        scores(t + 1, j + 1, g + (j + 1) // TG, 2)
                    if not first and j == 1:
                        route_logits(0, g - 1, 6)
                    elif not (final and j >= TG - 2):
                        if not first and j == 0:
                            pe.wait_ge(r[0]["pos_read"], g)
                        queries(t + 2, j)
                    if not first and j == 3:
                        pe.wait_ge(*((r[0]["logits_read"], g) if final else (qt_ready, t + 3)))
                        route_rank(0, g - 1, 6)
                    values(t, g)
                    if not first and j == 1:
                        pe.wait_ge(r[0]["logits_read"], g)
                        queries(t + 2, j)

            pe.wait_ge(consts_ready, 1)
            pe.wait_ge(keys_ready, 1)
            pe.wait_ge(dve_setup, 4 + NBLK)
            queries(0, 0)
            for part in range(len(PARTS)):
                scores(0, 0, 0, part)
            queries(1, 1)
            attend(0, True, False)
            with pe.Fori(1, G - 1) as g:
                attend(g, False, False)
            attend(G - 1, False, True)
            turn_heads(NT - 1)
            project(NT - 1)

            def route_all(k, g, banks):
                route_turn(k, g, banks[0])
                route_logits(k, g, banks[1])
                route_rank(k, g, banks[2])

            pe.wait_ge(added, NT)
            pe.wait_ge(in_small1, 16 * 10)
            tr(bank(4, 0, P), u1[:])
            tr(bank(4, P, 2 * P), u2[:]).then_inc(pe_setup1, 1)
            pe.wait_ge(in_ffn1, 64)
            tr(bank(7, 0, E * FC), g1_n[:], E * FC)
            tr(bank(7, E * FC, 2 * E * FC), be1_n[:], E * FC)
            tr(bank(7, 2 * E * FC, 2 * E * FC + E), b2_n[:], E).then_inc(pe_setup1, 1)

            def shifts(experts):
                for e in experts:
                    for c in range(FC):
                        a = e * FC + c
                        last = mm(bank(7, 128 + e, 129 + e), w2[1][:, a * D:(a + 1) * D], be1_t[:, a:a + 1],
                                  start=(c == 0), stop=(c == FC - 1))
                return last

            pe.wait_ge(act_setup1, 1)
            mm(bank(5, 0, B * KL), u1_t[:], ctx_t[:]).then_inc(pe_setup1, 1)
            pe.wait_ge(act_setup1, 3)
            mm(bank(5, 0, B * KL), u2_t[:], kp_a[:]).then_inc(pe_setup1, 1)
            mm(bank(6, 0, 1), u2_t[:], ub1[:]).then_inc(pe_setup1, 1)
            route_turn(0, G - 1, 0)
            route_logits(0, G - 1, 1)
            pe.wait_ge(act_setup1, 4)
            mm(bank(5, 0, B * KL), u2[:], kp_t[:]).then_inc(pe_setup1, 1)
            pe.wait_ge(act_setup1, 5)
            mm(bank(5, 0, B * KL), u1[:], fold_u[:]).then_inc(pe_setup1, 1)
            pe.wait_ge(act_setup1, 8)
            mm(bank(5, 0, B * KL), bq1_rep[:], kp_t[:]).then_inc(pe_setup1, 1)
            shifts(range(0, 2))
            route_rank(0, G - 1, 2)
            shifts(range(2, E)).then_inc(pe_setup1, 1)

            pe.wait_ge(dve_setup1, 1)
            tr(bank(7, 256, 384), shift_t[:]).then_inc(pe_setup1, 1)

            def experts(k):
                m = r[k]

                def turn_x(s, j):
                    pe.wait_ge(m["loaded"][j % XBUF], uses(s, j) + 16)
                    W(pe, m["xst_ready"], s - 1)
                    tr(bank(6 + j % 2, 0, P), xs[:, (j % XBUF) * RW:(j % XBUF) * RW + D]).then_inc(m["xst_done"], 1)

                def experts_of(i):
                    v = pe.value_load(packed_i[0:1, bass.ds(i, 1)], min_val=0, max_val=2 ** (EBITS * (XBUF + 2)) - 1)
                    return [(v >> (EBITS * n)) & (E - 1) for n in range(XBUF + 2)]

                def hidden(s, j, e):
                    pe.wait_ge(m["xst_ready"], s + 1)
                    W(pe, m["act_done"], s - 1)
                    mm(bank(j % 2), xs_t[:, (j % 2) * D:(j % 2 + 1) * D], w1[k][:, bass.ds(e * F, F)], stop=False)
                    mm(bank(j % 2), at(pick, e, P), bias_p[k][:, 0:F], start=False).then_inc(m["h_done"], 1)

                def turn_h(s, j):
                    pe.wait_ge(m["act_done"] if k == 0 else hn_ready, s + 1)
                    W(pe, m["ht_ready"], s - 1)
                    src = hid if k == 0 else hidn
                    for c in range(FC):
                        last = tr(bank(2 + j % 2, c * P, (c + 1) * P), src[:, (j % 2) * F + c * P:][:, 0:P])
                    last.then_inc(m["ht_done"], 1)

                def output(s, j, e):
                    pe.wait_ge(m["ht_ready"], s + 1)
                    W(pe, m["y_ready" if k == 0 else "y_read"], s - 1)
                    for c in range(FC):
                        mm(bank(4 + j % 2, 0, D), hid_t[:, (j % 2) * F + c * P:][:, 0:P],
                           w2[k][:, bass.ds(e * F + c * D, D)], start=(c == 0), stop=False)
                    mm(bank(4 + j % 2, 0, D), at(pick, e, P), bias_p[k][:, F:F + D], start=False).then_inc(m["y_done"], 1)

                def tile(s, j, left, e):
                    turn_h(s, j)
                    if left > 2:
                        hidden(s + 2, j + 2, e[j + 2])
                    if left > 3:
                        turn_x(s + 3, j + 3)
                    output(s, j, e[j])

                U = XBUF
                e = experts_of(0)
                for s in range(3):
                    turn_x(s, s)
                for s in range(2):
                    hidden(s, s, e[s])
                for s in range(U):
                    tile(s, s, U, e)
                with pe.Fori(1, NS // U) as i:
                    e = experts_of(i)
                    for j in range(U):
                        tile(i * U + j, j, U, e)
                done = NS // U * U
                e = experts_of(NPASS - 1)
                for s in range(done, NS):
                    tile(s, s - done, NS - s, e)

            pe.wait_ge(dve_setup1, 2)
            pe.wait_ge(in_ffn0, 32)
            pe.wait_ge(r[0]["tables_ready"], 1)
            experts(0)

            def scores1(g):
                pe.wait_ge(x1t_ready, g + 1)
                for j in range(TG):
                    last = mm(bank(1, j * KL, (j + 1) * KL), xn1_t[:, j * P:(j + 1) * P], fold[:, bass.ds(g * KL, KL)])
                last.then_inc(s1_done, 1)

            def turn1(g):
                pe.wait_ge(ln1_ready, g + 1)
                for j in range(TG):
                    last = tr(bank(0, j * P, (j + 1) * P), xn1[:, j * D:(j + 1) * D])
                last.then_inc(x1t_done, 1)

            def values1(g):
                pe.wait_ge(e1_done, g + 1)
                for j in range(TG):
                    last = tr(bank(2, j * P, (j + 1) * P)[0:KL, :], pr1[:, j * KL:(j + 1) * KL])
                last.then_inc(p1t_done, 1)
                pe.wait_ge(p1t_ready, g + 1)
                for j in range(TG):
                    last = mm(bank(3, j * D, (j + 1) * D), pr1_t[:, j * P:(j + 1) * P], ctx_z[:, bass.ds(g * D, D)])
                last.then_inc(pv1_done, 1)

            def attend1(g, attends=True, ahead=True, routes=True):
                if attends:
                    values1(g)
                if routes:
                    route_turn(1, g - 1, 4)
                if ahead:
                    turn1(g + 1)
                if routes:
                    route_logits(1, g - 1, 5)
                if ahead:
                    scores1(g + 1)
                if routes:
                    route_rank(1, g - 1, 6)

            turn1(0)
            scores1(0)
            attend1(0, routes=False)
            with pe.Fori(1, G - 1) as g:
                attend1(g)
            attend1(G - 1, ahead=False)
            attend1(G, attends=False, ahead=False)
            pe.wait_ge(r[1]["tables_ready"], 1)
            pe.wait_ge(folded, 1)
            experts(1)

        @block.scalar
        def _(act):
            sc_ = nc.scalar

            def copy(o, i, s=None):
                ins = sc_.activation(o, i, ACT.Copy)
                return ins.then_inc(s, 1) if s is not None else ins

            act.wait_ge(pe_setup, 1)
            copy(ctx_t[:], bank(0, 0, B * KL), act_setup)
            for g in range(G):
                act.wait_ge(xt_done, g + 1)
                copy(at(xn_t, g, TG * P), bank(4 + g), xnt_ready)
            act.wait_ge(consts_ready, 1)

            def queried(t, j):
                act.wait_ge(q_done, t + 1)
                W(act, s_done, (t - 1) * len(PARTS))
                sc_.activation(two(q_t, j), bank(6, 0, P), ACT.Identity, bias=bq_scaled[:], scale=DH ** -0.5).then_inc(qt_ready, 1)

            def exps(t, j, parts=range(len(PARTS))):
                for part in parts:
                    h0, h1 = PARTS[part]
                    if part < 2:
                        act.wait_ge(sub_done, t * 2 + part + 1)
                        p = two(probs, j, NBLK * P)[:, h0 * KL:h1 * KL]
                        last = sc_.activation(p, p, ACT.Exp)
                    else:
                        act.wait_ge(max_done, t + 1)
                        for h in range(h0, h1):
                            last = sc_.activation(two(probs, j, NBLK * P)[:, h * KL:(h + 1) * KL],
                                                  bank(part, (h - h0) * KL, (h - h0 + 1) * KL), ACT.Exp, bias=two(neg_max, j, H)[:, h:h + 1])
                    last.then_inc(exp_done, 1)

            def turned_probs(t):
                act.wait_ge(pt_done, t + 1)
                W(act, pv_done, t)
                copy(probs_t[:], bank(3, 0, NBLK * P), ptr_ready)

            def turned_heads(t):
                act.wait_ge(ot_done, t + 1)
                copy(heads_t[:], bank(7, 256, 384), ott_ready)

            def route_turned(k, g, b):
                m = r[k]
                act.wait_ge(m["xgt_done"], g + 1)
                copy(xg_t[:], bank(b), m["xgt_ready"])

            def route_rows2(k, g):
                m = r[k]
                act.wait_ge(m["rows_ready"], g + 1)
                for rows in (rows2[:],) if k == 0 else (at(rows_all, g * 2 + c, TG * RW) for c in range(2)):
                    last = copy(rows.rearrange("p (t w) -> p t w", w=RW)[:, :, 0:D],
                                rows1[:].rearrange("p (t w) -> p t w", w=RW)[:, :, 0:D])
                last.then_inc(m["rows2_ready"], 1)

            def route_exp(k, g):
                m = r[k]
                act.wait_ge(m["gap_ready"], g + 1)
                sc_.activation(gap[:], gap[:], ACT.Exp).then_inc(m["gap_exp"], 1)

            def attend(g, first, final):
                for j in range(TG):
                    t = g * TG + j
                    turned_probs(t)
                    if not (first and j == 0):
                        turned_heads(t - 1)
                    if not first and j == 1:
                        route_turned(0, g - 1, 6)
                    if not (final and j == TG - 1):
                        exps(t + 1, j + 1, (0, 1))
                    if not (final and j >= TG - 2) and (first or j != 1):
                        queried(t + 2, j)
                    if not (final and j == TG - 1):
                        exps(t + 1, j + 1, (2,))
                    if not first and j == 1:
                        queried(t + 2, j)
                    if not first and j == 1:
                        route_rows2(0, g - 1)
                    if not first and j == 2:
                        route_exp(0, g - 1)

            queried(0, 0)
            queried(1, 1)
            exps(0, 0)
            attend(0, True, False)
            with act.Fori(1, G - 1) as g:
                attend(g, False, False)
            attend(G - 1, False, True)
            turned_heads(NT - 1)
            act.wait_ge(pe_setup1, 1)
            copy(u1_t[:], bank(4, 0, P))
            copy(u2_t[:], bank(4, P, 2 * P), act_setup1)
            act.wait_ge(pe_setup1, 2)
            copy(g1_t[:], bank(7, 0, E * FC))
            copy(be1_t[:], bank(7, E * FC, 2 * E * FC), act_setup1)
            act.wait_ge(pe_setup1, 3)
            sc_.activation(kp_a[:], bank(5, 0, B * KL), ACT.Identity, bias=ub1[:]).then_inc(act_setup1, 1)
            act.wait_ge(pe_setup1, 4)
            sc_.activation(kp_t[:], bank(5, 0, B * KL), ACT.Identity, bias=ub2[:]).then_inc(act_setup1, 1)
            route_turned(0, G - 1, 0)
            route_rows2(0, G - 1)
            act.wait_ge(pe_setup1, 6)
            copy(fold_u[:], bank(5, 0, B * KL), act_setup1)
            act.wait_ge(pe_setup1, 7)
            copy(fold[:], bank(5, 0, B * KL), act_setup1)
            sc_.activation(bq1[:], bank(6, 0, 1), ACT.Identity, bias=ub2[:]).then_inc(act_setup1, 1)
            act.wait_ge(act_setup1, 7)
            sc_.activation(bq1_rep[:], ones[:], ACT.Copy, scale=bq1[:]).then_inc(act_setup1, 1)
            act.wait_ge(pe_setup1, 8)
            copy(q_row[:], bank(5, 0, B * KL), act_setup1)
            route_exp(0, G - 1)
            sc_.activation(unused[:], eps[:], ACT.Gelu)

            def experts(k):
                m = r[k]

                def turned_x(s, j):
                    act.wait_ge(m["xst_done"], s + 1)
                    W(act, m["h_done"], s - 1)
                    copy(xs_t[:, (j % 2) * D:(j % 2 + 1) * D], bank(6 + j % 2, 0, P), m["xst_ready"])

                def turned_h(s, j):
                    act.wait_ge(m["ht_done"], s + 1)
                    W(act, m["y_done"], s - 1)
                    copy(two(hid_t, j, F), bank(2 + j % 2), m["ht_ready"])

                def activate(s, j):
                    act.wait_ge(m["h_done"], s + 1)
                    if k == 0:
                        W(act, m["ht_done"], s - 1)
                        sc_.activation(hid[:, (j % 2) * F:(j % 2 + 1) * F], bank(j % 2), ACT.Gelu).then_inc(m["act_done"], 1)
                    else:
                        W(act, hn_ready, s - 1)
                        sc_.activation(hid[:, (j % 2) * F:(j % 2 + 1) * F], bank(j % 2), ACT.Relu).then_inc(m["act_done"], 1)

                def deviation_h(s):
                    act.wait_ge(hstat_ready, s + 1)
                    sc_.activation(hrs[:, 0:1], hmv[:, 1:2], ACT.Sqrt, bias=eps[:]).then_inc(hsd_ready, 1)

                def activate_y(s, j):
                    act.wait_ge(m["y_done"], s + 1)
                    W(act, y_scaled, s - 1)
                    sc_.activation(ya[:, (j % 2) * D:(j % 2 + 1) * D], bank(4 + j % 2, 0, D), ACT.Relu).then_inc(m["y_read"], 1)

                def deviation_y(s):
                    act.wait_ge(ystat_ready, s + 1)
                    sc_.activation(yrs[:, 0:1], ymv[:, 1:2], ACT.Sqrt, bias=eps[:]).then_inc(ysd_ready, 1)

                def tile(s, j, left, first=False):
                    if k == 1:
                        turned_h(s, j)
                        if left > 1:
                            deviation_h(s + 1)
                        if not first:
                            deviation_y(s - 1)
                    if left > 2:
                        activate(s + 2, j + 2)
                    if left > 3:
                        turned_x(s + 3, j + 3)
                    if k == 1:
                        activate_y(s, j)

                turned_x(0, 0)
                turned_x(1, 1)
                activate(0, 0)
                turned_x(2, 2)
                activate(1, 1)
                if k == 1:
                    deviation_h(0)
                U = XBUF
                for s in range(U):
                    tile(s, s, U, s == 0)
                with act.Fori(1, NS // U) as i:
                    for j in range(U):
                        tile(i * U + j, j, U)
                for s in range(NS // U * U, NS):
                    tile(s, s, NS - s)
                if k == 1:
                    deviation_y(NS - 1)

            experts(0)
            sc_.activation(unused[:], eps[:], ACT.Exp)

            def turned1(g):
                act.wait_ge(x1t_done, g + 1)
                copy(xn1_t[:], bank(0), x1t_ready)

            def attend1(g, attends=True, ahead=True, routes=True):
                if attends:
                    act.wait_ge(s1_ready, g + 1)
                    for j in range(TG):
                        last = sc_.activation(pr1[:, j * KL:(j + 1) * KL], sc1[:, j * KL:(j + 1) * KL], ACT.Exp,
                                              bias=nmax1[:, j:j + 1], accum_out=sum1[:, j:j + 1])
                    last.then_inc(e1_done, 1)
                    act.wait_ge(p1t_done, g + 1)
                    copy(pr1_t[0:KL, :], bank(2)[0:KL, :], p1t_ready)
                if routes:
                    route_turned(1, g - 1, 4)
                if ahead:
                    turned1(g + 1)
                if routes:
                    route_rows2(1, g - 1)
                    route_exp(1, g - 1)

            turned1(0)
            attend1(0, routes=False)
            with act.Fori(1, G - 1) as g:
                attend1(g)
            attend1(G - 1, ahead=False)
            attend1(G, attends=False, ahead=False)
            sc_.activation(unused[:], eps[:], ACT.Sqrt)
            experts(1)

        @block.vector
        def _(dve):
            v = nc.vector
            chain = Steps(dve, dve_step)
            var_g = mvg[:].rearrange("p (t s) -> p t s", s=2)[:, :, 1]

            def rsqrt(y, a, t):
                n = y.shape[1]
                third = nw_y[0:y.shape[0], 0:n]
                chain(v.tensor_scalar(y.bitcast(I32), a.bitcast(I32), -0.5, RSQRT_SEED, ALU.mult, ALU.add))
                squared = chain.start(v.tensor_tensor(t, y, y, ALU.mult))
                v.tensor_scalar(third, y, 3 / 8, None, ALU.mult)
                chain.until(squared)
                chain(v.tensor_tensor(t, t, a, ALU.mult))
                chain(v.scalar_tensor_tensor(t, t, -10 / 3, t, ALU.add, ALU.mult))
                chain(v.scalar_tensor_tensor(y, t, 5.0, third, ALU.add, ALU.mult))
                chain(v.scalar_tensor_tensor(t, y, -0.5, y, ALU.mult, ALU.mult))
                chain(v.tensor_tensor(t, t, a, ALU.mult))
                chain(v.scalar_tensor_tensor(y, t, 1.5, y, ALU.add, ALU.mult))

            def tiles_stats(t0, t1):
                for t in range(t0, t1):
                    last = v.bn_stats(stats[:, t * 6:(t + 1) * 6], x[:, t * D:(t + 1) * D])
                chain(last)
                for t in range(t0, t1):
                    last = v.bn_aggr(mv[:, t * 2:(t + 1) * 2], stats[:, t * 6:(t + 1) * 6])
                chain(last)

            def tiles_deviations(t0, t1):
                chain(v.tensor_scalar(nw_v[:, t0:t1], mv[:, 2 * t0:2 * t1].rearrange("p (t s) -> p t s", s=2)[:, :, 1], LN_EPS, None, ALU.add))
                rsqrt(rstd[:, t0:t1], nw_v[:, t0:t1], nw_t[:, t0:t1])

            dve.wait_ge(in_x, 16 * G)
            tiles_stats(0, NT)
            tiles_deviations(0, NT)
            for g in range(G):
                for t in range(g * TG, (g + 1) * TG):
                    last = v.tensor_scalar(xn[:, t * D:(t + 1) * D], x[:, t * D:(t + 1) * D], mv[:, 2 * t:2 * t + 1],
                                           rstd[:, t:t + 1], ALU.subtract, ALU.mult)
                last.then_inc(xn_ready, 1)

            dve.wait_ge(blanks_ready, 1)
            dve.wait_ge(ident_ready, 1)
            dve.wait_ge(in_attn0, 16 * 12)
            v.tensor_scalar(bv_rep[:], ones[:], bv[:], None, ALU.mult).then_inc(dve_setup, 1)
            v.tensor_copy(place[:, 0:HK].rearrange("p (h k) -> p h k", k=KL), spread(ident[:, 0:KL], H, 1))
            v.tensor_scalar(hide[0:B, :].rearrange("b (h k) -> b h k", k=KL), spread(mask_u8[:], H, 1), HIDE, None, ALU.mult)
            dve.wait_ge(pe_setup, 3)
            vals = bank(0)[0:KL, :]
            part = [v_parts[0:KL, n * B * D:(n + 1) * B * D] for n in range(3)]
            chain(v.tensor_copy(part[0], vals))
            chain(v.tensor_tensor(v_rest[0:KL, :], vals, part[0], ALU.subtract))
            chain(v.tensor_copy(part[1], v_rest[0:KL, :]))
            chain(v.tensor_tensor(part[2], v_rest[0:KL, :], part[1], ALU.subtract))
            chain(v.tensor_tensor(rows2[0:E, 0:D], emb[:], emb[:], ALU.mult))
            chain(v.reduce_sum(nw_v[0:E, 0:1], rows2[0:E, 0:D], AX.X))
            rsqrt(norm2[0:E, 0:1], nw_v[0:E, 0:1], nw_t[0:E, 0:1])
            chain(v.tensor_tensor(nw_v[0:E, 0:1], nw_v[0:E, 0:1], norm2[0:E, 0:1], ALU.mult))
            chain(v.tensor_scalar(nw_v[0:E, 0:1], nw_v[0:E, 0:1], NORM_EPS, None, ALU.add))
            chain(v.reciprocal(nw_t[0:E, 0:1], nw_v[0:E, 0:1]))
            v.tensor_scalar(rows1[0:E, 0:D], emb[:], nw_t[0:E, 0:1], None, ALU.mult).then_inc(dve_setup, 1)
            dve.wait_ge(pe_setup, 4)
            v.tensor_tensor(out_row[:], bank(2, 0, D), bo_all[:], ALU.add).then_inc(dve_setup, 1)
            chain(v.tensor_scalar(k_t[:], bank(1, 0, B * KL), bk[:], None, ALU.add))
            dve.wait_ge(pe_setup, 5)
            v.tensor_copy(rt[:], bank(3, 0, 2 * E)).then_inc(dve_setup, 1)
            dve.wait_ge(consts_ready, 1)
            v.tensor_copy(pick[:].rearrange("p (e m) -> p e m", e=E), spread(pick_row[:], P)).then_inc(r[0]["pos_read"], 1)
            v.tensor_scalar(cache_all[:], cache_all[:], 0.1, None, ALU.mult)
            v.tensor_scalar(bq_scaled[:], bq[:], DH ** -0.5, None, ALU.mult)
            vh = v_heads[:].rearrange("p (b c h v) -> p b c h v", b=B, c=NBLK, v=VC)
            v.tensor_copy(v_heads[:].rearrange("p (b r v) -> p b r v", b=B, v=VC)[:, :, :, DH], spread(block_of[:], B, 1))
            for c in range(NBLK):
                dve.wait_ge(pe_setup, 6 + c)
                v.tensor_tensor(vh[:, :, c, :, 0:DH], bank((4 + c) % 8).rearrange("p (b h v) -> p b h v", b=B, v=DH),
                                spread(spread(block_of[:, c * H:(c + 1) * H], B, 1), DH, 3), ALU.mult).then_inc(dve_setup, 1)

            def subtract(t, j, part, between=None):
                dve.wait_ge(s_done, t * len(PARTS) + part + 1)
                h0, h1 = PARTS[part]
                nm = two(neg_max, j, H)[:, h0:h1]
                s3 = bank(part, 0, (h1 - h0) * KL).rearrange("p (h k) -> p h k", k=KL)
                maxima = v.tensor_reduce(nm, s3, AX.X, ALU.max, negate=True)
                if part == 2:
                    maxima.then_inc(max_done, 1)
                    return
                found = chain.start(maxima)
                if between:
                    between()
                chain.until(found)
                if part == 0:
                    W(dve, pt_done, t - 1)
                v.tensor_tensor(two(probs, j, NBLK * P)[:, h0 * KL:h1 * KL].rearrange("p (h k) -> p h k", k=KL),
                                s3, spread(nm, KL), ALU.add).then_inc(sub_done, 1)

            def divide(t):
                dve.wait_ge(pv_done, t + 1)
                o = bank(7, 0, H * VC).rearrange("p (h v) -> p h v", v=VC)
                chain(v.reciprocal(inv[:], o[:, :, DH]))
                W(dve, ot_done, t)
                v.tensor_tensor(heads_out[:].rearrange("p (h v) -> p h v", v=DH), o[:, :, 0:DH], spread(inv[:], DH),
                                ALU.mult).then_inc(o_ready, 1)

            def add(t):
                dve.wait_ge(proj_done, t + 1)
                dve.wait_ge(x_biased, 1)
                v.tensor_tensor(at(x, t, D), bank(7, 384, 512), at(x, t, D), ALU.add).then_inc(added, 1)

            def group_moments(groups):
                for g, n in groups:
                    for i in range(TG):
                        j = n * TG + i
                        last = v.bn_stats(statg[:, j * 6:(j + 1) * 6], at(x, g * TG + i, D))
                chain(last, consts_ready)
                for g, n in groups:
                    for j in range(n * TG, (n + 1) * TG):
                        last = v.bn_aggr(mvg[:, j * 2:(j + 1) * 2], statg[:, j * 6:(j + 1) * 6])
                chain(last)

            def group_stats(groups):
                group_moments(groups)
                lo, hi = min(n for g, n in groups) * TG, max(n + 1 for g, n in groups) * TG
                chain(v.tensor_scalar(nw_v[:, lo:hi], var_g[:, lo:hi], LN_EPS, None, ALU.add))
                rsqrt(rstdg[:, lo:hi], nw_v[:, lo:hi], nw_t[:, lo:hi])

            def normalise(o, w, g, n):
                for i in range(TG):
                    j = n * TG + i
                    last = v.tensor_scalar(o[:, i * w:i * w + D], at(x, g * TG + i, D), mvg[:, 2 * j:2 * j + 1],
                                           rstdg[:, j:j + 1], ALU.subtract, ALU.mult)
                return last

            def route_stats(g):
                wait_alone(dve, consts_ready, (added, (g + 1) * TG))
                group_moments([(g, 0)])
                v.tensor_scalar(nw_v[:, TG:2 * TG], var_g[:, 0:TG], float(D), None, ALU.mult)
                chain(v.tensor_scalar(nw_v[:, 0:TG], var_g[:, 0:TG], LN_EPS, None, ALU.add))
                rsqrt(rstdg[:], nw_v[:, 0:2 * TG], nw_t[:, 0:2 * TG])

            def route_norm(k, g):
                m = r[k]
                W(dve, *((m["scattered"], g * (16 * 2 * TG)) if k == 0 else (m["rows2_ready"], g)))
                normalise(rows1, RW, g, 0)
                for c, base in enumerate((0.0, float(TOK))):
                    rows = (rows1, rows2)[c][:] if k == 0 else at(rows_all, g * 2 + c, TG * RW)
                    last = v.tensor_scalar(rows.rearrange("p (t w) -> p t w", w=RW)[:, :, D], at(token_id, g, TG),
                                           base, None, ALU.add)
                last.then_inc(m["rows_ready"], 1)

            def by_e(t):
                return t[:].rearrange("p (t e) -> p t e", e=E)

            def route_read(k, g, b):
                m = r[k]
                n = (2 if k == 0 else 1) * TG * E
                dve.wait_ge(m["logits_done"], g + 1)
                v.tensor_copy(logits[:, 0:n], bank(b, 0, n)).then_inc(m["logits_read"], 1)

            def pick_one(values, value, ramp, onehot, op):
                chain(v.tensor_reduce(value, values, AX.X, op))
                chain(v.tensor_tensor(by_e(hit), values, spread(value, E), ALU.is_equal))
                chain(v.tensor_tensor(by_e(key), by_e(hit), spread(ramp[:], TG, 1), ALU.mult))
                chain(v.tensor_reduce(best[:], by_e(key), AX.X, ALU.max))
                chain(v.tensor_tensor(by_e(onehot), by_e(key), spread(best[:], E), ALU.is_equal))

            def route_scores(k, g):
                m = r[k]
                dve.wait_ge(m["logits_read"], g + 1)
                if k == 1:
                    chain(v.tensor_tensor(by_e(sc), logits[:, 0:TG * E].rearrange("p (t e) -> p t e", e=E),
                                          spread(br_all[:], TG, 1), ALU.add))
                    return
                pair = logits[:].rearrange("p (t e) -> p t e", e=2 * E)
                least = pair[:, :, 0:E]
                a = chain.start(v.tensor_tensor(norm2[:], nw_v[:, TG:2 * TG], rstdg[:, TG:2 * TG], ALU.mult))
                b = chain.start(v.tensor_reduce(top1[:], least, AX.X, ALU.min))
                chain.until(a)
                a = chain.start(v.tensor_tensor(norm2[:], norm2[:], rstdg[:, 0:TG], ALU.mult))
                chain.until(b)
                b = chain.start(v.tensor_tensor(by_e(hit), least, spread(top1[:], E), ALU.is_equal))
                chain.until(a)
                a = chain.start(v.tensor_scalar(norm2[:], norm2[:], NORM_EPS, None, ALU.add))
                chain.until(b)
                b = chain.start(v.tensor_tensor(by_e(key), by_e(hit), spread(up8[:], TG, 1), ALU.mult))
                chain.until(a)
                a = chain.start(v.reciprocal(inv_norm[:], norm2[:]))
                chain.until(b)
                b = chain.start(v.tensor_reduce(best[:], by_e(key), AX.X, ALU.max))
                chain.until(a)
                a = chain.start(v.tensor_tensor(by_e(sc), pair[:, :, E:2 * E], spread(inv_norm[:], E), ALU.mult))
                chain.until(b)
                b = chain.start(v.tensor_tensor(by_e(oh1), by_e(key), spread(best[:], E), ALU.is_equal))
                chain.until(a)
                chain(v.tensor_tensor(by_e(sc), by_e(sc), spread(cache_all[:], TG, 1), ALU.add))
                chain(v.scalar_tensor_tensor(sc[:], oh1[:], DROP, sc[:], ALU.mult, ALU.add))

            def route_first(k, g):
                pick_one(by_e(sc), top1[:], down8, oh1, ALU.max)
                chain(v.scalar_tensor_tensor(sc[:], oh1[:], 2 * DROP, sc[:], ALU.mult, ALU.add))

            def route_second(k, g):
                pick_one(by_e(sc), top2[:], down8, oh2, ALU.max)
                v.tensor_tensor(gap[:], top2[:], top1[:], ALU.subtract).then_inc(r[k]["gap_ready"], 1)

            def route_chosen(k, g):
                v.tensor_tensor(chosen[:], oh1[:], oh2[:], ALU.add).then_inc(r[k]["chosen_ready"], 1)

            def route_choose(k, g):
                route_scores(k, g)
                route_first(k, g)
                route_second(k, g)
                route_chosen(k, g)

            def route_place(k, g, b):
                m = r[k]
                dve.wait_ge(m["gap_exp"], g + 1)
                a = chain.start(v.tensor_scalar(top1[:], gap[:], 1.0, None, ALU.add))
                dve.wait_ge(m["pos_done"], g + 1)
                v.tensor_tensor(by_e(posn), bank(b, 0, TG * E).rearrange("p (t e) -> p t e", e=E), spread(region0[:], TG, 1),
                                ALU.add).then_inc(m["pos_read"], 1)
                v.tensor_reduce(added_up[:], chosen[:].rearrange("p (t e) -> p e t", e=E), AX.X, ALU.add)
                chain.until(a)
                a = chain.start(v.reciprocal(best[:], top1[:]))
                dve.wait_ge(m["pos_read"], g + 2 - k)
                both = "p (c n) -> p c n"
                c1 = chain.start(v.tensor_tensor(key_both[:].rearrange(both, c=2), oh_both[:].rearrange(both, c=2), spread(posn[:], 2, 1), ALU.mult))
                chain.until(a)
                gg = at(gate, g, 2 * TG).rearrange("p (t c) -> p t c", c=2)
                v.tensor_copy(gg[:, :, 0], best[:])
                chain.until(c1)
                c1 = chain.start(v.tensor_reduce(row_f[:], by_e(key_both), AX.X, ALU.add))
                v.tensor_tensor(gg[:, :, 1], best[:], gap[:], ALU.mult)
                if k == 1:
                    W(dve, m["scattered"], g * (16 * 2 * TG))
                chain.until(c1)
                v.tensor_copy(row_both[:], row_f[:]).then_inc(m["rows_placed"], 1)
                chain(v.tensor_tensor(by_e(running), by_e(running), spread(added_up[:], TG, 1), ALU.add))

            def tables(k, b):
                m = r[k]
                dve.wait_ge(m["pos_done"], G)
                chain(v.tensor_copy(count[:, 0:E], bank(b, TG * E, TG * E + E)))
                n16 = TOK // P
                g16 = gt[:, 0:E * n16].rearrange("p (e n) -> p e n", n=n16)
                chain(v.tensor_tensor(g16, spread(count[:, 0:E], n16), spread(ramp16[:], E, 1), ALU.is_gt))
                chain(v.tensor_reduce(ends[0][:, E:], g16, AX.X, ALU.add))
                for n, step in enumerate((1, 2, 4)):
                    chain(v.tensor_tensor(ends[n + 1][:, E:], ends[n][:, E:], ends[n][:, E - step:2 * E - step], ALU.add))
                g3, w3 = (t[:].rearrange("p (s e) -> p s e", e=E) for t in (gt, gtw))
                v.tensor_scalar(coef[:], ends[0][:, E:], -float(P), float(REGION), ALU.mult, ALU.add)
                chain(v.tensor_tensor(g3, spread(ramp_s[:], E), spread(ends[3][:, E:], NS, 1), ALU.is_ge))
                chain(v.tensor_tensor(w3, g3, spread(coef[:], NS, 1), ALU.mult))
                chain(v.tensor_reduce(slot_row[:], w3, AX.X, ALU.add))
                chain(v.scalar_tensor_tensor(slot_row[:], ramp_s[:], float(P), slot_row[:], ALU.mult, ALU.add))
                v.tensor_copy(slot_row_i[:], slot_row[:]).then_inc(m["slots_ready"], 1)
                chain(v.tensor_reduce(slot_e[:, 0:NS], g3[:, :, 0:E - 1], AX.X, ALU.add))
                v.tensor_copy(slot_e_i[:], slot_e[:, 0:NS])

                def nth(n):
                    return slot_e[:, n:n + NPASS * XBUF].rearrange("p (i u) -> p i u", u=XBUF)[:, :, 0]

                chain(v.scalar_tensor_tensor(packed[:], nth(XBUF + 1), float(E), nth(XBUF), ALU.mult, ALU.add))
                for n in range(XBUF - 1, -1, -1):
                    chain(v.scalar_tensor_tensor(packed[:], packed[:], float(E), nth(n), ALU.mult, ALU.add))
                v.tensor_copy(packed_i[:], packed[:]).then_inc(m["tables_ready"], 1)
                v.tensor_tensor(coef[:], count[:, 1:E + 1], count[:, 0:E], ALU.subtract)
                chain(v.tensor_reduce(e_all[:], g3, AX.X, ALU.add))
                v.scalar_tensor_tensor(local[:], e_all[:], -float(REGION), slot_row[:], ALU.mult, ALU.add)
                chain(v.tensor_tensor(w3, g3, spread(coef[:], NS, 1), ALU.mult))
                chain(v.tensor_reduce(cnt_s[:], w3, AX.X, ALU.add))
                chain(v.tensor_scalar(cnt_s[:], cnt_s[:], count[:, 0:1], token_id[:, 0:1], ALU.add, ALU.subtract))
                chain(v.tensor_tensor(valid[:], local[:], cnt_s[:], ALU.is_lt))
                chain(v.tensor_scalar(pad_row[:], valid[:], -1.0, 1.0, ALU.mult, ALU.add))
                chain(v.tensor_tensor(pad_row[:], pad_row[:], dump_row[:], ALU.mult))

            def bias_parts(k):
                chain(v.tensor_copy(bias_p[k][:], bias_f[k][:]))
                chain(v.tensor_tensor(bias_r[:], bias_f[k][:], bias_p[k][:], ALU.subtract))
                chain(v.tensor_copy(bias_q[:], bias_r[:]))
                chain(v.tensor_tensor(bias_r[:], bias_r[:], bias_q[:], ALU.subtract))
                chain(v.tensor_copy(bias_p[k][32:64, :], bias_q[32:64, :]))
                chain(v.tensor_copy(bias_p[k][64:96, :], bias_r[64:96, :]))

            def route_step(g, j):
                if j == 0:
                    route_stats(g)
                    route_norm(0, g)
                if j == 1:
                    route_read(0, g, 6)
                    route_scores(0, g)
                if j == 2:
                    route_first(0, g)
                    route_second(0, g)
                    route_chosen(0, g)
                if j == 3:
                    route_place(0, g, 6)

            def attend(g, first, final):
                for j in range(TG):
                    t = g * TG + j
                    if not (first and j == 0):
                        divide(t - 1)
                    for part in range(len(PARTS)):
                        between = (lambda: add(t - 1)) if part == 1 and not (first and j == 0) else None
                        if not (final and j == TG - 1):
                            subtract(t + 1, j + 1, part, between)
                        elif between:
                            between()
                    if not first:
                        route_step(g - 1, j)

            for part in range(len(PARTS)):
                subtract(0, 0, part)
            attend(0, True, False)
            with dve.Fori(1, G - 1) as g:
                chain.enter(g - 1, DVE_GROUP)
                attend(g, False, False)
                chain.leave(G - 2)
            attend(G - 1, False, True)
            divide(NT - 1)
            add(NT - 1)
            route_stats(G - 1)
            route_norm(0, G - 1)
            route_read(0, G - 1, 1)
            route_choose(0, G - 1)
            route_place(0, G - 1, 2)
            tables(0, 2)
            dve.wait_ge(in_bias, 16 * 9)
            bias_parts(0)

            dve.wait_ge(pe_setup1, 9)
            chain(v.tensor_copy(coef[:], bank(7, 2 * E * FC, 2 * E * FC + E)))
            for n in range(3):
                ins = v.tensor_tensor(shift_t[:, 32 * n:32 * n + E], bank(7, 128, 128 + E), coef[:], ALU.add)
            ins.then_inc(dve_setup1, 1)
            v.memset(running[:], 0.0)
            v.memset(pr1_t[:], 0.0)
            chain(v.tensor_copy(ctx_z[0:KL, :], ctx_n[0:KL, :]))
            dve.wait_ge(pe_setup1, 10)
            v.tensor_copy(bias_f[1][:, F:F + D], bank(7, 256, 384)).then_inc(dve_setup1, 1)
            dve.wait_ge(dve_setup1, 2)
            bias_parts(1)

            def experts(k):
                m = r[k]

                def return_row(s, j):
                    n = j % XBUF
                    dve.wait_ge(m["loaded"][n], uses(s, j) + 16)
                    W(dve, m["returned"][n], uses(s, j))
                    v.tensor_scalar(ret[:, n:n + 1], xs[:, n * RW + D:][:, 0:1], at(valid, s, 1), at(pad_row, s, 1),
                                    ALU.mult, ALU.add).then_inc(m["ret_ready"], 1)

                def turned_h(s, j):
                    dve.wait_ge(m["ht_done"], s + 1)
                    W(dve, m["y_done"], s - 1)
                    v.tensor_copy(hid_t[:, (j % 2) * F:(j % 2 + 1) * F], bank(2 + j % 2)).then_inc(m["ht_ready"], 1)

                def stats_h(s, j):
                    dve.wait_ge(m["act_done"], s + 1)
                    chain(v.bn_stats(hst[:], two(hid, j, F)), consts_ready)
                    v.bn_aggr(hmv[:], hst[:]).then_inc(hstat_ready, 1)

                def normalise_h(s, j):
                    dve.wait_ge(hsd_ready, s + 1)
                    chain(v.reciprocal(hrs[:, 1:2], hrs[:, 0:1]))
                    W(dve, m["ht_done"], s - 1)
                    v.tensor_scalar(two(hidn, j, F), two(hid, j, F), hmv[:, 0:1], hrs[:, 1:2],
                                    ALU.subtract, ALU.mult).then_inc(hn_ready, 1)

                def stats_y(s, j):
                    dve.wait_ge(m["y_read"], s + 1)
                    chain(v.bn_stats(yst[:], two(ya, j)), consts_ready)
                    v.bn_aggr(ymv[:], yst[:]).then_inc(ystat_ready, 1)

                def finish(s, j):
                    n = j % XBUF
                    if k == 0:
                        dve.wait_ge(m["y_done"], s + 1)
                        W(dve, m["returned"][n], uses(s, j))
                        v.tensor_copy(ys[:, n * D:(n + 1) * D], bank(4 + j % 2, 0, D)).then_inc(m["y_ready"], 1)
                        return
                    dve.wait_ge(ysd_ready, s + 1)
                    chain(v.reciprocal(yrs[:, 1:2], yrs[:, 0:1]))
                    v.tensor_scalar(two(ya, j), two(ya, j), ymv[:, 0:1], yrs[:, 1:2], ALU.subtract, ALU.mult).then_inc(m["y_ready"], 1)

                def tile(s, j, left, first=False):
                    if k == 0:
                        turned_h(s, j)
                        if left > 1:
                            return_row(s + 1, j + 1)
                        finish(s, j)
                        return
                    if left > 1:
                        stats_h(s + 1, j + 1)
                    if not first:
                        stats_y(s - 1, j - 1)
                    if left > 1:
                        return_row(s + 1, j + 1)
                        normalise_h(s + 1, j + 1)
                    if not first:
                        finish(s - 1, j - 1)

                return_row(0, 0)
                if k == 1:
                    stats_h(0, 0)
                    normalise_h(0, 0)
                U = XBUF
                for s in range(U):
                    tile(s, s, U, s == 0)
                with dve.Fori(1, NS // U) as i:
                    chain.enter(i - 1, U * DVE_TILE[k])
                    for j in range(U):
                        tile(i * U + j, j, U)
                    chain.leave(NS // U - 1)
                for s in range(NS // U * U, NS):
                    tile(s, s, NS - s)
                if k == 1:
                    stats_y(NS - 1, NS - 1)
                    finish(NS - 1, NS - 1)

            experts(0)

            def combine(k, g):
                m = r[k]
                dve.wait_ge(m["fetched"][g], 32)
                for c in range(2):
                    for i in range(TG):
                        last = v.scalar_tensor_tensor(at(x, g * TG + i, D), at(back, (g * 2 + c) * TG + i, D),
                                                      gate[:, (g * TG + i) * 2 + c:][:, 0:1], at(x, g * TG + i, D), ALU.mult, ALU.add)
                    if c == 0:
                        chain(last)
                last.then_inc(m["combined"], 1)

            def prepare1(g):
                for i in range(TG):
                    last = v.tensor_scalar(xn1[:, i * D:(i + 1) * D], at(x, g * TG + i, D), mv[:, bass.ds((g * TG + i) * 2, 1)],
                                           at(rstd, g * TG + i, 1), ALU.subtract, ALU.mult)
                last.then_inc(ln1_ready, 1)
                chain(v.scalar_tensor_tensor(fside_q[:].rearrange("p (t k) -> p t k", k=KL), spread(at(q_row, g, KL), TG, 1), D ** -0.5,
                                             fside[:].rearrange("p (t k) -> p t k", k=KL), ALU.mult, ALU.add))

            def attend1(g, attends=True, ahead=True, routes=True):
                if attends:
                    dve.wait_ge(s1_done, g + 1)
                    chain(v.scalar_tensor_tensor(sc1[:], bank(1, 0, TG * KL), D ** -0.5, fside_q[:], ALU.mult, ALU.add))
                    v.tensor_reduce(nmax1[:], sc1[:].rearrange("p (t k) -> p t k", k=KL), AX.X, ALU.max, negate=True).then_inc(s1_ready, 1)
                if routes:
                    group_stats([(g - 1, 0)])
                    route_norm(1, g - 1)
                if ahead:
                    prepare1(g + 1)
                if attends:
                    dve.wait_ge(e1_done, g + 1)
                    chain(v.reciprocal(inv1[:], sum1[:]))
                    dve.wait_ge(pv1_done, g + 1)
                    for i in range(TG):
                        last = v.scalar_tensor_tensor(at(x, g * TG + i, D), bank(3, i * D, (i + 1) * D), inv1[:, i:i + 1],
                                                      at(x, g * TG + i, D), ALU.mult, ALU.add)
                    chain(last)
                if routes:
                    route_read(1, g - 1, 5)
                    route_choose(1, g - 1)
                    route_place(1, g - 1, 6)

            for g in range(G):
                if g < G // 2:
                    combine(0, g)
                    dve.wait_ge(r[0]["combined"], g + 1)
                else:
                    dve.wait_ge(pool_combined, g + 1 - G // 2)
                tiles_stats(g * TG, (g + 1) * TG)
                if g == 0:
                    tiles_deviations(0, TG)
                    prepare1(0)
            tiles_deviations(TG, NT)
            attend1(0, routes=False)
            with dve.Fori(1, G - 1) as g:
                chain.enter(g - 1, DVE_GROUP1)
                attend1(g)
                chain.leave(G - 2)
            attend1(G - 1, ahead=False)
            attend1(G, attends=False, ahead=False)
            tables(1, 6)
            experts(1)
            for g in (0, 2, 3):
                combine(1, g)


INPUTS = ["x", "ctx_1024", "fside_1xSxS2_0", "mask_BxS2_bk0", "L0_xattn_W_Q", "L0_xattn_b_Q", "L0_xattn_W_K", "L0_xattn_b_K",
          "L0_xattn_W_V", "L0_xattn_b_V", "L0_xattn_W_O", "L0_xattn_b_O", "L0_ffn_uzman_embeddings", "L0_ffn_W1", "L0_ffn_b1",
          "L0_ffn_W2", "L0_ffn_b2", "L0_ffn_onbellek_durumu", "L1_xattn_W1", "L1_xattn_b1", "L1_xattn_W2", "L1_xattn_b2",
          "L1_ffn_Wr", "L1_ffn_br", "L1_ffn_W1", "L1_ffn_b1", "L1_ffn_g1", "L1_ffn_be1", "L1_ffn_W2", "L1_ffn_b2",
          "L1_ffn_g2", "L1_ffn_be2"]


def kernel(**inputs):
    import numpy as np
    import concourse.bacc as bacc
    from concourse.bass_utils import run_bass_kernel_spmd

    nc = bacc.Bacc("TRN2", target_bir_lowering=False, num_devices=1)
    arrays, d = {}, {}
    for name in INPUTS:
        a = np.ascontiguousarray(inputs[name])
        arrays["in_" + name] = a
        d[name] = nc.dram_tensor("in_" + name, a.shape, mybir.dt.from_np(a.dtype), kind="ExternalInput").ap()
    out = nc.dram_tensor("out", (B, S, D), F32, kind="ExternalOutput").ap()
    xslots = nc.dram_tensor("xslots", (XROWS, RW), F32, kind="Internal").ap()
    yslots = nc.dram_tensor("yslots", (YROWS, D), F32, kind="Internal").ap()
    build(nc, d, out, xslots, yslots)
    return run_bass_kernel_spmd(nc, [arrays], core_ids=[0]).results[0]["out"]
```
